# Optimizing a Trainium2 kernel written in Bass

```python
import numpy as np
import jax
import jax.numpy as jnp

def _softmax(x, axis=-1):
    return jax.nn.softmax(x, axis=axis)
def _gelu(x):
    return jax.nn.gelu(x, approximate=True)
def _silu(x):
    return jax.nn.silu(x)
def _sigmoid(x):
    return jax.nn.sigmoid(x)
def _layernorm(x, axis=-1, eps=1e-5):
    m = jnp.mean(x, axis=axis, keepdims=True)
    v = jnp.var(x, axis=axis, keepdims=True)
    return (x - m) / jnp.sqrt(v + eps)
def _scatter_add(tgt, idx, src, axis=0):
    return tgt.at[idx].add(src)
def _segment_sum(src, seg, n):
    return jax.ops.segment_sum(src, seg, n)

kernel_name = 'mk_conv_preact_d2_conv_nchw256_49f7a8'

def setup_inputs(seed: int = 0):
    np.random.seed(seed)
    _w = jnp.asarray
    def _rec_inputs():
        import jax
        import jax.numpy as jnp
        _gk = jax.random.key(seed)
        x = 7.22e-05 + 1 * jax.random.normal(jax.random.fold_in(_gk, 1), (8, 256, 64, 64), jnp.float32)
        return x
    x = _rec_inputs()
    def _L0_conv_setup():
        import jax, jax.numpy as jnp
        import numpy as np
        B, C, H, W = (8, 256, 64, 64)
        KS = 3
        ECA_K = 3
        FUSION = 0.5
        BN_EPS = 1e-05

        def _ddf(x, W_filter, b_filter, w_eca, W_proj, b_proj, gamma, beta):
            b, c, h, w = x.shape
            pooled = x.mean(axis=(2, 3))
            fp = jnp.pad(pooled, ((0, 0), (1, 1)))
            eca = w_eca[0] * fp[:, :c] + w_eca[1] * fp[:, 1:c + 1] + w_eca[2] * fp[:, 2:c + 2]
            attn = jax.nn.sigmoid(eca)
            channel_feat = x * attn[:, :, None, None]
            filt = jnp.einsum('bchw,oc->bohw', x, W_filter) + b_filter[None, :, None, None]
            filt = filt.reshape(b, c, KS * KS, h, w)
            xp = jnp.pad(x, ((0, 0), (0, 0), (1, 1), (1, 1)))
            patches = jnp.stack([xp[:, :, i:i + h, j:j + w] for i in range(KS) for j in range(KS)], axis=2)
            spatial_feat = jnp.sum(patches * filt, axis=2)
            fused = FUSION * channel_feat + (1.0 - FUSION) * spatial_feat
            y = jnp.einsum('bchw,oc->bohw', fused, W_proj) + b_proj[None, :, None, None]
            mean = y.mean(axis=(0, 2, 3))
            var = y.var(axis=(0, 2, 3))
            y = (y - mean[None, :, None, None]) * jax.lax.rsqrt(var[None, :, None, None] + BN_EPS)
            return y * gamma[None, :, None, None] + beta[None, :, None, None]
        key = jax.random.key(seed)
        ks = jax.random.split(key, 8)
        x = jax.random.normal(ks[0], (B, C, H, W), dtype=jnp.float32)
        W_filter = jax.random.normal(ks[1], (C * KS * KS, C), dtype=jnp.float32) * (1.0 / np.sqrt(C))
        b_filter = jax.random.normal(ks[2], (C * KS * KS,), dtype=jnp.float32) * 0.01
        w_eca = jax.random.normal(ks[3], (ECA_K,), dtype=jnp.float32) * 0.5
        W_proj = jax.random.normal(ks[4], (C, C), dtype=jnp.float32) * (1.0 / np.sqrt(C))
        b_proj = jax.random.normal(ks[5], (C,), dtype=jnp.float32) * 0.01
        gamma = jnp.ones((C,), dtype=jnp.float32)
        beta = jnp.zeros((C,), dtype=jnp.float32)
        return {'x': x, 'W_filter': W_filter, 'b_filter': b_filter, 'w_eca': w_eca, 'W_proj': W_proj, 'b_proj': b_proj, 'gamma': gamma, 'beta': beta}
    _L0_conv_all = _L0_conv_setup()
    _L0_conv_in = {k: v for k, v in _L0_conv_all.items() if k in ('W_filter', 'b_filter', 'w_eca', 'W_proj', 'b_proj', 'gamma', 'beta', )}
    del _L0_conv_all

    def _L1_conv_setup():
        import jax, jax.numpy as jnp
        import numpy as np
        C = 256
        K = 7
        GC = 16
        G = C // GC
        RED = C // 2
        BN_EPS = 1e-05

        def _unfold(x, k):
            b, c, h, w = x.shape
            p = (k - 1) // 2
            xp = jnp.pad(x, ((0, 0), (0, 0), (p, p), (p, p)))
            patches = jnp.stack([xp[:, :, i:i + h, j:j + w] for i in range(k) for j in range(k)], axis=2)
            return patches
        key = jax.random.key(seed)
        ks = jax.random.split(key, 8)
        x = jax.random.normal(ks[0], (4, C, 56, 56), dtype=jnp.float32)
        w1 = jax.random.normal(ks[1], (RED, C), dtype=jnp.float32) * (1.0 / np.sqrt(C))
        b1 = jax.random.normal(ks[2], (RED,), dtype=jnp.float32) * 0.01
        gamma = jnp.ones((RED,), dtype=jnp.float32)
        beta = jnp.zeros((RED,), dtype=jnp.float32)
        run_mean = jax.random.normal(ks[3], (RED,), dtype=jnp.float32) * 0.01
        run_var = jnp.abs(jax.random.normal(ks[4], (RED,), dtype=jnp.float32)) * 0.1 + 1.0
        w2 = jax.random.normal(ks[5], (G * K * K, RED), dtype=jnp.float32) * (1.0 / np.sqrt(RED))
        b2 = jax.random.normal(ks[6], (G * K * K,), dtype=jnp.float32) * 0.01
        return {'x': x, 'w1': w1, 'b1': b1, 'gamma': gamma, 'beta': beta, 'run_mean': run_mean, 'run_var': run_var, 'w2': w2, 'b2': b2}
    _L1_conv_all = _L1_conv_setup()
    _L1_conv_in = {k: v for k, v in _L1_conv_all.items() if k in ('w1', 'b1', 'gamma', 'beta', 'run_mean', 'run_var', 'w2', 'b2', )}
    del _L1_conv_all

    return {
        "x": x,
        "L0_conv_W_filter": _L0_conv_in["W_filter"],
        "L0_conv_b_filter": _L0_conv_in["b_filter"],
        "L0_conv_w_eca": _L0_conv_in["w_eca"],
        "L0_conv_W_proj": _L0_conv_in["W_proj"],
        "L0_conv_b_proj": _L0_conv_in["b_proj"],
        "L0_conv_gamma": _L0_conv_in["gamma"],
        "L0_conv_beta": _L0_conv_in["beta"],
        "L1_conv_w1": _L1_conv_in["w1"],
        "L1_conv_b1": _L1_conv_in["b1"],
        "L1_conv_gamma": _L1_conv_in["gamma"],
        "L1_conv_beta": _L1_conv_in["beta"],
        "L1_conv_run_mean": _L1_conv_in["run_mean"],
        "L1_conv_run_var": _L1_conv_in["run_var"],
        "L1_conv_w2": _L1_conv_in["w2"],
        "L1_conv_b2": _L1_conv_in["b2"],
    }

def reference(x, L0_conv_W_filter, L0_conv_b_filter, L0_conv_w_eca, L0_conv_W_proj, L0_conv_b_proj, L0_conv_gamma, L0_conv_beta, L1_conv_w1, L1_conv_b1, L1_conv_gamma, L1_conv_beta, L1_conv_run_mean, L1_conv_run_var, L1_conv_w2, L1_conv_b2):
    import jax
    import jax.numpy as jnp
    def _L0_conv_ref(x, W_filter, b_filter, w_eca, W_proj, b_proj, gamma, beta):
        import jax, jax.numpy as jnp
        import numpy as np
        B, C, H, W = (8, 256, 64, 64)
        KS = 3
        ECA_K = 3
        FUSION = 0.5
        BN_EPS = 1e-05

        def _ddf(x, W_filter, b_filter, w_eca, W_proj, b_proj, gamma, beta):
            b, c, h, w = x.shape
            pooled = x.mean(axis=(2, 3))
            fp = jnp.pad(pooled, ((0, 0), (1, 1)))
            eca = w_eca[0] * fp[:, :c] + w_eca[1] * fp[:, 1:c + 1] + w_eca[2] * fp[:, 2:c + 2]
            attn = jax.nn.sigmoid(eca)
            channel_feat = x * attn[:, :, None, None]
            filt = jnp.einsum('bchw,oc->bohw', x, W_filter) + b_filter[None, :, None, None]
            filt = filt.reshape(b, c, KS * KS, h, w)
            xp = jnp.pad(x, ((0, 0), (0, 0), (1, 1), (1, 1)))
            patches = jnp.stack([xp[:, :, i:i + h, j:j + w] for i in range(KS) for j in range(KS)], axis=2)
            spatial_feat = jnp.sum(patches * filt, axis=2)
            fused = FUSION * channel_feat + (1.0 - FUSION) * spatial_feat
            y = jnp.einsum('bchw,oc->bohw', fused, W_proj) + b_proj[None, :, None, None]
            mean = y.mean(axis=(0, 2, 3))
            var = y.var(axis=(0, 2, 3))
            y = (y - mean[None, :, None, None]) * jax.lax.rsqrt(var[None, :, None, None] + BN_EPS)
            return y * gamma[None, :, None, None] + beta[None, :, None, None]
        return _ddf(x, W_filter, b_filter, w_eca, W_proj, b_proj, gamma, beta)

    def _L1_conv_ref(x, w1, b1, gamma, beta, run_mean, run_var, w2, b2):
        import jax, jax.numpy as jnp
        import numpy as np
        C = 256
        K = 7
        GC = 16
        G = C // GC
        RED = C // 2
        BN_EPS = 1e-05

        def _unfold(x, k):
            b, c, h, w = x.shape
            p = (k - 1) // 2
            xp = jnp.pad(x, ((0, 0), (0, 0), (p, p), (p, p)))
            patches = jnp.stack([xp[:, :, i:i + h, j:j + w] for i in range(k) for j in range(k)], axis=2)
            return patches
        b, c, h, w = x.shape
        r = jnp.einsum('bchw,oc->bohw', x, w1) + b1[None, :, None, None]
        inv_std = jax.lax.rsqrt(run_var + BN_EPS)
        r = (r - run_mean[None, :, None, None]) * (gamma * inv_std)[None, :, None, None] + beta[None, :, None, None]
        r = jax.nn.relu(r)
        wm = jnp.einsum('bchw,oc->bohw', r, w2) + b2[None, :, None, None]
        wm = wm.reshape(b, G, 1, K * K, h, w)
        xu = _unfold(x, K).reshape(b, G, GC, K * K, h, w)
        eps = jnp.finfo(xu.dtype).eps
        out = (wm * xu + eps).sum(axis=3)
        return out.reshape(b, c, h, w)

    def _gn(v, G=32, eps=1e-5):
        B_, C_, H_, W_ = v.shape
        g = v.reshape(B_, G, C_ // G, H_, W_)
        m = jnp.mean(g, axis=(2, 3, 4), keepdims=True)
        s = jnp.var(g, axis=(2, 3, 4), keepdims=True)
        return ((g - m) / jnp.sqrt(s + eps)).reshape(v.shape)

    def _ln_c(v, eps=1e-6):
        m = jnp.mean(v, axis=1, keepdims=True)
        s = jnp.var(v, axis=1, keepdims=True)
        return (v - m) / jnp.sqrt(s + eps)

    def _ln_t(v, eps=1e-5):
        m = jnp.mean(v, axis=-1, keepdims=True)
        s = jnp.var(v, axis=-1, keepdims=True)
        return (v - m) / jnp.sqrt(s + eps)

    def _to_tokens(v):
        B_, C_, H_, W_ = v.shape
        return v.reshape(B_, C_, H_ * W_).transpose(0, 2, 1)
    def _from_tokens(t, like):
        B_, C_, H_, W_ = like.shape
        return t.transpose(0, 2, 1).reshape(B_, C_, H_, W_)

    x = x + _L0_conv_ref(_gn(x), L0_conv_W_filter, L0_conv_b_filter, L0_conv_w_eca, L0_conv_W_proj, L0_conv_b_proj, L0_conv_gamma, L0_conv_beta)
    x = x + _L1_conv_ref(_gn(x), L1_conv_w1, L1_conv_b1, L1_conv_gamma, L1_conv_beta, L1_conv_run_mean, L1_conv_run_var, L1_conv_w2, L1_conv_b2)
    return x


_drawn_inputs = setup_inputs


def setup_inputs(seed=0):
    import zlib

    import numpy as np

    out = dict(_drawn_inputs(seed))
    spreads = {'L0_conv_gamma': (1.0, 0.2),
     'L0_conv_beta': (0.0, 0.1),
     'L1_conv_gamma': (1.0, 0.2),
     'L1_conv_beta': (0.0, 0.1)}
    factors = {'L0_conv_b_filter': 5.695,
     'L0_conv_w_eca': 43.749,
     'L0_conv_b_proj': 64.0,
     'L1_conv_b1': 5.856,
     'L1_conv_run_mean': 5.736,
     'L1_conv_b2': 4.099}
    for name, (base, spread) in spreads.items():
        noise = np.random.default_rng([zlib.crc32(name.encode()), seed]).standard_normal(out[name].shape)
        drawn = base * np.exp(spread * noise) if base else spread * noise
        out[name] = jnp.asarray(drawn.astype(out[name].dtype))
    for name, factor in factors.items():
        out[name] = (out[name] * factor).astype(out[name].dtype)
    return out
```

```python
import concourse.bass as bass
from concourse import mybir
from contextlib import ExitStack

F32 = mybir.dt.float32
F32R = mybir.dt.float32r
ALU = mybir.AluOpType
ACT = mybir.ActivationFunctionType

P = 128
B, C, H, W = 8, 256, 64, 64
CT = C // P
PX = H * W
GN_CH = C // 32
GN_EPS = 1e-5
BN_EPS = 1e-5
K0 = 9
ROWS = 8
N = ROWS * W
CHUNKS = H // ROWS
WP = W + 2
HP = H + 2
TAPS = CT * K0
RING = 6
K1 = 7
HALO = K1 // 2
GROUPS = 16
RED = C // 2
BR, BC = 4, 6
PR, PC = BR + K1 - 1, BC + K1 - 1
PATCH = PR * PC
POS = BR * BC
NBR = H // BR
NBC = -(-W // BC)
BLK = NBR * NBC
WHOLE = W // BC * BC
QUARTERS = 4
QROWS = H // QUARTERS
QBR = QROWS // BR
QBLK = QBR * NBC
HROWS = QROWS + 2 * HALO
PAIRS = 8
PCH = C // PAIRS
GC = C // GROUPS
W2_AT = PC * (BR - 1) + BC - 1
W2_LEN = W2_AT + PATCH + 1
FINFO_EPS = 2.0 ** -23


def positive(engine, semaphore, value):
    if not isinstance(value, int) or value > 0:
        engine.wait_ge(semaphore, value)


def build(nc, a, y_dram, x1_dram, r_dram, w2_dram, out):
    with ExitStack() as ctx:
        ystats = ctx.enter_context(nc.sbuf_tensor("ystats", [P, CT, B * CHUNKS, 6], F32))
        layer0(nc, a, y_dram, ystats)
        ab = ctx.enter_context(nc.sbuf_tensor("ab", [P, B, PAIRS, 2], F32))
        layer1_features(nc, a, y_dram, x1_dram, r_dram, w2_dram, ystats, ab)
        layer1_involution(nc, a, x1_dram, r_dram, w2_dram, out, ab)


def newton(dve, sem, count, rstd, var, tmp):
    steps = (
        lambda: dve.tensor_tensor(tmp, rstd, rstd, ALU.mult),
        lambda: dve.tensor_tensor(tmp, tmp, var, ALU.mult),
        lambda: dve.tensor_scalar(tmp, tmp, -0.5, 1.5, ALU.mult, ALU.add),
        lambda: dve.tensor_tensor(rstd, rstd, tmp, ALU.mult),
    )
    for n, step in enumerate(steps):
        step().then_inc(sem, 1)
        dve.wait_ge(sem, count + n + 1)


def layer0(nc, a, y_dram, ystats):
    x_v = a["x"].rearrange("b (t p) h w -> b p t h w", p=P)
    y_v = y_dram.rearrange("b (t p) n -> b t p n", p=P)

    with ExitStack() as ctx:
        def sb(name, shape, dt=F32):
            return ctx.enter_context(nc.sbuf_tensor(name, shape, dt))

        def sem(name):
            return ctx.enter_context(nc.semaphore(name))

        wf_hi = sb("wf_hi", [P, CT, CT, K0, P], F32R)
        wf_lo = sb("wf_lo", [P, CT, CT, K0, P], F32R)
        wp_hi = sb("wp_hi", [P, CT, C], F32R)
        wp_lo = sb("wp_lo", [P, CT, C], F32R)
        xn = sb("xn", [P, 2, CT, HP, WP])
        prod = sb("prod", [P, 2, K0, N])
        sums = sb("sums", [P, 2, 4, N])
        fused = sb("fused", [P, 2, N])
        fu_hi = sb("fu_hi", [P, 2, CT, N], F32R)
        fu_lo = sb("fu_lo", [P, 2, CT, N], F32R)
        x_hi = sb("x_hi", [P, 2, CT, N], F32R)
        x_lo = sb("x_lo", [P, 2, CT, N], F32R)
        ybuf = sb("ybuf", [P, 2, N])
        bf = sb("bf", [P, CT, K0])
        bfc = sb("bfc", [P, 2, CT])
        bp = sb("bp", [P, CT])
        weca = sb("weca", [P, 3])
        band = sb("band", [P, CT, C])
        gavg = sb("gavg", [P, P])
        xst = sb("xst", [P, CT, CHUNKS, 6])
        mv = sb("mv", [P, CT, 2])
        gm = sb("gm", [P, CT])
        dm = sb("dm", [P, CT])
        ev = sb("ev", [P, CT])
        gv = sb("gv", [P, CT])
        rstd = sb("rstd", [P, CT])
        nt = sb("nt", [P, CT])
        nb = sb("nb", [P, CT])
        pooled = sb("pooled", [P, CT])
        attn = sb("attn", [P, CT])
        raw = prod[:, :, :, :].rearrange("p s k n -> p (s k n)")
        NF = CT * CT * K0 * P
        wf_raw = raw[:, 0:NF]
        wp_raw = raw[:, NF:NF + CT * C]
        sh_raw = raw[:, NF + CT * C:NF + CT * C + 3 * CT * C].rearrange("p (s t c) -> p s t c", s=3, t=CT)

        filt = ctx.enter_context(nc.psum_tensor("filt", [P, RING, N], F32))
        yps = ctx.enter_context(nc.psum_tensor("yps", [P, N], F32))
        sps = ctx.enter_context(nc.psum_tensor("sps", [P, N], F32))

        consts_in, filters_in = sem("consts_in"), sem("filters_in")
        x_in = sem("x_in")
        zeroed = sem("zeroed")
        w_hi_done, w_lo_done = sem("w_hi_done"), sem("w_lo_done")
        xn_done = sem("xn_done")
        x_hi_done, x_lo_done = sem("x_hi_done"), sem("x_lo_done")
        tap_ready, tap_used = sem("tap_ready"), sem("tap_used")
        pair_sums = sem("pair_sums")
        pool_sums = sem("pool_sums")
        half_sum, fused_done = sem("half_sum"), sem("fused_done")
        fu_hi_done, fu_lo_done = sem("fu_hi_done"), sem("fu_lo_done")
        y_ready, y_copied, y_stats = sem("y_ready"), sem("y_copied"), sem("y_stats")
        y_out = [sem(f"y_out{m}") for m in range(CT)]
        x_stats, chain, band_step = sem("x_stats"), sem("chain"), sem("band_step")
        mean_in, gmean_ps, dev_in, gvar_ps = sem("mean_in"), sem("gmean_ps"), sem("dev_in"), sem("gvar_ps")
        gvar_in, root = sem("gvar_in"), sem("root")
        norm_ready, eca_ps, attn_done, centre_done = sem("norm_ready"), sem("eca_ps"), sem("attn_done"), sem("centre_done")

        CHAIN = 10
        LAST = B - 1
        NPARTS = 3 * CT

        def batches(engine, body):
            body(0, 0, True, False)
            with engine.Fori(0, (LAST - 1) // 2) as two:
                body(2 * two + 1, 1, False, False)
                body(2 * two + 2, 0, False, False)
            body(LAST, 1, False, True)

        with nc.Block() as block:

            @block.sync
            def _(sp):
                sp.dma_start(gavg[:, :], a["group_average"]).then_inc(consts_in, 16)
                sp.dma_start(sh_raw, a["shifts"].rearrange("s (t p) c -> p s t c", p=P)).then_inc(consts_in, 16)
                sp.dma_start(weca[:, :], a["w_eca"].rearrange("(o k) -> o k", o=1).to_broadcast([P, 3])).then_inc(consts_in, 16)
                sp.dma_start(bf[:, :, :], a["b_filter"]).then_inc(consts_in, 16)
                sp.dma_start(bp[:, :], a["b_proj"]).then_inc(consts_in, 16)
                sp.wait_ge(zeroed, 2)
                for t in range(CT):
                    for h in range(2):
                        sp.dma_start(xn[:, 0, t, 1 + 32 * h:33 + 32 * h, 1:1 + W],
                                     x_v[0, :, t, 32 * h:32 * h + 32, :]).then_inc(x_in, 16)
                sp.dma_start(wf_raw, a["wf_t"]).then_inc(filters_in, 16)
                sp.dma_start(wp_raw, a["wp_t"]).then_inc(filters_in, 16)

                for b in range(1, B):
                    sp.wait_ge(x_in, (b * 2 * CT) * 16)
                    positive(sp, tap_used, (b - 1) * CHUNKS * TAPS)
                    for t in range(CT):
                        for h in range(2):
                            sp.dma_start(xn[:, b % 2, t, 1 + 32 * h:33 + 32 * h, 1:1 + W],
                                         x_v[b, :, t, 32 * h:32 * h + 32, :]).then_inc(x_in, 16)

            @block.gpsimd
            def _(pool):
                pool.memset(xn[:, 0, :, :, :], 0.0).then_inc(zeroed, 1)
                pool.memset(xn[:, 1, :, :, :], 0.0).then_inc(zeroed, 1)

                def split_x(b, j, s):
                    n1 = b * CHUNKS + (j + 1)
                    pool.wait_ge(x_hi_done, n1)
                    for t in range(CT):
                        src = xn[:, s, t, 1 + ROWS * j:1 + ROWS * j + ROWS, 1:1 + W]
                        last = pool.tensor_tensor(x_lo[:, j % 2, t, :].rearrange("p (h w) -> p h w", w=W), src,
                                                  x_hi[:, j % 2, t, :].bitcast(F32).rearrange("p (h w) -> p h w", w=W),
                                                  ALU.subtract)
                    last.then_inc(x_lo_done, 1)

                split_x(0, 0, 0)

                def batch(b, s, first, last):
                    for j in range(CHUNKS):
                        for t in range(CT):
                            i = b * (CHUNKS * CT) + (j * CT + t)
                            done = b * (CHUNKS * TAPS) + (j * TAPS + t * K0)
                            positive(pool, fused_done, i - 1)
                            pool.wait_ge(tap_used, done + 4)
                            pool.tensor_tensor(sums[:, t, 0:2, :], prod[:, t, 0:2, :], prod[:, t, 2:4, :],
                                               ALU.add).then_inc(pair_sums, 1)
                            pool.wait_ge(tap_used, done + 8)
                            pool.tensor_tensor(sums[:, t, 2:4, :], prod[:, t, 4:6, :], prod[:, t, 6:8, :],
                                               ALU.add).then_inc(pair_sums, 1)
                            pool.wait_ge(pair_sums, 2 * i + 2)
                            pool.tensor_tensor(sums[:, t, 0:2, :], sums[:, t, 0:2, :], sums[:, t, 2:4, :],
                                               ALU.add).then_inc(pool_sums, 1)
                            if t == 0 and not (last and j == CHUNKS - 1):
                                if j < CHUNKS - 1:
                                    split_x(b, j + 1, s)
                                else:
                                    split_x(b + 1, 0, 1 - s)

                batches(pool, batch)

            @block.scalar
            def _(act):
                PARTS = (0, 2, 5, CHUNKS)

                def normalise(b, s, parts):
                    act.wait_ge(norm_ready, b + 1)
                    for part in parts:
                        r0, r1 = PARTS[part] * ROWS, PARTS[part + 1] * ROWS
                        for t in range(CT):
                            v = xn[:, s, t, 1 + r0:1 + r1, 1:1 + W]
                            act.activation(v, v, ACT.Identity, bias=nb[:, t:t + 1],
                                           scale=rstd[:, t:t + 1]).then_inc(xn_done, 1)

                def split_x(b, j, s):
                    n = b * CHUNKS + j
                    part = 1 if j < 2 else 2 if j < 5 else 3
                    act.wait_ge(xn_done, b * NPARTS + CT * part)
                    positive(act, tap_ready, (n - 1) * TAPS)
                    positive(act, x_lo_done, n - 1)
                    for t in range(CT):
                        src = xn[:, s, t, 1 + ROWS * j:1 + ROWS * j + ROWS, 1:1 + W]
                        last = act.activation(x_hi[:, j % 2, t, :].rearrange("p (h w) -> p h w", w=W), src, ACT.Identity)
                    last.then_inc(x_hi_done, 1)

                def split_fused(b, j, t):
                    i = b * (CHUNKS * CT) + (j * CT + t)
                    act.wait_ge(fused_done, i + 1)
                    positive(act, y_ready, b * (CHUNKS * CT) + (j * CT - CT))
                    positive(act, fu_lo_done, i - 3)
                    act.activation(fu_hi[:, j % 2, t, :], fused[:, t, :], ACT.Identity).then_inc(fu_hi_done, 1)

                def copy_y(b, j, m):
                    yi = b * (CHUNKS * CT) + (j * CT + m)
                    act.wait_ge(y_ready, yi + 1)
                    positive(act, y_out[m], b * (16 * CHUNKS) + 16 * j)
                    positive(act, y_stats, yi - 1)
                    act.activation(ybuf[:, m, :], yps[:, :], ACT.Identity, bias=bp[:, m:m + 1],
                                   scale=0.5).then_inc(y_copied, 1)
                    act.wait_ge(y_copied, yi + 1)
                    at = N * (j % CHUNKS)
                    act.dma_start(y_v[b if j >= 0 else b - 1, m, :, at:at + N], ybuf[:, m, :]).then_inc(y_out[m], 16)

                def sqrt(b1):
                    act.wait_ge(gvar_in, b1 + 1)
                    act.activation(rstd[:, :], gv[:, :], ACT.Sqrt).then_inc(root, 1)

                def attention(b1):
                    act.wait_ge(eca_ps, b1 + 1)
                    positive(act, centre_done, b1)
                    act.activation(attn[:, :], sps[:, 0:CT], ACT.Sigmoid).then_inc(attn_done, 1)

                act.wait_ge(filters_in, 32)
                act.activation(wf_hi[:, :, :, :, :].rearrange("p a b k n -> p (a b k n)"), wf_raw,
                               ACT.Identity).then_inc(w_hi_done, 1)
                act.activation(wp_hi[:, :, :].rearrange("p t n -> p (t n)"), wp_raw, ACT.Identity).then_inc(w_hi_done, 1)
                sqrt(0)
                normalise(0, 0, (0,))
                split_x(0, 0, 0)
                normalise(0, 0, (1, 2))
                attention(0)

                def batch(b, s, first, last):
                    for j in range(CHUNKS):
                        i = b * (CHUNKS * CT) + j * CT
                        if j < CHUNKS - 1:
                            split_x(b, j + 1, s)
                        elif not last:
                            normalise(b + 1, 1 - s, (0,))
                            split_x(b + 1, 0, 1 - s)
                            attention(b + 1)
                        if not (first and j == 0):
                            copy_y(b, j - 1, 0)
                        split_fused(b, j, 0)
                        if not last and j == CHUNKS - 2:
                            sqrt(b + 1)
                        if not last and j == CHUNKS - 1:
                            normalise(b + 1, 1 - s, (1, 2))
                        if not (first and j == 0):
                            copy_y(b, j - 1, 1)
                        split_fused(b, j, 1)

                batches(act, batch)
                copy_y(LAST, CHUNKS - 1, 0)
                copy_y(LAST, CHUNKS - 1, 1)
                for m in range(CT):
                    act.wait_ge(y_out[m], 16 * B * CHUNKS)

            @block.vector
            def _(dve):
                def stats(b1, s, j):
                    for t in range(CT):
                        src = xn[:, s, t, 1 + ROWS * j:1 + ROWS * j + ROWS, 1:1 + W]
                        dve.wait_ge(x_in, b1 * (16 * 2 * CT) + 16 * 2 * CT)
                        dve.bn_stats(xst[:, t, j, :], src).then_inc(x_stats, 1)

                def step(ins, b1, n):
                    ins.then_inc(chain, 1)
                    dve.wait_ge(chain, b1 * CHAIN + n)

                def mean(b1):
                    for t in range(CT):
                        dve.bn_aggr(mv[:, t, :], xst[:, t, :, :].rearrange("p j s -> p (j s)")).then_inc(mean_in, 1)

                def deviation(b1):
                    dve.wait_ge(gmean_ps, b1 + 1)
                    step(dve.tensor_copy(gm[:, :], sps[:, 0:CT]), b1, 1)
                    dve.wait_ge(mean_in, b1 * CT + CT)
                    step(dve.tensor_tensor(dm[:, :], mv[:, :, 0], gm[:, :], ALU.subtract), b1, 2)
                    step(dve.tensor_tensor(ev[:, :], dm[:, :], dm[:, :], ALU.mult), b1, 3)
                    dve.tensor_tensor(ev[:, :], ev[:, :], mv[:, :, 1], ALU.add).then_inc(dev_in, 1)

                def variance(b1):
                    dve.wait_ge(gvar_ps, b1 + 1)
                    dve.tensor_scalar(gv[:, :], sps[:, 0:CT], GN_EPS, None, ALU.add).then_inc(gvar_in, 1)

                def norm(b1):
                    dve.wait_ge(gvar_in, b1 + 1)
                    dve.wait_ge(root, b1 + 1)
                    step(dve.reciprocal(rstd[:, :], rstd[:, :]), b1, 4)
                    newton(dve, chain, b1 * CHAIN + 4, rstd[:, :], gv[:, :], nt[:, :])
                    step(dve.tensor_tensor(pooled[:, :], dm[:, :], rstd[:, :], ALU.mult), b1, 9)
                    step(dve.tensor_tensor(nb[:, :], gm[:, :], rstd[:, :], ALU.mult), b1, 10)
                    dve.tensor_scalar(nb[:, :], nb[:, :], -1.0, None, ALU.mult).then_inc(norm_ready, 1)

                def centre(b1, s):
                    dve.wait_ge(attn_done, b1 + 1)
                    dve.tensor_tensor(bfc[:, s, :], bf[:, :, K0 // 2], attn[:, :], ALU.add).then_inc(centre_done, 1)

                def fuse(i, t):
                    dve.wait_ge(pool_sums, i + 1)
                    positive(dve, fu_hi_done, i - 1)
                    positive(dve, fu_lo_done, i - 1)
                    dve.tensor_tensor(fused[:, t, :], sums[:, t, 0, :], sums[:, t, 1, :], ALU.add).then_inc(half_sum, 1)
                    dve.wait_ge(half_sum, i + 1)
                    dve.tensor_tensor(fused[:, t, :], fused[:, t, :], prod[:, t, K0 - 1, :], ALU.add).then_inc(fused_done, 1)

                def split_fused(i, j, t):
                    dve.wait_ge(fu_hi_done, i + 1)
                    dve.wait_ge(fused_done, i + 1)
                    positive(dve, y_ready, i - t - CT)
                    dve.tensor_tensor(fu_lo[:, j % 2, t, :], fused[:, t, :], fu_hi[:, j % 2, t, :].bitcast(F32),
                                      ALU.subtract).then_inc(fu_lo_done, 1)

                def take_y_stats(yi, m, col):
                    dve.wait_ge(y_copied, yi + 1)
                    dst = ystats[:, m, col, :]
                    dve.bn_stats(dst, ybuf[:, m, :]).then_inc(y_stats, 1)

                for j in range(CHUNKS):
                    stats(0, 0, j)
                dve.wait_ge(x_stats, CHUNKS * CT)
                mean(0)
                dve.wait_ge(consts_in, 16 * 5)
                dve.tensor_scalar(band[:, :, :], sh_raw[:, 0, :, :], weca[:, 0:1], None, ALU.mult).then_inc(band_step, 1)
                for n in (1, 2):
                    dve.wait_ge(band_step, n)
                    dve.scalar_tensor_tensor(band[:, :, :], sh_raw[:, n, :, :], weca[:, n:n + 1], band[:, :, :],
                                             op0=ALU.mult, op1=ALU.add).then_inc(band_step, 1)
                deviation(0)
                variance(0)
                norm(0)
                dve.wait_ge(w_hi_done, 2)
                dve.tensor_tensor(wf_lo[:, :, :, :, :].rearrange("p a b k n -> p (a b k n)"), wf_raw,
                                  wf_hi[:, :, :, :, :].rearrange("p a b k n -> p (a b k n)").bitcast(F32),
                                  ALU.subtract).then_inc(w_lo_done, 1)
                dve.tensor_tensor(wp_lo[:, :, :].rearrange("p t n -> p (t n)"), wp_raw,
                                  wp_hi[:, :, :].rearrange("p t n -> p (t n)").bitcast(F32),
                                  ALU.subtract).then_inc(w_lo_done, 1)
                centre(0, 0)
                dve.wait_ge(w_lo_done, 2)
                dve.wait_ge(band_step, 3)
                dve.wait_ge(centre_done, 1)

                def batch(b, s, first, last):
                    for j in range(CHUNKS):
                        dve.wait_ge(xn_done, b * NPARTS + CT * (1 if j < 1 else 2 if j < 4 else 3))
                        for t in range(CT):
                            i = b * (CHUNKS * CT) + (j * CT + t)
                            done = b * (CHUNKS * TAPS) + (j * TAPS + t * K0)
                            positive(dve, fused_done, i - 1)
                            for k in range(K0):
                                dve.wait_ge(tap_ready, done + k + 1)
                                patch = xn[:, s, t, ROWS * j + k // 3:ROWS * j + k // 3 + ROWS, k % 3:k % 3 + W]
                                bias = bf[:, t, k:k + 1] if k != K0 // 2 else bfc[:, s, t:t + 1]
                                dve.scalar_tensor_tensor(prod[:, t, k, :].rearrange("p (h w) -> p h w", w=W),
                                                         filt[:, (t * K0 + k) % RING, :].rearrange("p (h w) -> p h w", w=W),
                                                         bias, patch, op0=ALU.add, op1=ALU.mult).then_inc(tap_used, 1)
                                if (j, t, k) == (0, 0, 2):
                                    dve.wait_ge(centre_done, b + 1)
                                if k == 2 and not (first and j * CT + t < 3):
                                    back = j * CT + t - 3
                                    take_y_stats(b * (CHUNKS * CT) + back, back % CT, b * CHUNKS + back // CT)
                                if k == 3 and not last and 1 <= j <= 4:
                                    stats(b + 1, 1 - s, 2 * (j - 1) + t)
                                if k == 3 and not last and (j, t) == (6, 1):
                                    variance(b + 1)
                                if k == 5 and not last and (j, t) == (4, 1):
                                    dve.wait_ge(x_stats, b * (CHUNKS * CT) + 2 * CHUNKS * CT)
                                if k == 5 and not (first and j * CT + t < 1):
                                    fuse(i - 1, (t - 1) % CT)
                                if k == 7 and not (first and j * CT + t < 1):
                                    split_fused(i - 1, j if t else j - 1, (t - 1) % CT)
                        if not last and j == 4:
                            mean(b + 1)
                        if not last and j == 5:
                            deviation(b + 1)
                        if not last and j == 6:
                            norm(b + 1)
                        if not last and j == 7:
                            centre(b + 1, 1 - s)

                batches(dve, batch)
                items = B * CHUNKS * CT
                fuse(items - 1, CT - 1)
                split_fused(items - 1, CHUNKS - 1, CT - 1)
                for back in (3, 2, 1):
                    take_y_stats(items - back, (items - back) % CT, (items - back) // CT)
                dve.wait_ge(y_stats, items)

            @block.tensor
            def _(pe):
                def group_mean(b1):
                    pe.wait_ge(mean_in, b1 * CT + CT)
                    positive(pe, attn_done, b1)
                    pe.matmul(sps[:, 0:CT], gavg[:, :], mv[:, :, 0], start=True, stop=True).then_inc(gmean_ps, 1)

                def group_var(b1):
                    pe.wait_ge(dev_in, b1 + 1)
                    pe.matmul(sps[:, 0:CT], gavg[:, :], ev[:, :], start=True, stop=True).then_inc(gvar_ps, 1)

                def eca(b1):
                    pe.wait_ge(norm_ready, b1 + 1)
                    for m in range(CT):
                        for t in range(CT):
                            last = pe.matmul(sps[:, m:m + 1], band[:, t, P * m:P * m + P], pooled[:, t:t + 1],
                                             start=(t == 0), stop=(t == CT - 1))
                    last.then_inc(eca_ps, 1)

                def split_products(dst, w_hi, w_lo, v_hi, v_lo):
                    terms = [(w, v, t) for t in range(CT) for w, v in ((w_hi, v_hi), (w_hi, v_lo), (w_lo, v_hi))]
                    for n, (w, v, t) in enumerate(terms):
                        last = pe.matmul(dst, w(t), v(t), start=(n == 0), stop=(n == len(terms) - 1))
                    return last

                def taps(b, j, t):
                    n = b * CHUNKS + j
                    if t == 0:
                        pe.wait_ge(x_lo_done, n + 1)
                    for k in range(K0):
                        positive(pe, tap_used, n * TAPS + (t * K0 + k + 1 - RING))
                        split_products(filt[:, (t * K0 + k) % RING, :],
                                       lambda c: wf_hi[:, c, t, k, :], lambda c: wf_lo[:, c, t, k, :],
                                       lambda c: x_hi[:, j % 2, c, :], lambda c: x_lo[:, j % 2, c, :]).then_inc(tap_ready, 1)

                def project(b, j, m):
                    yi = b * (CHUNKS * CT) + (j * CT + m)
                    pe.wait_ge(fu_lo_done, b * (CHUNKS * CT) + (j * CT + CT))
                    positive(pe, y_copied, yi)
                    split_products(yps[:, :],
                                   lambda c: wp_hi[:, c, P * m:P * m + P], lambda c: wp_lo[:, c, P * m:P * m + P],
                                   lambda c: fu_hi[:, j % 2, c, :], lambda c: fu_lo[:, j % 2, c, :]).then_inc(y_ready, 1)

                pe.wait_ge(consts_in, 16 * 5)
                group_mean(0)
                group_var(0)
                pe.wait_ge(band_step, 3)
                eca(0)
                pe.wait_ge(w_lo_done, 2)
                taps(0, 0, 0)
                taps(0, 0, 1)

                def batch(b, s, first, last):
                    for j in range(CHUNKS):
                        end = last and j == CHUNKS - 1
                        for t in range(CT):
                            if not end:
                                taps(b, j + 1, t)
                            project(b, j, t)
                            if t == 0 and not last and j == 4:
                                group_mean(b + 1)
                            if t == 0 and not last and j == 5:
                                group_var(b + 1)
                            if t == 0 and not last and j == 6:
                                eca(b + 1)

                batches(pe, batch)


def layer1_features(nc, a, y_dram, x1_dram, r_dram, w2_dram, ystats, ab):
    PIECES = 4
    PN = PX // PIECES
    x_v = a["x"].rearrange("b (t p) h w -> b p t (h w)", p=P)
    y_v = y_dram.rearrange("b (t p) n -> b p t n", p=P)
    x1_v = x1_dram.rearrange("b (t p) n -> b p t n", p=P)
    with ExitStack() as ctx:
        def sb(name, shape, dt=F32):
            return ctx.enter_context(nc.sbuf_tensor(name, shape, dt))

        def sem(name):
            return ctx.enter_context(nc.semaphore(name))

        xs = sb("xs", [P, 2, CT, PX])
        ys = sb("ys", [P, 2, CT, PN])
        rb = sb("rb", [P, 2, POS, NBR, NBC])
        w1t = sb("w1t", [P, CT, RED])
        w1s = sb("w1s", [P, 2, CT, RED])
        cols = sb("cols", [P, 9])
        gavg1 = sb("gavg1", [P, P])
        sel = sb("sel", [P, QUARTERS, P])
        w2_raw = sb("w2_raw", [P, GROUPS * W2_LEN])
        w2_hi = sb("w2_hi", [P, GROUPS * W2_LEN], F32R)
        w2_lo = sb("w2_lo", [P, GROUPS * W2_LEN], F32R)
        ymv = sb("ymv", [P, CT, 2])
        bvar = sb("bvar", [P, 3])
        brs = sb("brs", [P, 3])
        bnt = sb("bnt", [P, 3])
        bsc = sb("bsc", [P, 3])
        ysh = sb("ysh", [P, CT])
        rsh = sb("rsh", [P, 1])
        rbias = sb("rbias", [P, 2])
        st = sb("st", [P, CT, CHUNKS, 6])
        mv1 = sb("mv1", [P, CT, 2])
        gm1 = sb("gm1", [P, CT])
        dm1 = sb("dm1", [P, CT])
        ev1 = sb("ev1", [P, CT])
        gv1 = sb("gv1", [P, CT])
        rt1 = sb("rt1", [P, CT])
        nt1 = sb("nt1", [P, CT])
        nrm = sb("nrm", [P, CT, 2])

        rps = ctx.enter_context(nc.psum_tensor("rps", [P, 4, N], F32))
        cps1 = ctx.enter_context(nc.psum_tensor("cps1", [P, N], F32))

        vec_in, w2_in = sem("vec_in"), sem("w2_in")
        xy_in = [sem(f"xy_in{n}") for n in range(2)]
        w2_hi_done, w2_lo_done, w2_out = sem("w2_hi_done"), sem("w2_lo_done"), sem("w2_out")
        r_zeroed = sem("r_zeroed")
        bn_chain, bn_var, bn_root, bn_ready = sem("bn_chain"), sem("bn_var"), sem("bn_root"), sem("bn_ready")
        y_scaled, x1_done, x1_out = sem("y_scaled"), sem("x1_done"), [sem(f"x1_out{n}") for n in range(2)]
        x1_stats, mean1, chain1, scratch = sem("x1_stats"), sem("mean1"), sem("chain1"), sem("scratch")
        gmean1, dev1, gvar1, gvar1_in, root1 = sem("gmean1"), sem("dev1"), sem("gvar1"), sem("gvar1_in"), sem("root1")
        norm1, w1_scaled, small_ps, small_done = sem("norm1"), sem("w1_scaled"), sem("small_ps"), sem("small_done")
        r_ready, r_copied, r_out = sem("r_ready"), sem("r_copied"), [sem(f"r_out{n}") for n in range(2)]

        CHAIN = 11

        def batches(engine, body):
            body(0, 0)
            body(1, 1)
            with engine.Fori(1, B // 2) as two:
                body(2 * two, 0)
                body(2 * two + 1, 1)

        with nc.Block() as block:

            @block.sync
            def _(sp):
                sp.dma_start(cols[:, :], a["columns"]).then_inc(vec_in, 16)
                sp.dma_start(gavg1[:, :], a["group_average"]).then_inc(vec_in, 16)
                sp.dma_start(sel[:, :, :], a["select"]).then_inc(vec_in, 16)
                sp.dma_start(w1t[:, :, :], a["w1_t"]).then_inc(vec_in, 16)
                for b in range(B):
                    s = b % 2
                    if b >= 2:
                        sp.wait_ge(x1_out[s], 16 * PIECES * (b // 2))
                        sp.wait_ge(r_ready, (b - 1) * CHUNKS)
                    for q in range(PIECES):
                        n = b * PIECES + q
                        if n >= 2:
                            sp.wait_ge(x1_done, n - 1)
                        sp.dma_start(ys[:, n % 2, :, :], y_v[b, :, :, PN * q:PN * q + PN]).then_inc(xy_in[n % 2], 16)
                        sp.dma_start(xs[:, s, :, PN * q:PN * q + PN],
                                     x_v[b, :, :, PN * q:PN * q + PN]).then_inc(xy_in[n % 2], 16)
                    if b == 0:
                        sp.dma_start(w2_raw[:, :], a["w2_pad"]).then_inc(w2_in, 16)
                for part, (w, done) in enumerate(((w2_hi, w2_hi_done), (w2_lo, w2_lo_done))):
                    sp.wait_ge(done, 1)
                    sp.dma_start(w2_dram[:, :, part, :].rearrange("g p n -> p g n"),
                                 w[:, :].bitcast(F32).rearrange("p (g n) -> p g n", g=PAIRS)).then_inc(w2_out, 16)
                sp.wait_ge(w2_out, 32)

            @block.gpsimd
            def _(pool):
                pool.memset(rb[:, :, :, :, :], 0.0).then_inc(r_zeroed, 1)

                def batch(b, s):
                    for q in range(PIECES):
                        pool.wait_ge(x1_done, b * PIECES + (q + 1))
                        pool.dma_start(x1_v[b, :, :, PN * q:PN * q + PN],
                                       xs[:, s, :, PN * q:PN * q + PN]).then_inc(x1_out[s], 16)
                    pool.wait_ge(r_copied, b * (4 * CHUNKS) + 4 * CHUNKS)
                    pool.dma_start(r_dram[b], rb[:, s, :, :, :].rearrange("p k r c -> p (k r c)")).then_inc(r_out[s], 16)

                for b in range(B):
                    batch(b, b % 2)
                for s in range(2):
                    pool.wait_ge(x1_out[s], 16 * PIECES * B // 2)
                    pool.wait_ge(r_out[s], 16 * B // 2)

            @block.scalar
            def _(act):
                act.wait_ge(bn_var, 1)
                act.activation(brs[:, :], bvar[:, :], ACT.Sqrt).then_inc(bn_root, 1)
                act.wait_ge(bn_ready, 1)

                def batch(b, s):
                    for q in range(PIECES):
                        act.wait_ge(xy_in[q % 2], b * (16 * PIECES) + 32 * (q // 2 + 1))
                        for t in range(CT):
                            act.activation(ys[:, q % 2, t, :], ys[:, q % 2, t, :], ACT.Identity, bias=ysh[:, t:t + 1],
                                           scale=bsc[:, t:t + 1]).then_inc(y_scaled, 1)
                    if isinstance(b, int) and b == 0:
                        act.wait_ge(w2_in, 16)
                        act.activation(w2_hi[:, :], w2_raw[:, :], ACT.Identity).then_inc(w2_hi_done, 1)
                    act.wait_ge(gvar1_in, b + 1)
                    act.activation(rt1[:, :], gv1[:, :], ACT.Sqrt).then_inc(root1, 1)
                    act.wait_ge(small_done, b + 1)
                    act.wait_ge(r_zeroed, 1)
                    for j in range(CHUNKS):
                        act.wait_ge(r_ready, b * CHUNKS + (j + 1))
                        if j == 0:
                            positive(act, r_out[s], (b // 2) * 16 if isinstance(b, int) else (b - s) * 8)
                        for h in range(2):
                            br = 2 * j + h
                            src = rps[:, j % 4, 256 * h:256 * h + 256].rearrange("p (i w) -> p i w", i=BR)
                            dst = rb[:, s, :, br, :].rearrange("p (i j) c -> p i j c", i=BR)
                            for c0, c1, w0, w1 in ((0, W // BC, 0, BC), (W // BC, NBC, 0, W - WHOLE)):
                                act.activation(dst[:, :, w0:w1, c0:c1],
                                               src[:, :, BC * c0:min(BC * c1, W)].rearrange(
                                                   "p i (c j) -> p i j c", j=w1 - w0),
                                               ACT.Relu, bias=rbias[:, s:s + 1], scale=bsc[:, 2:3]).then_inc(r_copied, 1)

                batches(act, batch)

            @block.vector
            def _(dve):
                gamma0, beta0 = cols[:, 0:2], cols[:, 2:4]
                b1, gamma1, beta1, rmean, rvar = (cols[:, n:n + 1] for n in range(4, 9))
                dve.wait_ge(vec_in, 64)
                for t in range(CT):
                    dve.bn_aggr(ymv[:, t, :], ystats[:, t, :, :].rearrange("p n s -> p (n s)")).then_inc(bn_chain, 1)
                dve.wait_ge(bn_chain, 2)
                dve.tensor_scalar(bvar[:, 0:2], ymv[:, :, 1], BN_EPS, None, ALU.add).then_inc(bn_chain, 1)
                dve.tensor_scalar(bvar[:, 2:3], rvar, BN_EPS, None, ALU.add).then_inc(bn_chain, 1)
                dve.wait_ge(bn_chain, 4)
                dve.tensor_copy(bnt[:, :], bvar[:, :]).then_inc(bn_var, 1)
                dve.wait_ge(bn_var, 1)
                dve.wait_ge(bn_root, 1)
                dve.reciprocal(brs[:, :], brs[:, :]).then_inc(bn_chain, 1)
                dve.wait_ge(bn_chain, 5)
                newton(dve, bn_chain, 5, brs[:, :], bvar[:, :], bnt[:, :])
                dve.tensor_tensor(bsc[:, 0:2], brs[:, 0:2], gamma0, ALU.mult).then_inc(bn_chain, 1)
                dve.tensor_tensor(bsc[:, 2:3], brs[:, 2:3], gamma1, ALU.mult).then_inc(bn_chain, 1)
                dve.wait_ge(bn_chain, 11)
                dve.tensor_tensor(ysh[:, :], ymv[:, :, 0], bsc[:, 0:2], ALU.mult).then_inc(bn_chain, 1)
                dve.tensor_tensor(rsh[:, :], b1, rmean, ALU.subtract).then_inc(bn_chain, 1)
                dve.wait_ge(bn_chain, 13)
                dve.tensor_tensor(ysh[:, :], beta0, ysh[:, :], ALU.subtract).then_inc(bn_ready, 1)
                dve.tensor_tensor(rsh[:, :], rsh[:, :], bsc[:, 2:3], ALU.mult).then_inc(bn_chain, 1)
                dve.wait_ge(bn_chain, 14)
                dve.tensor_tensor(rsh[:, :], rsh[:, :], beta1, ALU.add).then_inc(bn_chain, 1)
                dve.wait_ge(bn_chain, 15)

                def batch(b, s):
                    def step(ins, n):
                        ins.then_inc(chain1, 1)
                        dve.wait_ge(chain1, b * CHAIN + n)

                    for q in range(PIECES):
                        dve.wait_ge(y_scaled, b * (PIECES * CT) + CT * (q + 1))
                        piece = xs[:, s, :, PN * q:PN * q + PN]
                        dve.tensor_tensor(piece, piece, ys[:, q % 2, :, :], ALU.add).then_inc(x1_done, 1)
                        dve.wait_ge(x1_done, b * PIECES + (q + 1))
                        for t in range(CT):
                            for j in (2 * q, 2 * q + 1):
                                dve.bn_stats(st[:, t, j, :], xs[:, s, t, N * j:N * j + N]).then_inc(x1_stats, 1)
                    if isinstance(b, int) and b == 0:
                        dve.wait_ge(w2_hi_done, 1)
                        dve.tensor_tensor(w2_lo[:, :], w2_raw[:, :], w2_hi[:, :].bitcast(F32),
                                          ALU.subtract).then_inc(w2_lo_done, 1)
                    dve.wait_ge(bn_ready, 1)
                    dve.wait_ge(x1_stats, b * (CHUNKS * CT) + CHUNKS * CT)
                    dve.memset(nt1[:, :], 0.0).then_inc(scratch, 1)
                    for t in range(CT):
                        dve.bn_aggr(mv1[:, t, :], st[:, t, :, :].rearrange("p j s -> p (j s)")).then_inc(mean1, 1)
                    dve.wait_ge(gmean1, b + 1)
                    step(dve.tensor_copy(gm1[:, :], cps1[:, 0:CT]), 1)
                    dve.wait_ge(mean1, b * CT + CT)
                    step(dve.tensor_tensor(dm1[:, :], mv1[:, :, 0], gm1[:, :], ALU.subtract), 2)
                    step(dve.tensor_tensor(ev1[:, :], dm1[:, :], dm1[:, :], ALU.mult), 3)
                    dve.tensor_tensor(ev1[:, :], ev1[:, :], mv1[:, :, 1], ALU.add).then_inc(dev1, 1)
                    dve.wait_ge(gvar1, b + 1)
                    dve.tensor_scalar(gv1[:, :], cps1[:, 0:CT], GN_EPS, None, ALU.add).then_inc(gvar1_in, 1)
                    dve.wait_ge(gvar1_in, b + 1)
                    dve.wait_ge(root1, b + 1)
                    step(dve.reciprocal(rt1[:, :], rt1[:, :]), 4)
                    dve.wait_ge(scratch, b + 1)
                    newton(dve, chain1, b * CHAIN + 4, rt1[:, :], gv1[:, :], nt1[:, :])
                    step(dve.tensor_tensor(gm1[:, :], gm1[:, :], rt1[:, :], ALU.mult), 9)
                    step(dve.tensor_copy(nrm[:, :, 0], rt1[:, :]), 10)
                    dve.tensor_scalar(nrm[:, :, 1], gm1[:, :], -1.0, None, ALU.mult).then_inc(norm1, 1)
                    for t in range(CT):
                        dve.tensor_scalar(w1s[:, s, t, :], w1t[:, t, :], rt1[:, t:t + 1], None,
                                          ALU.mult).then_inc(w1_scaled, 1)
                    dve.wait_ge(small_ps, b + 1)
                    dve.tensor_copy(ab[:, b, :, :], cps1[:, 16:16 + 2 * PAIRS].rearrange("p (a n) -> p a n", n=2))\
                        .then_inc(chain1, 1)
                    dve.tensor_scalar(rbias[:, s:s + 1], cps1[:, 64:65], bsc[:, 2:3], rsh[:, :], ALU.mult,
                                      ALU.add).then_inc(small_done, 1)
                    dve.wait_ge(chain1, b * CHAIN + 11)

                batches(dve, batch)

            @block.tensor
            def _(pe):
                pe.wait_ge(vec_in, 64)

                def batch(b, s):
                    pe.wait_ge(mean1, b * CT + CT)
                    positive(pe, small_done, b)
                    pe.matmul(cps1[:, 0:CT], gavg1[:, :], mv1[:, :, 0], start=True, stop=True).then_inc(gmean1, 1)
                    pe.wait_ge(dev1, b + 1)
                    pe.matmul(cps1[:, 0:CT], gavg1[:, :], ev1[:, :], start=True, stop=True).then_inc(gvar1, 1)
                    pe.wait_ge(norm1, b + 1)
                    for p in range(PAIRS):
                        pe.matmul(cps1[:, 16 + 2 * p:18 + 2 * p], sel[:, p % 4, :], nrm[:, p // 4, :],
                                  start=True, stop=True)
                    for t in range(CT):
                        last = pe.matmul(cps1[:, 64:65], w1t[:, t, :], nrm[:, t, 1:2], start=(t == 0), stop=(t == CT - 1))
                    last.then_inc(small_ps, 1)
                    pe.wait_ge(w1_scaled, b * CT + CT)
                    for j in range(CHUNKS):
                        positive(pe, r_copied, b * (4 * CHUNKS) + 4 * (j - 3))
                        for t in range(CT):
                            last = pe.matmul(rps[:, j % 4, :], w1s[:, s, t, :], xs[:, s, t, N * j:N * j + N],
                                             start=(t == 0), stop=(t == CT - 1))
                        last.then_inc(r_ready, 1)

                batches(pe, batch)


def layer1_involution(nc, a, x1_dram, r_dram, w2_dram, out, ab):
    x1_v = x1_dram.rearrange("b (a c) (h w) -> b a c h w", c=PCH, w=W)
    out_v = out.rearrange("b (a c) (q r) w -> b a q c (r w)", c=PCH, q=QUARTERS)
    r_v = r_dram.rearrange("(t s) p (k n) -> t p k s n", s=2, k=POS)
    with ExitStack() as ctx:
        def sb(name, shape, dt=F32):
            return ctx.enter_context(nc.sbuf_tensor(name, shape, dt))

        def sem(name):
            return ctx.enter_context(nc.semaphore(name))

        cols2 = sb("cols2", [PATCH, 2 * BLK, 2, BR, BC])
        r_hi = sb("r_hi", [P, POS, 2, BLK], F32R)
        r_lo = sb("r_lo", [P, POS, 2, BLK], F32R)
        xt = sb("xt", [PATCH, 2, QBLK, P])
        xq = sb("xq", [P, 2, HROWS, W])
        xnq = sb("xnq", [P, NBC, HROWS, PC])
        w2u = sb("w2u", [P, 2, 2, W2_LEN], F32R)
        b2u = sb("b2u", [PATCH, 2, POS])
        abu = sb("abu", [P, 2, 3, 2])
        msk = sb("msk", [P, 3, 2])
        gsel = sb("gsel", [P, 2])
        eps = sb("eps", [P, 1, 1])
        ident = sb("ident", [P, P])
        r_raw = r_lo[:, :, :, :].bitcast(F32)

        aps = ctx.enter_context(nc.psum_tensor("aps", [P, 2, 2, N], F32))
        tps = ctx.enter_context(nc.psum_tensor("tps", [P, 2, N], F32))
        cps = ctx.enter_context(nc.psum_tensor("cps", [P, 2, N], F32))

        PARTS = 4
        PP = POS // PARTS
        TG = QBLK // 4
        CG = QBR + 1

        const_in, r_in, w2_in = sem("const_in"), sem("r_in"), sem("w2u_in")
        xq_in = [sem(f"xq_in{s}") for s in range(2)]
        pads, eps_set = sem("pads"), sem("eps_set")
        r_hi_done, r_lo_done = sem("r_hi_done"), sem("r_lo_done")
        a_ready, a_dve, a_act = sem("a_ready"), sem("a_dve"), sem("a_act")
        norm_here, xn_ready, res_begun = sem("norm_here"), sem("xn_ready"), sem("res_begun")
        t_ready, t_copied = sem("t_ready"), sem("t_copied")
        c_ready, c_first, c_done = sem("c_ready"), sem("c_first"), sem("c_done")
        stored = [sem(f"stored{s}") for s in range(2)]

        def windows(s, r0, r1):
            at = xq[:, s, r0:r1, BC - HALO:BC - HALO + PC]
            dims = [list(d) for d in at.ap]
            return bass.AP(at.tensor, at.offset, [dims[0], [BC, NBC - 2], *dims[1:]])

        def rows_of(bank):
            return cps[:, bank, 0:2 * BR * WHOLE].rearrange("p (g i w) -> p g i w", g=2, i=BR)

        def ends_of(bank):
            return cps[:, bank, 0:2 * QROWS * BC].rearrange("p (g r j) -> p g r j", g=2, j=BC)

        def by_act(k):
            return k % 4 == 3

        def n_act(k):
            return (k + 1) // 4

        def n_dve(k):
            return k + 1 - n_act(k)

        A_ACT, A_DVE = n_act(POS - 1), n_dve(POS - 1)

        def units(engine, begin, unit):
            begin(0)
            unit(0, 0)
            with engine.Fori(1, PAIRS) as p:
                unit(0, p)
            with engine.Fori(1, B // 2) as t:
                begin(t)
                with engine.Fori(0, PAIRS) as p:
                    unit(t, p)

        def at_transposes(k):
            if 1 <= k <= TG:
                return 0, k - 1
            if k >= POS - TG:
                return 1, k - (POS - TG)
            return None

        with nc.Block() as block:

            @block.sync
            def _(sp):
                sp.dma_start(ident[:, :], a["identity"]).then_inc(const_in, 16)
                sp.dma_start(msk[:, :, :], a["row_masks"]).then_inc(const_in, 16)
                sp.dma_start(gsel[:, :], a["group_masks"]).then_inc(const_in, 16)
                sp.wait_ge(pads, 1)

                def begin(t):
                    positive(sp, a_ready, t * (PAIRS * POS))
                    for part in range(PARTS):
                        for s in range(2):
                            sp.dma_start(r_raw[:, PP * part:PP * part + PP, s, :],
                                         r_v[t, :, PP * part:PP * part + PP, s, :]).then_inc(r_in, 16)

                def unit(t, p):
                    u = t * PAIRS + p
                    positive(sp, c_ready, u * (2 * CG) - (2 * CG - 1))
                    sp.dma_start(w2u[:, :, :, :].bitcast(F32).rearrange("p a g n -> p (a g n)"),
                                 w2_dram[p].rearrange("p a n -> p (a n)")).then_inc(w2_in, 16)
                    sp.dma_start(b2u[:, :, :].rearrange("p g k -> p (g k)"), a["b2_band"][p]).then_inc(w2_in, 16)
                    for s in range(2):
                        positive(sp, stored[s], u * (16 * QUARTERS))
                        for q in range(QUARTERS):
                            r0, r1 = max(QROWS * q - HALO, 0), min(QROWS * q + QROWS + HALO, H)
                            d = r0 - (QROWS * q - HALO)
                            sp.dma_start(xq[PCH * q:PCH * q + PCH, s, d:d + r1 - r0, :],
                                         x1_v[2 * t + s, p, :, r0:r1, :]).then_inc(xq_in[s], 16)

                units(sp, begin, unit)

            @block.gpsimd
            def _(pool):
                pool.memset(eps[:, :, :], K1 * K1 * FINFO_EPS).then_inc(eps_set, 1)
                pool.wait_ge(eps_set, 1)
                pool.memset(xq[:, :, :, :], 0.0).then_inc(pads, 1)
                pool.memset(xnq[:, :, :, :], 0.0).then_inc(pads, 1)

                def unit(t, p):
                    u = t * PAIRS + p
                    for s in range(2):
                        pool.wait_ge(xn_ready, u * 2 + (s + 1))
                        inner = xq[:, s, HALO:HALO + QROWS, :]
                        pool.tensor_tensor(inner, inner, eps[:, :, :].to_broadcast([P, QROWS, W]),
                                           ALU.add).then_inc(res_begun, 1)

                units(pool, lambda t: None, unit)

            @block.scalar
            def _(act):
                act.wait_ge(pads, 2)

                def begin(t):
                    positive(act, a_ready, t * (PAIRS * POS))
                    act.wait_ge(r_in, t * (PARTS * 32) + PARTS * 32)
                    for part in range(PARTS):
                        k = slice(PP * part, PP * part + PP)
                        act.activation(r_hi[:, k, :, :], r_raw[:, k, :, :], ACT.Identity).then_inc(r_hi_done, 1)

                def unit(t, p):
                    u = t * PAIRS + p

                    def normalise(s):
                        act.wait_ge(xq_in[s], u * (16 * QUARTERS) + 16 * QUARTERS)
                        act.wait_ge(norm_here, u + 1)
                        positive(act, t_ready, u * (2 * TG) + TG * s)
                        for n, (r0, r1) in enumerate(((HALO, HALO + QROWS), (0, HALO), (HALO + QROWS, HROWS))):
                            over = BC * (NBC - 1) - HALO
                            for dst, src in (
                                (xnq[:, 0, r0:r1, HALO:PC], xq[:, s, r0:r1, 0:PC - HALO]),
                                (xnq[:, NBC - 1, r0:r1, 0:W - over], xq[:, s, r0:r1, over:W]),
                                (xnq[:, 1:NBC - 1, r0:r1, :], windows(s, r0, r1)),
                            ):
                                last = act.activation(dst, src, ACT.Identity, bias=abu[:, s, n, 1:2],
                                                      scale=abu[:, s, n, 0:1])
                        last.then_inc(xn_ready, 1)

                    normalise(0)
                    for k in range(POS):
                        if by_act(k):
                            act.wait_ge(a_ready, u * POS + (k + 1))
                            positive(act, c_ready, u * (2 * CG))
                            for g in range(2):
                                last = act.activation(cols2[:, :, g, k // BC, k % BC],
                                                      aps[0:PATCH, k % 2, g, 0:2 * BLK], ACT.Identity,
                                                      bias=b2u[:, g, k:k + 1])
                            last.then_inc(a_act, 1)
                        if at_transposes(k):
                            s, g = at_transposes(k)
                            n = s * TG + g
                            act.wait_ge(t_ready, u * (2 * TG) + (n + 1))
                            positive(act, c_ready, u * (2 * CG))
                            act.activation(xt[:, s, 4 * g:4 * g + 4, :].rearrange("p n c -> p (n c)"),
                                           tps[0:PATCH, n % 2, :], ACT.Identity).then_inc(t_copied, 1)
                        if k == TG:
                            normalise(1)
                    for s in range(2):
                        act.wait_ge(c_done, u * (2 * CG) + CG * (s + 1))
                        for q in range(QUARTERS):
                            act.dma_start(out_v[2 * t + s, p, q],
                                          xq[PCH * q:PCH * q + PCH, s, HALO:HALO + QROWS, :].rearrange("p r w -> p (r w)"))\
                                .then_inc(stored[s], 16)

                units(act, begin, unit)
                for s in range(2):
                    act.wait_ge(stored[s], 16 * QUARTERS * PAIRS * B // 2)

            @block.vector
            def _(dve):
                dve.wait_ge(const_in, 48)

                def begin(t):
                    for part in range(PARTS):
                        k = slice(PP * part, PP * part + PP)
                        dve.wait_ge(r_hi_done, t * PARTS + (part + 1))
                        dve.tensor_tensor(r_lo[:, k, :, :], r_raw[:, k, :, :], r_hi[:, k, :, :].bitcast(F32),
                                          ALU.subtract).then_inc(r_lo_done, 1)

                def unit(t, p):
                    u = t * PAIRS + p
                    positive(dve, xn_ready, 2 * u)
                    for s in range(2):
                        last = dve.tensor_tensor(abu[:, s, :, :],
                                                 ab[:, 2 * t + s, p, :].rearrange("p (o n) -> p o n", o=1).to_broadcast([P, 3, 2]),
                                                 msk[:, :, :], ALU.mult)
                    last.then_inc(norm_here, 1)
                    for k in range(POS):
                        if not by_act(k):
                            dve.wait_ge(a_ready, u * POS + (k + 1))
                            positive(dve, c_ready, u * (2 * CG))
                            dve.tensor_tensor(cols2[:, :, :, k // BC, k % BC].rearrange("p n g -> p g n"),
                                              aps[0:PATCH, k % 2, :, 0:2 * BLK],
                                              b2u[:, :, k:k + 1].to_broadcast([PATCH, 2, 2 * BLK]),
                                              ALU.add).then_inc(a_dve, 1)
                    for s in range(2):
                        dve.wait_ge(res_begun, u * 2 + (s + 1))
                        for c in range(CG):
                            n = s * CG + c
                            dve.wait_ge(c_ready, u * (2 * CG) + (n + 1))
                            if c < QBR:
                                src = rows_of(n % 2)
                                dst = xq[:, s, HALO + BR * c:HALO + BR * c + BR, 0:WHOLE]
                            else:
                                src = ends_of(n % 2)[:, :, :, 0:W - WHOLE]
                                dst = xq[:, s, HALO:HALO + QROWS, WHOLE:W]
                            dve.scalar_tensor_tensor(dst, src[:, 1], gsel[:, 1:2], dst, op0=ALU.mult,
                                                     op1=ALU.add).then_inc(c_first, 1)
                            dve.wait_ge(c_first, u * (2 * CG) + (n + 1))
                            dve.scalar_tensor_tensor(dst, src[:, 0], gsel[:, 0:1], dst, op0=ALU.mult,
                                                     op1=ALU.add).then_inc(c_done, 1)

                units(dve, begin, unit)

            @block.tensor
            def _(pe):
                pe.wait_ge(const_in, 48)

                def unit(t, p):
                    u = t * PAIRS + p
                    pe.wait_ge(w2_in, u * 32 + 32)
                    for k in range(POS):
                        i, j = k // BC, k % BC
                        if k % PP == 0:
                            pe.wait_ge(r_lo_done, t * PARTS + (k // PP + 1))
                        back = k - 2
                        if back >= 0:
                            if by_act(back):
                                pe.wait_ge(a_act, u * A_ACT + n_act(back))
                            else:
                                pe.wait_ge(a_dve, u * A_DVE + n_dve(back))
                        elif by_act(back + POS):
                            positive(pe, a_act, u * A_ACT)
                        else:
                            positive(pe, a_dve, u * A_DVE)
                        for g in range(2):
                            terms = ((0, r_hi), (0, r_lo), (1, r_hi))
                            for n, (part, r) in enumerate(terms):
                                last = pe.matmul(aps[0:PATCH, k % 2, g, 0:2 * BLK],
                                                 w2u[:, part, g, W2_AT - PC * i - j:W2_AT - PC * i - j + PATCH],
                                                 r[:, k, :, :].rearrange("p s n -> p (s n)"),
                                                 start=(n == 0), stop=(n == 2))
                        last.then_inc(a_ready, 1)
                        if at_transposes(k):
                            s, g = at_transposes(k)
                            n = s * TG + g
                            if g == 0:
                                pe.wait_ge(xn_ready, u * 2 + (s + 1))
                            positive(pe, t_copied, u * (2 * TG) + (n - 1))
                            for m in range(4):
                                r, c = (4 * g + m) // NBC, (4 * g + m) % NBC
                                last = pe.transpose(tps[0:PATCH, n % 2, P * m:P * m + P],
                                                    xnq[:, c, BR * r:BR * r + PR, :].rearrange("p r c -> p (r c)"), ident[:, :])
                            last.then_inc(t_ready, 1)
                    pe.wait_ge(a_act, u * A_ACT + A_ACT)
                    pe.wait_ge(a_dve, u * A_DVE + A_DVE)
                    for s in range(2):
                        pe.wait_ge(t_copied, u * (2 * TG) + TG * (s + 1))
                        for c in range(CG):
                            n = s * CG + c
                            positive(pe, c_done, u * (2 * CG) + (n - 1))
                            blocks = [(c, m) for m in range(W // BC)] if c < QBR else [(m, W // BC) for m in range(QBR)]
                            for m, (r, col) in enumerate(blocks):
                                if c < QBR:
                                    dst = rows_of(n % 2)[:, :, :, BC * m:BC * m + BC]
                                else:
                                    dst = ends_of(n % 2)[:, :, BR * m:BR * m + BR, :]
                                for q in range(QUARTERS):
                                    at = s * BLK + (QBR * q + r) * NBC + col
                                    last = pe.matmul(dst[PCH * q:PCH * q + PCH],
                                                     xt[:, s, r * NBC + col, PCH * q:PCH * q + PCH],
                                                     cols2[:, at, :, :, :].rearrange("p g i j -> p (g i j)"),
                                                     start=True, stop=True)
                            last.then_inc(c_ready, 1)

                units(pe, lambda t: None, unit)


def kernel(**inputs):
    import numpy as np
    import concourse.bacc as bacc
    from concourse.bass_utils import run_bass_kernel_spmd

    nc = bacc.Bacc("TRN2", target_bir_lowering=False, num_devices=1)
    i = {n: np.ascontiguousarray(v) for n, v in inputs.items()}

    wf_t = i["L0_conv_W_filter"].reshape(CT, P, K0, CT, P).transpose(4, 3, 0, 2, 1)
    wp_t = i["L0_conv_W_proj"].reshape(C, CT, P).transpose(2, 1, 0)
    vectors = [i[n].reshape(-1, P).T for n in ("L0_conv_gamma", "L0_conv_beta", "L1_conv_b1", "L1_conv_gamma",
                                               "L1_conv_beta", "L1_conv_run_mean", "L1_conv_run_var")]
    taps = i["L1_conv_w2"].reshape(GROUPS, K1, K1, RED)
    w2_pad = np.zeros((RED, GROUPS, W2_LEN), np.float32)
    for r in range(K1):
        w2_pad[:, :, W2_AT + PC * r:W2_AT + PC * r + K1] = taps[:, r].transpose(2, 0, 1)
    b2_band = np.zeros((PAIRS, 2, BR, BC, PR, PC), np.float32)
    b2 = i["L1_conv_b2"].reshape(PAIRS, 2, K1, K1)
    for r in range(BR):
        for c in range(BC):
            b2_band[:, :, r, c, r:r + K1, c:c + K1] = b2
    c = np.arange(C)
    shifts = np.stack([(c[:, None] == c[None, :] + d) for d in (-1, 0, 1)]).astype(np.float32)
    p = np.arange(P)
    group_average = ((p[:, None] // GN_CH == p[None, :] // GN_CH) / GN_CH).astype(np.float32)
    select = np.stack([(p[:, None] == PCH * n + p[None, :] % PCH) for n in range(4)], 1).astype(np.float32)
    quarter = p // PCH
    row_masks = np.stack([quarter >= 0, quarter > 0, quarter < QUARTERS - 1], 1).astype(np.float32)
    group_masks = np.stack([p % PCH // GC == n for n in range(2)], 1).astype(np.float32)
    arrays = {
        "x": i["x"], "wf_t": wf_t.reshape(P, -1), "wp_t": wp_t.reshape(P, -1),
        "b_filter": i["L0_conv_b_filter"].reshape(CT, P, K0).transpose(1, 0, 2), "w_eca": i["L0_conv_w_eca"],
        "b_proj": i["L0_conv_b_proj"].reshape(CT, P).T,
        "columns": np.concatenate(vectors, 1), "w1_t": i["L1_conv_w1"].reshape(RED, CT, P).transpose(2, 1, 0),
        "w2_pad": w2_pad.reshape(RED, -1), "b2_band": b2_band.transpose(0, 4, 5, 1, 2, 3).reshape(PAIRS, PATCH, 2 * POS),
        "shifts": shifts, "group_average": group_average, "select": select,
        "row_masks": np.repeat(row_masks[:, :, None], 2, 2), "group_masks": group_masks,
        "identity": np.eye(P, dtype=np.float32),
    }
    arrays = {n: np.ascontiguousarray(v) for n, v in arrays.items()}
    a = {n: nc.dram_tensor(n, v.shape, F32, kind="ExternalInput").ap() for n, v in arrays.items()}
    y_dram = nc.dram_tensor("y", (B, C, PX), F32, kind="Internal").ap()
    x1_dram = nc.dram_tensor("x1", (B, C, PX), F32, kind="Internal").ap()
    r_dram = nc.dram_tensor("r", (B, P, POS * BLK), F32, kind="Internal").ap()
    w2_dram = nc.dram_tensor("w2_parts", (PAIRS, P, 2, 2 * W2_LEN), F32, kind="Internal").ap()
    out = nc.dram_tensor("out", (B, C, H, W), F32, kind="ExternalOutput").ap()
    build(nc, a, y_dram, x1_dram, r_dram, w2_dram, out)
    return run_bass_kernel_spmd(nc, [arrays], core_ids=[0]).results[0]["out"]
```

```python
import concourse.bass as bass
from concourse import mybir
from contextlib import ExitStack

F32 = mybir.dt.float32
F32R = mybir.dt.float32r
ALU = mybir.AluOpType
ACT = mybir.ActivationFunctionType

P = 128
B, C, H, W = 8, 256, 64, 64
CT = C // P
PX = H * W
GN_CH = C // 32
GN_EPS = 1e-5
BN_EPS = 1e-5
K0 = 9
ROWS = 8
N = ROWS * W
CHUNKS = H // ROWS
WP = W + 2
HP = H + 2
TAPS = CT * K0
RING = 6
K1 = 7
HALO = K1 // 2
GROUPS = 16
RED = C // 2
BR, BC = 4, 6
PR, PC = BR + K1 - 1, BC + K1 - 1
PATCH = PR * PC
POS = BR * BC
NBR = H // BR
NBC = -(-W // BC)
BLK = NBR * NBC
WHOLE = W // BC * BC
QUARTERS = 4
QROWS = H // QUARTERS
QBR = QROWS // BR
QBLK = QBR * NBC
HROWS = QROWS + 2 * HALO
PAIRS = 8
PCH = C // PAIRS
GC = C // GROUPS
W2_AT = PC * (BR - 1) + BC - 1
W2_LEN = W2_AT + PATCH + 1
FINFO_EPS = 2.0 ** -23


def positive(engine, semaphore, value):
    if not isinstance(value, int) or value > 0:
        engine.wait_ge(semaphore, value)


def build(nc, a, y_dram, x1_dram, r_dram, w2_dram, out):
    with ExitStack() as ctx:
        ab = ctx.enter_context(nc.sbuf_tensor("ab", [P, B, PAIRS, 2], F32))
        with nc.sbuf_tensor("ystats", [P, CT, B * CHUNKS, 6], F32) as ystats:
            layer0(nc, a, y_dram, ystats)
            layer1_features(nc, a, y_dram, x1_dram, r_dram, w2_dram, ystats, ab)
        layer1_involution(nc, a, x1_dram, r_dram, w2_dram, out, ab)


def newton(dve, sem, count, rstd, var, tmp):
    steps = (
        lambda: dve.tensor_tensor(tmp, rstd, rstd, ALU.mult),
        lambda: dve.tensor_tensor(tmp, tmp, var, ALU.mult),
        lambda: dve.tensor_scalar(tmp, tmp, -0.5, 1.5, ALU.mult, ALU.add),
        lambda: dve.tensor_tensor(rstd, rstd, tmp, ALU.mult),
    )
    for n, step in enumerate(steps):
        step().then_inc(sem, 1)
        dve.wait_ge(sem, count + n + 1)


def layer0(nc, a, y_dram, ystats):
    x_v = a["x"].rearrange("b (t p) h w -> b p t h w", p=P)
    y_v = y_dram.rearrange("b (t p) n -> b t p n", p=P)

    with ExitStack() as ctx:
        def sb(name, shape, dt=F32):
            return ctx.enter_context(nc.sbuf_tensor(name, shape, dt))

        def sem(name):
            return ctx.enter_context(nc.semaphore(name))

        wf_hi = sb("wf_hi", [P, CT, CT, K0, P], F32R)
        wf_lo = sb("wf_lo", [P, CT, CT, K0, P], F32R)
        wp_hi = sb("wp_hi", [P, CT, C], F32R)
        wp_lo = sb("wp_lo", [P, CT, C], F32R)
        xn = sb("xn", [P, 2, CT, HP, WP])
        prod = sb("prod", [P, 2, K0, N])
        sums = sb("sums", [P, 2, 4, N])
        fused = sb("fused", [P, 2, N])
        fu_hi = sb("fu_hi", [P, 2, CT, N], F32R)
        fu_lo = sb("fu_lo", [P, 2, CT, N], F32R)
        x_hi = sb("x_hi", [P, 2, CT, N], F32R)
        x_lo = sb("x_lo", [P, 2, CT, N], F32R)
        ybuf = sb("ybuf", [P, 2, N])
        bf = sb("bf", [P, CT, K0])
        bfc = sb("bfc", [P, 2, CT])
        bp = sb("bp", [P, CT])
        weca = sb("weca", [P, 3])
        band = sb("band", [P, CT, C])
        gavg = sb("gavg", [P, P])
        xst = sb("xst", [P, CT, CHUNKS, 6])
        mv = sb("mv", [P, CT, 2])
        gm = sb("gm", [P, CT])
        dm = sb("dm", [P, CT])
        ev = sb("ev", [P, CT])
        gv = sb("gv", [P, CT])
        rstd = sb("rstd", [P, CT])
        nt = sb("nt", [P, CT])
        nb = sb("nb", [P, CT])
        pooled = sb("pooled", [P, CT])
        attn = sb("attn", [P, CT])
        raw = prod[:, :, :, :].rearrange("p s k n -> p (s k n)")
        NF = CT * CT * K0 * P
        wf_raw = raw[:, 0:NF]
        wp_raw = raw[:, NF:NF + CT * C]
        sh_raw = raw[:, NF + CT * C:NF + CT * C + 3 * CT * C].rearrange("p (s t c) -> p s t c", s=3, t=CT)

        filt = ctx.enter_context(nc.psum_tensor("filt", [P, RING, N], F32))
        yps = ctx.enter_context(nc.psum_tensor("yps", [P, N], F32))
        sps = ctx.enter_context(nc.psum_tensor("sps", [P, N], F32))

        consts_in, filters_in = sem("consts_in"), sem("filters_in")
        x_in = sem("x_in")
        zeroed = sem("zeroed")
        w_hi_done, w_lo_done = sem("w_hi_done"), sem("w_lo_done")
        xn_done = sem("xn_done")
        x_hi_done, x_lo_done = sem("x_hi_done"), sem("x_lo_done")
        tap_ready, tap_used = sem("tap_ready"), sem("tap_used")
        pair_sums = sem("pair_sums")
        pool_sums = sem("pool_sums")
        half_sum, fused_done = sem("half_sum"), sem("fused_done")
        fu_hi_done, fu_lo_done = sem("fu_hi_done"), sem("fu_lo_done")
        y_ready, y_copied, y_stats = sem("y_ready"), sem("y_copied"), sem("y_stats")
        y_out = [sem(f"y_out{m}") for m in range(CT)]
        x_stats, chain, band_step = sem("x_stats"), sem("chain"), sem("band_step")
        mean_in, gmean_ps, dev_in, gvar_ps = sem("mean_in"), sem("gmean_ps"), sem("dev_in"), sem("gvar_ps")
        gvar_in, root = sem("gvar_in"), sem("root")
        norm_ready, eca_ps, attn_done, centre_done = sem("norm_ready"), sem("eca_ps"), sem("attn_done"), sem("centre_done")

        CHAIN = 10
        LAST = B - 1
        NPARTS = 3 * CT

        def batches(engine, body):
            body(0, 0, True, False)
            with engine.Fori(0, (LAST - 1) // 2) as two:
                body(2 * two + 1, 1, False, False)
                body(2 * two + 2, 0, False, False)
            body(LAST, 1, False, True)

        with nc.Block() as block:

            @block.sync
            def _(sp):
                sp.dma_start(gavg[:, :], a["group_average"]).then_inc(consts_in, 16)
                sp.dma_start(sh_raw, a["shifts"].rearrange("s (t p) c -> p s t c", p=P)).then_inc(consts_in, 16)
                sp.dma_start(weca[:, :], a["w_eca"].rearrange("(o k) -> o k", o=1).to_broadcast([P, 3])).then_inc(consts_in, 16)
                sp.dma_start(bf[:, :, :], a["b_filter"]).then_inc(consts_in, 16)
                sp.dma_start(bp[:, :], a["b_proj"]).then_inc(consts_in, 16)
                sp.wait_ge(zeroed, 2)
                for t in range(CT):
                    for h in range(2):
                        sp.dma_start(xn[:, 0, t, 1 + 32 * h:33 + 32 * h, 1:1 + W],
                                     x_v[0, :, t, 32 * h:32 * h + 32, :]).then_inc(x_in, 16)
                sp.dma_start(wf_raw, a["wf_t"]).then_inc(filters_in, 16)
                sp.dma_start(wp_raw, a["wp_t"]).then_inc(filters_in, 16)

                for b in range(1, B):
                    sp.wait_ge(x_in, (b * 2 * CT) * 16)
                    positive(sp, tap_used, (b - 1) * CHUNKS * TAPS)
                    for t in range(CT):
                        for h in range(2):
                            sp.dma_start(xn[:, b % 2, t, 1 + 32 * h:33 + 32 * h, 1:1 + W],
                                         x_v[b, :, t, 32 * h:32 * h + 32, :]).then_inc(x_in, 16)

            @block.gpsimd
            def _(pool):
                pool.memset(xn[:, 0, :, :, :], 0.0).then_inc(zeroed, 1)
                pool.memset(xn[:, 1, :, :, :], 0.0).then_inc(zeroed, 1)

                def split_x(b, j, s):
                    n1 = b * CHUNKS + (j + 1)
                    pool.wait_ge(x_hi_done, n1)
                    for t in range(CT):
                        src = xn[:, s, t, 1 + ROWS * j:1 + ROWS * j + ROWS, 1:1 + W]
                        last = pool.tensor_tensor(x_lo[:, j % 2, t, :].rearrange("p (h w) -> p h w", w=W), src,
                                                  x_hi[:, j % 2, t, :].bitcast(F32).rearrange("p (h w) -> p h w", w=W),
                                                  ALU.subtract)
                    last.then_inc(x_lo_done, 1)

                split_x(0, 0, 0)

                def batch(b, s, first, last):
                    for j in range(CHUNKS):
                        for t in range(CT):
                            i = b * (CHUNKS * CT) + (j * CT + t)
                            done = b * (CHUNKS * TAPS) + (j * TAPS + t * K0)
                            positive(pool, fused_done, i - 1)
                            pool.wait_ge(tap_used, done + 4)
                            pool.tensor_tensor(sums[:, t, 0:2, :], prod[:, t, 0:2, :], prod[:, t, 2:4, :],
                                               ALU.add).then_inc(pair_sums, 1)
                            pool.wait_ge(tap_used, done + 8)
                            pool.tensor_tensor(sums[:, t, 2:4, :], prod[:, t, 4:6, :], prod[:, t, 6:8, :],
                                               ALU.add).then_inc(pair_sums, 1)
                            pool.wait_ge(pair_sums, 2 * i + 2)
                            pool.tensor_tensor(sums[:, t, 0:2, :], sums[:, t, 0:2, :], sums[:, t, 2:4, :],
                                               ALU.add).then_inc(pool_sums, 1)
                            if t == 0 and not (last and j == CHUNKS - 1):
                                if j < CHUNKS - 1:
                                    split_x(b, j + 1, s)
                                else:
                                    split_x(b + 1, 0, 1 - s)

                batches(pool, batch)

            @block.scalar
            def _(act):
                PARTS = (0, 2, 5, CHUNKS)

                def normalise(b, s, parts):
                    act.wait_ge(norm_ready, b + 1)
                    for part in parts:
                        r0, r1 = PARTS[part] * ROWS, PARTS[part + 1] * ROWS
                        for t in range(CT):
                            v = xn[:, s, t, 1 + r0:1 + r1, 1:1 + W]
                            act.activation(v, v, ACT.Identity, bias=nb[:, t:t + 1],
                                           scale=rstd[:, t:t + 1]).then_inc(xn_done, 1)

                def split_x(b, j, s):
                    n = b * CHUNKS + j
                    part = 1 if j < 2 else 2 if j < 5 else 3
                    act.wait_ge(xn_done, b * NPARTS + CT * part)
                    positive(act, tap_ready, (n - 1) * TAPS)
                    positive(act, x_lo_done, n - 1)
                    for t in range(CT):
                        src = xn[:, s, t, 1 + ROWS * j:1 + ROWS * j + ROWS, 1:1 + W]
                        last = act.activation(x_hi[:, j % 2, t, :].rearrange("p (h w) -> p h w", w=W), src, ACT.Identity)
                    last.then_inc(x_hi_done, 1)

                def split_fused(b, j, t):
                    i = b * (CHUNKS * CT) + (j * CT + t)
                    act.wait_ge(fused_done, i + 1)
                    positive(act, y_ready, b * (CHUNKS * CT) + (j * CT - CT))
                    positive(act, fu_lo_done, i - 3)
                    act.activation(fu_hi[:, j % 2, t, :], fused[:, t, :], ACT.Identity).then_inc(fu_hi_done, 1)

                def copy_y(b, j, m):
                    yi = b * (CHUNKS * CT) + (j * CT + m)
                    act.wait_ge(y_ready, yi + 1)
                    positive(act, y_out[m], b * (16 * CHUNKS) + 16 * j)
                    positive(act, y_stats, yi - 1)
                    act.activation(ybuf[:, m, :], yps[:, :], ACT.Identity, bias=bp[:, m:m + 1],
                                   scale=0.5).then_inc(y_copied, 1)
                    act.wait_ge(y_copied, yi + 1)
                    at = N * (j % CHUNKS)
                    act.dma_start(y_v[b if j >= 0 else b - 1, m, :, at:at + N], ybuf[:, m, :]).then_inc(y_out[m], 16)

                def sqrt(b1):
                    act.wait_ge(gvar_in, b1 + 1)
                    act.activation(rstd[:, :], gv[:, :], ACT.Sqrt).then_inc(root, 1)

                def attention(b1):
                    act.wait_ge(eca_ps, b1 + 1)
                    positive(act, centre_done, b1)
                    act.activation(attn[:, :], sps[:, 0:CT], ACT.Sigmoid).then_inc(attn_done, 1)

                act.wait_ge(filters_in, 32)
                act.activation(wf_hi[:, :, :, :, :].rearrange("p a b k n -> p (a b k n)"), wf_raw,
                               ACT.Identity).then_inc(w_hi_done, 1)
                act.activation(wp_hi[:, :, :].rearrange("p t n -> p (t n)"), wp_raw, ACT.Identity).then_inc(w_hi_done, 1)
                sqrt(0)
                normalise(0, 0, (0,))
                split_x(0, 0, 0)
                normalise(0, 0, (1, 2))
                attention(0)

                def batch(b, s, first, last):
                    for j in range(CHUNKS):
                        i = b * (CHUNKS * CT) + j * CT
                        if j < CHUNKS - 1:
                            split_x(b, j + 1, s)
                        elif not last:
                            normalise(b + 1, 1 - s, (0,))
                            split_x(b + 1, 0, 1 - s)
                            attention(b + 1)
                        if not (first and j == 0):
                            copy_y(b, j - 1, 0)
                        split_fused(b, j, 0)
                        if not last and j == CHUNKS - 2:
                            sqrt(b + 1)
                        if not last and j == CHUNKS - 1:
                            normalise(b + 1, 1 - s, (1, 2))
                        if not (first and j == 0):
                            copy_y(b, j - 1, 1)
                        split_fused(b, j, 1)

                batches(act, batch)
                copy_y(LAST, CHUNKS - 1, 0)
                copy_y(LAST, CHUNKS - 1, 1)
                for m in range(CT):
                    act.wait_ge(y_out[m], 16 * B * CHUNKS)

            @block.vector
            def _(dve):
                def stats(b1, s, j):
                    for t in range(CT):
                        src = xn[:, s, t, 1 + ROWS * j:1 + ROWS * j + ROWS, 1:1 + W]
                        dve.wait_ge(x_in, b1 * (16 * 2 * CT) + 16 * 2 * CT)
                        dve.bn_stats(xst[:, t, j, :], src).then_inc(x_stats, 1)

                def step(ins, b1, n):
                    ins.then_inc(chain, 1)
                    dve.wait_ge(chain, b1 * CHAIN + n)

                def mean(b1):
                    for t in range(CT):
                        dve.bn_aggr(mv[:, t, :], xst[:, t, :, :].rearrange("p j s -> p (j s)")).then_inc(mean_in, 1)

                def deviation(b1):
                    dve.wait_ge(gmean_ps, b1 + 1)
                    step(dve.tensor_copy(gm[:, :], sps[:, 0:CT]), b1, 1)
                    dve.wait_ge(mean_in, b1 * CT + CT)
                    step(dve.tensor_tensor(dm[:, :], mv[:, :, 0], gm[:, :], ALU.subtract), b1, 2)
                    step(dve.tensor_tensor(ev[:, :], dm[:, :], dm[:, :], ALU.mult), b1, 3)
                    dve.tensor_tensor(ev[:, :], ev[:, :], mv[:, :, 1], ALU.add).then_inc(dev_in, 1)

                def variance(b1):
                    dve.wait_ge(gvar_ps, b1 + 1)
                    dve.tensor_scalar(gv[:, :], sps[:, 0:CT], GN_EPS, None, ALU.add).then_inc(gvar_in, 1)

                def norm(b1):
                    dve.wait_ge(gvar_in, b1 + 1)
                    dve.wait_ge(root, b1 + 1)
                    step(dve.reciprocal(rstd[:, :], rstd[:, :]), b1, 4)
                    newton(dve, chain, b1 * CHAIN + 4, rstd[:, :], gv[:, :], nt[:, :])
                    step(dve.tensor_tensor(pooled[:, :], dm[:, :], rstd[:, :], ALU.mult), b1, 9)
                    step(dve.tensor_tensor(nb[:, :], gm[:, :], rstd[:, :], ALU.mult), b1, 10)
                    dve.tensor_scalar(nb[:, :], nb[:, :], -1.0, None, ALU.mult).then_inc(norm_ready, 1)

                def centre(b1, s):
                    dve.wait_ge(attn_done, b1 + 1)
                    dve.tensor_tensor(bfc[:, s, :], bf[:, :, K0 // 2], attn[:, :], ALU.add).then_inc(centre_done, 1)

                def fuse(i, t):
                    dve.wait_ge(pool_sums, i + 1)
                    positive(dve, fu_hi_done, i - 1)
                    positive(dve, fu_lo_done, i - 1)
                    dve.tensor_tensor(fused[:, t, :], sums[:, t, 0, :], sums[:, t, 1, :], ALU.add).then_inc(half_sum, 1)
                    dve.wait_ge(half_sum, i + 1)
                    dve.tensor_tensor(fused[:, t, :], fused[:, t, :], prod[:, t, K0 - 1, :], ALU.add).then_inc(fused_done, 1)

                def split_fused(i, j, t):
                    dve.wait_ge(fu_hi_done, i + 1)
                    dve.wait_ge(fused_done, i + 1)
                    positive(dve, y_ready, i - t - CT)
                    dve.tensor_tensor(fu_lo[:, j % 2, t, :], fused[:, t, :], fu_hi[:, j % 2, t, :].bitcast(F32),
                                      ALU.subtract).then_inc(fu_lo_done, 1)

                def take_y_stats(yi, m, col):
                    dve.wait_ge(y_copied, yi + 1)
                    dst = ystats[:, m, col, :]
                    dve.bn_stats(dst, ybuf[:, m, :]).then_inc(y_stats, 1)

                for j in range(CHUNKS):
                    stats(0, 0, j)
                dve.wait_ge(x_stats, CHUNKS * CT)
                mean(0)
                dve.wait_ge(consts_in, 16 * 5)
                dve.tensor_scalar(band[:, :, :], sh_raw[:, 0, :, :], weca[:, 0:1], None, ALU.mult).then_inc(band_step, 1)
                for n in (1, 2):
                    dve.wait_ge(band_step, n)
                    dve.scalar_tensor_tensor(band[:, :, :], sh_raw[:, n, :, :], weca[:, n:n + 1], band[:, :, :],
                                             op0=ALU.mult, op1=ALU.add).then_inc(band_step, 1)
                deviation(0)
                variance(0)
                norm(0)
                dve.wait_ge(w_hi_done, 2)
                dve.tensor_tensor(wf_lo[:, :, :, :, :].rearrange("p a b k n -> p (a b k n)"), wf_raw,
                                  wf_hi[:, :, :, :, :].rearrange("p a b k n -> p (a b k n)").bitcast(F32),
                                  ALU.subtract).then_inc(w_lo_done, 1)
                dve.tensor_tensor(wp_lo[:, :, :].rearrange("p t n -> p (t n)"), wp_raw,
                                  wp_hi[:, :, :].rearrange("p t n -> p (t n)").bitcast(F32),
                                  ALU.subtract).then_inc(w_lo_done, 1)
                centre(0, 0)
                dve.wait_ge(w_lo_done, 2)
                dve.wait_ge(band_step, 3)
                dve.wait_ge(centre_done, 1)

                def batch(b, s, first, last):
                    for j in range(CHUNKS):
                        dve.wait_ge(xn_done, b * NPARTS + CT * (1 if j < 1 else 2 if j < 4 else 3))
                        for t in range(CT):
                            i = b * (CHUNKS * CT) + (j * CT + t)
                            done = b * (CHUNKS * TAPS) + (j * TAPS + t * K0)
                            positive(dve, fused_done, i - 1)
                            for k in range(K0):
                                dve.wait_ge(tap_ready, done + k + 1)
                                patch = xn[:, s, t, ROWS * j + k // 3:ROWS * j + k // 3 + ROWS, k % 3:k % 3 + W]
                                bias = bf[:, t, k:k + 1] if k != K0 // 2 else bfc[:, s, t:t + 1]
                                dve.scalar_tensor_tensor(prod[:, t, k, :].rearrange("p (h w) -> p h w", w=W),
                                                         filt[:, (t * K0 + k) % RING, :].rearrange("p (h w) -> p h w", w=W),
                                                         bias, patch, op0=ALU.add, op1=ALU.mult).then_inc(tap_used, 1)
                                if (j, t, k) == (0, 0, 2):
                                    dve.wait_ge(centre_done, b + 1)
                                if k == 2 and not (first and j * CT + t < 3):
                                    back = j * CT + t - 3
                                    take_y_stats(b * (CHUNKS * CT) + back, back % CT, b * CHUNKS + back // CT)
                                if k == 3 and not last and 1 <= j <= 4:
                                    stats(b + 1, 1 - s, 2 * (j - 1) + t)
                                if k == 3 and not last and (j, t) == (6, 1):
                                    variance(b + 1)
                                if k == 5 and not last and (j, t) == (4, 1):
                                    dve.wait_ge(x_stats, b * (CHUNKS * CT) + 2 * CHUNKS * CT)
                                if k == 5 and not (first and j * CT + t < 1):
                                    fuse(i - 1, (t - 1) % CT)
                                if k == 7 and not (first and j * CT + t < 1):
                                    split_fused(i - 1, j if t else j - 1, (t - 1) % CT)
                        if not last and j == 4:
                            mean(b + 1)
                        if not last and j == 5:
                            deviation(b + 1)
                        if not last and j == 6:
                            norm(b + 1)
                        if not last and j == 7:
                            centre(b + 1, 1 - s)

                batches(dve, batch)
                items = B * CHUNKS * CT
                fuse(items - 1, CT - 1)
                split_fused(items - 1, CHUNKS - 1, CT - 1)
                for back in (3, 2, 1):
                    take_y_stats(items - back, (items - back) % CT, (items - back) // CT)
                dve.wait_ge(y_stats, items)

            @block.tensor
            def _(pe):
                def group_mean(b1):
                    pe.wait_ge(mean_in, b1 * CT + CT)
                    positive(pe, attn_done, b1)
                    pe.matmul(sps[:, 0:CT], gavg[:, :], mv[:, :, 0], start=True, stop=True).then_inc(gmean_ps, 1)

                def group_var(b1):
                    pe.wait_ge(dev_in, b1 + 1)
                    pe.matmul(sps[:, 0:CT], gavg[:, :], ev[:, :], start=True, stop=True).then_inc(gvar_ps, 1)

                def eca(b1):
                    pe.wait_ge(norm_ready, b1 + 1)
                    for m in range(CT):
                        for t in range(CT):
                            last = pe.matmul(sps[:, m:m + 1], band[:, t, P * m:P * m + P], pooled[:, t:t + 1],
                                             start=(t == 0), stop=(t == CT - 1))
                    last.then_inc(eca_ps, 1)

                def split_products(dst, w_hi, w_lo, v_hi, v_lo):
                    terms = [(w, v, t) for t in range(CT) for w, v in ((w_hi, v_hi), (w_hi, v_lo), (w_lo, v_hi))]
                    for n, (w, v, t) in enumerate(terms):
                        last = pe.matmul(dst, w(t), v(t), start=(n == 0), stop=(n == len(terms) - 1))
                    return last

                def taps(b, j, t):
                    n = b * CHUNKS + j
                    if t == 0:
                        pe.wait_ge(x_lo_done, n + 1)
                    for k in range(K0):
                        positive(pe, tap_used, n * TAPS + (t * K0 + k + 1 - RING))
                        split_products(filt[:, (t * K0 + k) % RING, :],
                                       lambda c: wf_hi[:, c, t, k, :], lambda c: wf_lo[:, c, t, k, :],
                                       lambda c: x_hi[:, j % 2, c, :], lambda c: x_lo[:, j % 2, c, :]).then_inc(tap_ready, 1)

                def project(b, j, m):
                    yi = b * (CHUNKS * CT) + (j * CT + m)
                    pe.wait_ge(fu_lo_done, b * (CHUNKS * CT) + (j * CT + CT))
                    positive(pe, y_copied, yi)
                    split_products(yps[:, :],
                                   lambda c: wp_hi[:, c, P * m:P * m + P], lambda c: wp_lo[:, c, P * m:P * m + P],
                                   lambda c: fu_hi[:, j % 2, c, :], lambda c: fu_lo[:, j % 2, c, :]).then_inc(y_ready, 1)

                pe.wait_ge(consts_in, 16 * 5)
                group_mean(0)
                group_var(0)
                pe.wait_ge(band_step, 3)
                eca(0)
                pe.wait_ge(w_lo_done, 2)
                taps(0, 0, 0)
                taps(0, 0, 1)

                def batch(b, s, first, last):
                    for j in range(CHUNKS):
                        end = last and j == CHUNKS - 1
                        for t in range(CT):
                            if not end:
                                taps(b, j + 1, t)
                            project(b, j, t)
                            if t == 0 and not last and j == 4:
                                group_mean(b + 1)
                            if t == 0 and not last and j == 5:
                                group_var(b + 1)
                            if t == 0 and not last and j == 6:
                                eca(b + 1)

                batches(pe, batch)


def layer1_features(nc, a, y_dram, x1_dram, r_dram, w2_dram, ystats, ab):
    PIECES = 4
    PN = PX // PIECES
    x_v = a["x"].rearrange("b (t p) h w -> b p t (h w)", p=P)
    y_v = y_dram.rearrange("b (t p) n -> b p t n", p=P)
    x1_v = x1_dram.rearrange("b (t p) n -> b p t n", p=P)
    with ExitStack() as ctx:
        def sb(name, shape, dt=F32):
            return ctx.enter_context(nc.sbuf_tensor(name, shape, dt))

        def sem(name):
            return ctx.enter_context(nc.semaphore(name))

        xs = sb("xs", [P, 2, CT, PX])
        ys = sb("ys", [P, 2, CT, PN])
        rb = sb("rb", [P, 2, POS, NBR, NBC])
        w1t = sb("w1t", [P, CT, RED])
        w1s = sb("w1s", [P, 2, CT, RED])
        cols = sb("cols", [P, 9])
        gavg1 = sb("gavg1", [P, P])
        sel = sb("sel", [P, QUARTERS, P])
        w2_raw = sb("w2_raw", [P, GROUPS * W2_LEN])
        w2_hi = sb("w2_hi", [P, GROUPS * W2_LEN], F32R)
        w2_lo = sb("w2_lo", [P, GROUPS * W2_LEN], F32R)
        ymv = sb("ymv", [P, CT, 2])
        bvar = sb("bvar", [P, 3])
        brs = sb("brs", [P, 3])
        bnt = sb("bnt", [P, 3])
        bsc = sb("bsc", [P, 3])
        ysh = sb("ysh", [P, CT])
        rsh = sb("rsh", [P, 1])
        rbias = sb("rbias", [P, 2])
        st = sb("st", [P, CT, CHUNKS, 6])
        mv1 = sb("mv1", [P, CT, 2])
        gm1 = sb("gm1", [P, CT])
        dm1 = sb("dm1", [P, CT])
        ev1 = sb("ev1", [P, CT])
        gv1 = sb("gv1", [P, CT])
        rt1 = sb("rt1", [P, CT])
        nt1 = sb("nt1", [P, CT])
        nrm = sb("nrm", [P, CT, 2])

        rps = ctx.enter_context(nc.psum_tensor("rps", [P, 4, N], F32))
        cps1 = ctx.enter_context(nc.psum_tensor("cps1", [P, N], F32))

        vec_in, w2_in = sem("vec_in"), sem("w2_in")
        xy_in = [sem(f"xy_in{n}") for n in range(2)]
        w2_hi_done, w2_lo_done, w2_out = sem("w2_hi_done"), sem("w2_lo_done"), sem("w2_out")
        r_zeroed = sem("r_zeroed")
        bn_chain, bn_var, bn_root, bn_ready = sem("bn_chain"), sem("bn_var"), sem("bn_root"), sem("bn_ready")
        y_scaled, x1_done, x1_out = sem("y_scaled"), sem("x1_done"), [sem(f"x1_out{n}") for n in range(2)]
        x1_stats, mean1, chain1, scratch = sem("x1_stats"), sem("mean1"), sem("chain1"), sem("scratch")
        gmean1, dev1, gvar1, gvar1_in, root1 = sem("gmean1"), sem("dev1"), sem("gvar1"), sem("gvar1_in"), sem("root1")
        norm1, w1_scaled, small_ps, small_done = sem("norm1"), sem("w1_scaled"), sem("small_ps"), sem("small_done")
        r_ready, r_copied, r_out = sem("r_ready"), sem("r_copied"), [sem(f"r_out{n}") for n in range(2)]

        CHAIN = 11

        def batches(engine, body):
            body(0, 0)
            body(1, 1)
            with engine.Fori(1, B // 2) as two:
                body(2 * two, 0)
                body(2 * two + 1, 1)
            body(B, 0)

        def exists(b):
            return not isinstance(b, int) or 0 <= b < B

        with nc.Block() as block:

            @block.sync
            def _(sp):
                sp.dma_start(cols[:, :], a["columns"]).then_inc(vec_in, 16)
                sp.dma_start(gavg1[:, :], a["group_average"]).then_inc(vec_in, 16)
                sp.dma_start(sel[:, :, :], a["select"]).then_inc(vec_in, 16)
                sp.dma_start(w1t[:, :, :], a["w1_t"]).then_inc(vec_in, 16)
                def store(n):
                    b, q = n // PIECES, n % PIECES
                    sp.dma_start(x1_v[b, :, :, PN * q:PN * q + PN],
                                 xs[:, b % 2, :, PN * q:PN * q + PN]).then_inc(x1_out[b % 2], 16)

                for n in range(B * PIECES):
                    b, q, s = n // PIECES, n % PIECES, n // PIECES % 2
                    if n >= 2:
                        sp.wait_ge(x1_done, n - 1)
                        store(n - 2)
                    if b >= 2 and q == 0:
                        sp.wait_ge(x1_out[s], 16 * PIECES * (b // 2))
                        sp.wait_ge(r_ready, (b - 1) * CHUNKS)
                    sp.dma_start(ys[:, n % 2, :, :], y_v[b, :, :, PN * q:PN * q + PN]).then_inc(xy_in[n % 2], 16)
                    sp.dma_start(xs[:, s, :, PN * q:PN * q + PN],
                                 x_v[b, :, :, PN * q:PN * q + PN]).then_inc(xy_in[n % 2], 16)
                    if n == PIECES:
                        sp.dma_start(w2_raw[:, :], a["w2_pad"]).then_inc(w2_in, 16)
                for n in (B * PIECES - 2, B * PIECES - 1):
                    sp.wait_ge(x1_done, n + 1)
                    store(n)
                for part, (w, done) in enumerate(((w2_hi, w2_hi_done), (w2_lo, w2_lo_done))):
                    sp.wait_ge(done, 1)
                    sp.dma_start(w2_dram[:, :, part, :].rearrange("g p n -> p g n"),
                                 w[:, :].bitcast(F32).rearrange("p (g n) -> p g n", g=PAIRS)).then_inc(w2_out, 16)
                sp.wait_ge(w2_out, 32)
                for s in range(2):
                    sp.wait_ge(x1_out[s], 16 * PIECES * B // 2)

            @block.gpsimd
            def _(pool):
                pool.memset(rb[:, :, :, :, :], 0.0).then_inc(r_zeroed, 1)

                for b in range(B):
                    pool.wait_ge(r_copied, (b + 1) * 4 * CHUNKS)
                    pool.dma_start(r_dram[b], rb[:, b % 2, :, :, :].rearrange("p k r c -> p (k r c)"))\
                        .then_inc(r_out[b % 2], 16)
                for s in range(2):
                    pool.wait_ge(r_out[s], 16 * B // 2)

            @block.scalar
            def _(act):
                act.wait_ge(bn_var, 1)
                act.activation(brs[:, :], bvar[:, :], ACT.Sqrt).then_inc(bn_root, 1)
                act.wait_ge(bn_ready, 1)

                def scale_y(b, q):
                    act.wait_ge(xy_in[q % 2], b * (16 * PIECES) + 32 * (q // 2 + 1))
                    for t in range(CT):
                        act.activation(ys[:, q % 2, t, :], ys[:, q % 2, t, :], ACT.Identity, bias=ysh[:, t:t + 1],
                                       scale=bsc[:, t:t + 1]).then_inc(y_scaled, 1)

                def reduce(b, s, j):
                    act.wait_ge(r_ready, b * CHUNKS + (j + 1))
                    if j == 0:
                        act.wait_ge(small_done, b + 1)
                        positive(act, r_out[s], (b - s) * 8)
                    for h in range(2):
                        src = rps[:, j % 4, 256 * h:256 * h + 256].rearrange("p (i w) -> p i w", i=BR)
                        dst = rb[:, s, :, 2 * j + h, :].rearrange("p (i j) c -> p i j c", i=BR)
                        for c0, c1, w0, w1 in ((0, W // BC, 0, BC), (W // BC, NBC, 0, W - WHOLE)):
                            act.activation(dst[:, :, w0:w1, c0:c1],
                                           src[:, :, BC * c0:min(BC * c1, W)].rearrange(
                                               "p i (c j) -> p i j c", j=w1 - w0),
                                           ACT.Relu, bias=rbias[:, s:s + 1], scale=bsc[:, 2:3]).then_inc(r_copied, 1)

                def batch(b, s):
                    for q in range(PIECES):
                        if exists(b):
                            scale_y(b, q)
                        if exists(b - 1):
                            if q == 0:
                                act.wait_ge(gvar1_in, b)
                                act.activation(rt1[:, :], gv1[:, :], ACT.Sqrt).then_inc(root1, 1)
                            else:
                                for j in range(3 * q - 3, min(3 * q, CHUNKS)):
                                    reduce(b - 1, 1 - s, j)
                        if isinstance(b, int) and (b, q) == (1, 0):
                            act.wait_ge(w2_in, 16)
                            act.activation(w2_hi[:, :], w2_raw[:, :], ACT.Identity).then_inc(w2_hi_done, 1)

                act.wait_ge(r_zeroed, 1)
                batches(act, batch)

            @block.vector
            def _(dve):
                gamma0, beta0 = cols[:, 0:2], cols[:, 2:4]
                b1, gamma1, beta1, rmean, rvar = (cols[:, n:n + 1] for n in range(4, 9))
                dve.wait_ge(vec_in, 64)
                for t in range(CT):
                    dve.bn_aggr(ymv[:, t, :], ystats[:, t, :, :].rearrange("p n s -> p (n s)")).then_inc(bn_chain, 1)
                dve.wait_ge(bn_chain, 2)
                dve.tensor_scalar(bvar[:, 0:2], ymv[:, :, 1], BN_EPS, None, ALU.add).then_inc(bn_chain, 1)
                dve.tensor_scalar(bvar[:, 2:3], rvar, BN_EPS, None, ALU.add).then_inc(bn_chain, 1)
                dve.wait_ge(bn_chain, 4)
                dve.tensor_copy(bnt[:, :], bvar[:, :]).then_inc(bn_var, 1)
                dve.wait_ge(bn_var, 1)
                dve.wait_ge(bn_root, 1)
                dve.reciprocal(brs[:, :], brs[:, :]).then_inc(bn_chain, 1)
                dve.wait_ge(bn_chain, 5)
                newton(dve, bn_chain, 5, brs[:, :], bvar[:, :], bnt[:, :])
                dve.tensor_tensor(bsc[:, 0:2], brs[:, 0:2], gamma0, ALU.mult).then_inc(bn_chain, 1)
                dve.tensor_tensor(bsc[:, 2:3], brs[:, 2:3], gamma1, ALU.mult).then_inc(bn_chain, 1)
                dve.wait_ge(bn_chain, 11)
                dve.tensor_tensor(ysh[:, :], ymv[:, :, 0], bsc[:, 0:2], ALU.mult).then_inc(bn_chain, 1)
                dve.tensor_tensor(rsh[:, :], b1, rmean, ALU.subtract).then_inc(bn_chain, 1)
                dve.wait_ge(bn_chain, 13)
                dve.tensor_tensor(ysh[:, :], beta0, ysh[:, :], ALU.subtract).then_inc(bn_ready, 1)
                dve.tensor_tensor(rsh[:, :], rsh[:, :], bsc[:, 2:3], ALU.mult).then_inc(bn_chain, 1)
                dve.wait_ge(bn_chain, 14)
                dve.tensor_tensor(rsh[:, :], rsh[:, :], beta1, ALU.add).then_inc(bn_chain, 1)
                dve.wait_ge(bn_chain, 15)

                def add(b, s, q):
                    dve.wait_ge(y_scaled, b * (PIECES * CT) + CT * (q + 1))
                    piece = xs[:, s, :, PN * q:PN * q + PN]
                    dve.tensor_tensor(piece, piece, ys[:, q % 2, :, :], ALU.add).then_inc(x1_done, 1)
                    dve.wait_ge(x1_done, b * PIECES + (q + 1))
                    for t in range(CT):
                        for j in (2 * q, 2 * q + 1):
                            dve.bn_stats(st[:, t, j, :], xs[:, s, t, N * j:N * j + N]).then_inc(x1_stats, 1)
                    if q == PIECES - 1:
                        dve.wait_ge(x1_stats, b * (CHUNKS * CT) + CHUNKS * CT)
                        dve.memset(nt1[:, :], 0.0).then_inc(scratch, 1)
                        for t in range(CT):
                            dve.bn_aggr(mv1[:, t, :], st[:, t, :, :].rearrange("p j s -> p (j s)")).then_inc(mean1, 1)

                def norm(b, s):
                    def step(ins, n):
                        ins.then_inc(chain1, 1)
                        dve.wait_ge(chain1, b * CHAIN + n)

                    dve.wait_ge(gmean1, b + 1)
                    step(dve.tensor_copy(gm1[:, :], cps1[:, 0:CT]), 1)
                    dve.wait_ge(mean1, b * CT + CT)
                    step(dve.tensor_tensor(dm1[:, :], mv1[:, :, 0], gm1[:, :], ALU.subtract), 2)
                    step(dve.tensor_tensor(ev1[:, :], dm1[:, :], dm1[:, :], ALU.mult), 3)
                    dve.tensor_tensor(ev1[:, :], ev1[:, :], mv1[:, :, 1], ALU.add).then_inc(dev1, 1)
                    dve.wait_ge(gvar1, b + 1)
                    dve.tensor_scalar(gv1[:, :], cps1[:, 0:CT], GN_EPS, None, ALU.add).then_inc(gvar1_in, 1)
                    dve.wait_ge(gvar1_in, b + 1)
                    dve.wait_ge(root1, b + 1)
                    step(dve.reciprocal(rt1[:, :], rt1[:, :]), 4)
                    dve.wait_ge(scratch, b + 1)
                    newton(dve, chain1, b * CHAIN + 4, rt1[:, :], gv1[:, :], nt1[:, :])
                    step(dve.tensor_tensor(gm1[:, :], gm1[:, :], rt1[:, :], ALU.mult), 9)
                    step(dve.tensor_copy(nrm[:, :, 0], rt1[:, :]), 10)
                    dve.tensor_scalar(nrm[:, :, 1], gm1[:, :], -1.0, None, ALU.mult).then_inc(norm1, 1)
                    for t in range(CT):
                        dve.tensor_scalar(w1s[:, s, t, :], w1t[:, t, :], rt1[:, t:t + 1], None,
                                          ALU.mult).then_inc(w1_scaled, 1)
                    dve.wait_ge(small_ps, b + 1)
                    dve.tensor_copy(ab[:, b, :, :], cps1[:, 16:16 + 2 * PAIRS].rearrange("p (a n) -> p a n", n=2))\
                        .then_inc(chain1, 1)
                    dve.tensor_scalar(rbias[:, s:s + 1], cps1[:, 64:65], bsc[:, 2:3], rsh[:, :], ALU.mult,
                                      ALU.add).then_inc(small_done, 1)
                    dve.wait_ge(chain1, b * CHAIN + 11)

                def batch(b, s):
                    for q in range(PIECES):
                        if exists(b):
                            add(b, s, q)
                        if exists(b - 1) and q == 0:
                            norm(b - 1, 1 - s)
                        if isinstance(b, int) and (b, q) == (1, 0):
                            dve.wait_ge(w2_hi_done, 1)
                            dve.tensor_tensor(w2_lo[:, :], w2_raw[:, :], w2_hi[:, :].bitcast(F32),
                                              ALU.subtract).then_inc(w2_lo_done, 1)

                dve.wait_ge(bn_ready, 1)
                batches(dve, batch)

            @block.tensor
            def _(pe):
                pe.wait_ge(vec_in, 64)

                def batch(b1, s1):
                    if not exists(b1 - 1):
                        return
                    b, s = b1 - 1, 1 - s1
                    pe.wait_ge(mean1, b * CT + CT)
                    positive(pe, small_done, b)
                    pe.matmul(cps1[:, 0:CT], gavg1[:, :], mv1[:, :, 0], start=True, stop=True).then_inc(gmean1, 1)
                    pe.wait_ge(dev1, b + 1)
                    pe.matmul(cps1[:, 0:CT], gavg1[:, :], ev1[:, :], start=True, stop=True).then_inc(gvar1, 1)
                    pe.wait_ge(norm1, b + 1)
                    for p in range(PAIRS):
                        pe.matmul(cps1[:, 16 + 2 * p:18 + 2 * p], sel[:, p % 4, :], nrm[:, p // 4, :],
                                  start=True, stop=True)
                    for t in range(CT):
                        last = pe.matmul(cps1[:, 64:65], w1t[:, t, :], nrm[:, t, 1:2], start=(t == 0), stop=(t == CT - 1))
                    last.then_inc(small_ps, 1)
                    pe.wait_ge(w1_scaled, b * CT + CT)
                    for j in range(CHUNKS):
                        positive(pe, r_copied, b * (4 * CHUNKS) + 4 * (j - 3))
                        for t in range(CT):
                            last = pe.matmul(rps[:, j % 4, :], w1s[:, s, t, :], xs[:, s, t, N * j:N * j + N],
                                             start=(t == 0), stop=(t == CT - 1))
                        last.then_inc(r_ready, 1)

                batches(pe, batch)


def layer1_involution(nc, a, x1_dram, r_dram, w2_dram, out, ab):
    x1_v = x1_dram.rearrange("b (a c) (h w) -> b a c h w", c=PCH, w=W)
    out_v = out.rearrange("b (a c) (q r) w -> b a q c (r w)", c=PCH, q=QUARTERS)
    r_v = r_dram.rearrange("(t s) p (k n) -> t p k s n", s=2, k=POS)
    with ExitStack() as ctx:
        def sb(name, shape, dt=F32):
            return ctx.enter_context(nc.sbuf_tensor(name, shape, dt))

        def sem(name):
            return ctx.enter_context(nc.semaphore(name))

        cols2 = sb("cols2", [PATCH, 2 * BLK, 2, BR, BC])
        r_hi = sb("r_hi", [P, POS, 2, BLK], F32R)
        r_lo = sb("r_lo", [P, POS, 2, BLK], F32R)
        xt = sb("xt", [PATCH, 2, QBLK, P])
        xq = sb("xq", [P, HROWS, W])
        res = sb("res", [P, 2, QROWS, W])
        xnq = sb("xnq", [P, NBC, HROWS, PC])
        w2u = sb("w2u", [P, 2, 2, W2_LEN], F32R)
        b2u = sb("b2u", [PATCH, 2, POS])
        abu = sb("abu", [P, 2, 3, 2])
        msk = sb("msk", [P, 3, 2])
        gsel = sb("gsel", [P, 2])
        eps = sb("eps", [P, 1, 1])
        ident = sb("ident", [P, P])
        r_raw = r_lo[:, :, :, :].bitcast(F32)

        aps = ctx.enter_context(nc.psum_tensor("aps", [P, 2, 2, N], F32))
        tps = ctx.enter_context(nc.psum_tensor("tps", [P, 2, N], F32))
        cps = ctx.enter_context(nc.psum_tensor("cps", [P, 2, N], F32))

        PARTS = 8
        PP = POS // PARTS
        TG = QBLK // 4
        CG = QBR
        UNITS = PAIRS * B // 2

        const_in, w2_in, xq_in = sem("const_in"), sem("w2u_in"), sem("xq_in")
        r_in = [sem(f"r_in{part}") for part in range(PARTS)]
        pads, eps_set = sem("pads"), sem("eps_set")
        r_hi_done, r_lo_done = sem("r_hi_done"), sem("r_lo_done")
        a_ready, a_dve, a_act = sem("a_ready"), sem("a_dve"), sem("a_act")
        norm_here, xn_inner, xn_edges, res_begun = sem("norm_here"), sem("xn_inner"), sem("xn_edges"), sem("res_begun")
        t_ready, t_copied = sem("t_ready"), sem("t_copied")
        c_ready, c_first, c_done = sem("c_ready"), sem("c_first"), sem("c_done")
        stored = [sem(f"stored{s}") for s in range(2)]

        SECOND_NORM = 5
        SECOND_EDGES = (6, 7, 8)
        SECOND_AT = (9, 10, 11, 12, 13, 14, 16, 18, 20, 23, 23)
        NEXT_XQ = 9
        NEXT_NORM = 20
        R_SPLIT = (15, 17, 19, 21, 22)

        def windows(r0, r1):
            at = xq[:, r0:r1, BC - HALO:BC - HALO + PC]
            dims = [list(d) for d in at.ap]
            return bass.AP(at.tensor, at.offset, [dims[0], [BC, NBC - 2], *dims[1:]])

        def patch_columns(r0, r1):
            over = BC * (NBC - 1) - HALO
            return ((xnq[:, 0, r0:r1, HALO:PC], xq[:, r0:r1, 0:PC - HALO]),
                    (xnq[:, NBC - 1, r0:r1, 0:W - over], xq[:, r0:r1, over:W]),
                    (xnq[:, 1:NBC - 1, r0:r1, :], windows(r0, r1)))

        def rows_of(bank):
            return cps[:, bank, :].rearrange("p (g i w) -> p g i w", g=2, i=BR)

        def units(engine, unit):
            unit(0, 0, (0, 1))
            with engine.Fori(1, PAIRS - 1) as p:
                unit(0, p, (0, p + 1))
            with engine.Fori(1, B // 2) as t:
                unit(t - 1, PAIRS - 1, (t, 0))
                with engine.Fori(0, PAIRS - 1) as p:
                    unit(t, p, (t, p + 1))
            unit(B // 2 - 1, PAIRS - 1, None)

        def new_images(after):
            return after is not None and isinstance(after[1], int) and after[1] == 0

        def transposes_after(k):
            if k <= SECOND_NORM:
                return [(0, g) for g in range(2 * k, min(2 * k + 2, TG))]
            return [(1, g) for g in range(TG) if SECOND_AT[g] == k]

        with nc.Block() as block:

            @block.sync
            def _(sp):
                def load_image(t, p, s):
                    u = t * PAIRS + p
                    positive(sp, xn_inner, u * 2 + s)
                    positive(sp, xn_edges, u * 2 + s)
                    positive(sp, res_begun, u * 2 + s)
                    for q in range(QUARTERS):
                        r0, r1 = max(QROWS * q - HALO, 0), min(QROWS * q + QROWS + HALO, H)
                        d = r0 - (QROWS * q - HALO)
                        sp.dma_start(xq[PCH * q:PCH * q + PCH, d:d + r1 - r0, :],
                                     x1_v[2 * t + s, p, :, r0:r1, :]).then_inc(xq_in, 16)

                def load_w2(p):
                    sp.dma_start(w2u[:, :, :, :].bitcast(F32).rearrange("p a g n -> p (a g n)"),
                                 w2_dram[p].rearrange("p a n -> p (a n)")).then_inc(w2_in, 16)
                    sp.dma_start(b2u[:, :, :].rearrange("p g k -> p (g k)"), a["b2_band"][p]).then_inc(w2_in, 16)

                def load_r(t, part):
                    for n in range(2):
                        sp.dma_start(r_raw[:, PP * part:PP * part + PP, n, :],
                                     r_v[t, :, PP * part:PP * part + PP, n, :]).then_inc(r_in[part], 16)

                def store(u, t, p, s):
                    sp.wait_ge(c_done, u * (2 * CG) + CG * (s + 1))
                    for q in range(QUARTERS):
                        sp.dma_start(out_v[2 * t + s, p, q], res[PCH * q:PCH * q + PCH, s, :, :].rearrange("p r w -> p (r w)"))\
                            .then_inc(stored[s], 16)

                def unit(t, p, after):
                    u = t * PAIRS + p
                    for k in range(POS):
                        if new_images(after) and k % PP == PP - 1:
                            sp.wait_ge(a_ready, u * (2 * POS) + (2 * k + 2))
                            load_r(after[0], k // PP)
                        if k == NEXT_XQ and after:
                            load_image(*after, 0)
                    if after:
                        sp.wait_ge(c_ready, u * (2 * CG) + 1)
                        load_w2(after[1])
                    store(u, t, p, 0)
                    if after:
                        load_image(*after, 1)
                    store(u, t, p, 1)

                sp.dma_start(ident[:, :], a["identity"]).then_inc(const_in, 16)
                sp.dma_start(msk[:, :, :], a["row_masks"]).then_inc(const_in, 16)
                sp.dma_start(gsel[:, :], a["group_masks"]).then_inc(const_in, 16)
                load_w2(0)
                load_r(0, 0)
                sp.wait_ge(pads, 1)
                load_image(0, 0, 0)
                for part in range(1, PARTS):
                    load_r(0, part)
                load_image(0, 0, 1)
                units(sp, unit)
                for s in range(2):
                    sp.wait_ge(stored[s], 16 * QUARTERS * UNITS)

            @block.gpsimd
            def _(pool):
                def begin(t, p):
                    u = t * PAIRS + p
                    for s in range(2):
                        pool.wait_ge(xq_in, u * (2 * 16 * QUARTERS) + 16 * QUARTERS * (s + 1))
                        positive(pool, stored[s], u * (16 * QUARTERS))
                        pool.tensor_tensor(res[:, s, :, :], xq[:, HALO:HALO + QROWS, :], eps[:, :, :].to_broadcast([P, QROWS, W]),
                                           ALU.add).then_inc(res_begun, 1)

                pool.memset(eps[:, :, :], K1 * K1 * FINFO_EPS).then_inc(eps_set, 1)
                pool.wait_ge(eps_set, 1)
                pool.memset(xq[:, :, :], 0.0).then_inc(pads, 1)
                pool.memset(xnq[:, :, :, :], 0.0).then_inc(pads, 1)
                begin(0, 0)
                with pool.Fori(1, UNITS) as u:
                    begin(0, u)

            @block.scalar
            def _(act):
                def normalise(u, s):
                    act.wait_ge(xq_in, u * (2 * 16 * QUARTERS) + 16 * QUARTERS * (s + 1))
                    act.wait_ge(norm_here, u + 1)
                    positive(act, t_ready, u * (2 * TG) + TG * s)
                    dst, src = patch_columns(HALO, HALO + QROWS)[2]
                    act.activation(dst, src, ACT.Identity, bias=abu[:, s, 0, 1:2], scale=abu[:, s, 0, 0:1])                        .then_inc(xn_inner, 1)

                def split(t, k):
                    act.wait_ge(r_in[k // PP], t * 32 + 32)
                    act.activation(r_hi[:, k, :, :], r_raw[:, k, :, :], ACT.Identity).then_inc(r_hi_done, 1)

                def unit(t, p, after):
                    u = t * PAIRS + p
                    for k in range(POS):
                        act.wait_ge(a_ready, u * (2 * POS) + (2 * k + 2))
                        positive(act, c_ready, u * (2 * CG))
                        act.activation(cols2[:, :, 1, k // BC, k % BC], aps[0:PATCH, k % 2, 1, 0:2 * BLK],
                                       ACT.Identity, bias=b2u[:, 1, k:k + 1]).then_inc(a_act, 1)
                        for s, g in transposes_after(k):
                            n = s * TG + g
                            act.wait_ge(t_ready, u * (2 * TG) + (n + 1))
                            positive(act, c_ready, u * (2 * CG) - CG * (1 - s))
                            act.activation(xt[:, s, 4 * g:4 * g + 4, :].rearrange("p n c -> p (n c)"),
                                           tps[0:PATCH, n % 2, :], ACT.Identity).then_inc(t_copied, 1)
                        if k == SECOND_NORM:
                            normalise(u, 1)
                        if new_images(after) and k in R_SPLIT:
                            split(after[0], R_SPLIT.index(k))
                    if after:
                        normalise(u + 1, 0)
                    if new_images(after):
                        for k in range(len(R_SPLIT), POS):
                            split(after[0], k)

                act.wait_ge(pads, 2)
                normalise(0, 0)
                for k in range(POS):
                    split(0, k)
                units(act, unit)

            @block.vector
            def _(dve):
                def norm(t, p):
                    u = t * PAIRS + p
                    positive(dve, xn_inner, 2 * u)
                    positive(dve, xn_edges, 2 * u)
                    for s in range(2):
                        last = dve.tensor_tensor(abu[:, s, :, :],
                                                 ab[:, 2 * t + s, p, :].rearrange("p (o n) -> p o n", o=1).to_broadcast([P, 3, 2]),
                                                 msk[:, :, :], ALU.mult)
                    last.then_inc(norm_here, 1)

                def normalise_edges(u, s, edges):
                    dve.wait_ge(xq_in, u * (2 * 16 * QUARTERS) + 16 * QUARTERS * (s + 1))
                    dve.wait_ge(norm_here, u + 1)
                    positive(dve, t_ready, u * (2 * TG) + TG * s)
                    for edge in edges:
                        n, columns = ((1, patch_columns(0, HALO)), (2, patch_columns(HALO + QROWS, HROWS)),
                                      (0, patch_columns(HALO, HALO + QROWS)[0:2]))[edge]
                        for dst, src in columns:
                            last = dve.tensor_scalar(dst, src, abu[:, s, n, 0:1], abu[:, s, n, 1:2], ALU.mult, ALU.add)
                    if 2 in edges:
                        last.then_inc(xn_edges, 1)

                def split(t, k):
                    dve.wait_ge(r_hi_done, t * POS + (k + 1))
                    dve.tensor_tensor(r_lo[:, k, :, :], r_raw[:, k, :, :], r_hi[:, k, :, :].bitcast(F32),
                                      ALU.subtract).then_inc(r_lo_done, 1)

                def add_products(u, s, c):
                    if c == 0:
                        dve.wait_ge(res_begun, u * 2 + (s + 1))
                    n = s * CG + c
                    dve.wait_ge(c_ready, u * (2 * CG) + (n + 1))
                    src = rows_of(n % 2)
                    dst = res[:, s, BR * c:BR * c + BR, :]
                    dve.scalar_tensor_tensor(dst, src[:, 1], gsel[:, 1:2], dst, op0=ALU.mult,
                                             op1=ALU.add).then_inc(c_first, 1)
                    dve.wait_ge(c_first, u * (2 * CG) + (n + 1))
                    dve.scalar_tensor_tensor(dst, src[:, 0], gsel[:, 0:1], dst, op0=ALU.mult,
                                             op1=ALU.add).then_inc(c_done, 1)

                def unit(t, p, after):
                    u = t * PAIRS + p
                    for k in range(POS):
                        dve.wait_ge(a_ready, u * (2 * POS) + (2 * k + 1))
                        positive(dve, c_ready, u * (2 * CG))
                        dve.tensor_scalar(cols2[:, :, 0, k // BC, k % BC], aps[0:PATCH, k % 2, 0, 0:2 * BLK],
                                          b2u[:, 0, k:k + 1], None, ALU.add).then_inc(a_dve, 1)
                        if k in SECOND_EDGES:
                            normalise_edges(u, 1, (SECOND_EDGES.index(k),))
                        if k == NEXT_NORM and after:
                            norm(*after)
                        if new_images(after) and k in R_SPLIT:
                            split(after[0], R_SPLIT.index(k))
                    if after:
                        normalise_edges(u + 1, 0, (0, 1, 2))
                    k = len(R_SPLIT)
                    for n in range(2 * CG + 1):
                        if n > 0:
                            add_products(u, (n - 1) // CG, (n - 1) % CG)
                        if new_images(after):
                            upto = POS - 2 * (2 * CG - n)
                            for k in range(k, upto):
                                split(after[0], k)
                            k = upto

                dve.wait_ge(const_in, 48)
                dve.wait_ge(pads, 2)
                norm(0, 0)
                normalise_edges(0, 0, (0, 1, 2))
                for k in range(POS):
                    split(0, k)
                units(dve, unit)

            @block.tensor
            def _(pe):
                def transposes(u, s, g):
                    n = s * TG + g
                    if g == 0:
                        pe.wait_ge(xn_inner, u * 2 + (s + 1))
                        pe.wait_ge(xn_edges, u * 2 + (s + 1))
                    positive(pe, t_copied, u * (2 * TG) + (n - 1))
                    for m in range(4):
                        r, c = (4 * g + m) // NBC, (4 * g + m) % NBC
                        last = pe.transpose(tps[0:PATCH, n % 2, P * m:P * m + P],
                                            xnq[:, c, BR * r:BR * r + PR, :].rearrange("p r c -> p (r c)"), ident[:, :])
                    last.then_inc(t_ready, 1)

                def taps(u, k):
                    for g in range(2):
                        if k >= 2:
                            pe.wait_ge((a_dve, a_act)[g], u * POS + (k - 1))
                        terms = ((0, r_hi), (0, r_lo), (1, r_hi))
                        for n, (part, r) in enumerate(terms):
                            at = W2_AT - PC * (k // BC) - k % BC
                            last = pe.matmul(aps[0:PATCH, k % 2, g, 0:2 * BLK], w2u[:, part, g, at:at + PATCH],
                                             r[:, k, :, :].rearrange("p s n -> p (s n)"),
                                             start=(n == 0), stop=(n == 2))
                        last.then_inc(a_ready, 1)

                def products(u, s, c):
                    n = s * CG + c
                    if c == 0:
                        pe.wait_ge(t_copied, u * (2 * TG) + TG * (s + 1))
                    positive(pe, c_done, u * (2 * CG) + (n - 1))
                    for m in range(NBC):
                        width = min(BC, W - BC * m)
                        for q in range(QUARTERS):
                            at = s * BLK + (QBR * q + c) * NBC + m
                            last = pe.matmul(rows_of(n % 2)[PCH * q:PCH * q + PCH, :, :, BC * m:BC * m + width],
                                             xt[:, s, c * NBC + m, PCH * q:PCH * q + PCH],
                                             cols2[:, at, :, :, 0:width], start=True, stop=True)
                    last.then_inc(c_ready, 1)

                def unit(t, p, after):
                    u = t * PAIRS + p
                    pe.wait_ge(w2_in, u * 32 + 32)
                    for k in range(POS):
                        pe.wait_ge(r_lo_done, t * POS + (k + 1))
                        taps(u, k)
                        for s, g in transposes_after(k):
                            transposes(u, s, g)
                    pe.wait_ge(a_act, u * POS + POS)
                    pe.wait_ge(a_dve, u * POS + POS)
                    for s in range(2):
                        for c in range(CG):
                            products(u, s, c)

                pe.wait_ge(const_in, 48)
                units(pe, unit)


def kernel(**inputs):
    import numpy as np
    import concourse.bacc as bacc
    from concourse.bass_utils import run_bass_kernel_spmd

    nc = bacc.Bacc("TRN2", target_bir_lowering=False, num_devices=1)
    i = {n: np.ascontiguousarray(v) for n, v in inputs.items()}

    wf_t = i["L0_conv_W_filter"].reshape(CT, P, K0, CT, P).transpose(4, 3, 0, 2, 1)
    wp_t = i["L0_conv_W_proj"].reshape(C, CT, P).transpose(2, 1, 0)
    vectors = [i[n].reshape(-1, P).T for n in ("L0_conv_gamma", "L0_conv_beta", "L1_conv_b1", "L1_conv_gamma",
                                               "L1_conv_beta", "L1_conv_run_mean", "L1_conv_run_var")]
    taps = i["L1_conv_w2"].reshape(GROUPS, K1, K1, RED)
    w2_pad = np.zeros((RED, GROUPS, W2_LEN), np.float32)
    for r in range(K1):
        w2_pad[:, :, W2_AT + PC * r:W2_AT + PC * r + K1] = taps[:, r].transpose(2, 0, 1)
    b2_band = np.zeros((PAIRS, 2, BR, BC, PR, PC), np.float32)
    b2 = i["L1_conv_b2"].reshape(PAIRS, 2, K1, K1)
    for r in range(BR):
        for c in range(BC):
            b2_band[:, :, r, c, r:r + K1, c:c + K1] = b2
    c = np.arange(C)
    shifts = np.stack([(c[:, None] == c[None, :] + d) for d in (-1, 0, 1)]).astype(np.float32)
    p = np.arange(P)
    group_average = ((p[:, None] // GN_CH == p[None, :] // GN_CH) / GN_CH).astype(np.float32)
    select = np.stack([(p[:, None] == PCH * n + p[None, :] % PCH) for n in range(4)], 1).astype(np.float32)
    quarter = p // PCH
    row_masks = np.stack([quarter >= 0, quarter > 0, quarter < QUARTERS - 1], 1).astype(np.float32)
    group_masks = np.stack([p % PCH // GC == n for n in range(2)], 1).astype(np.float32)
    arrays = {
        "x": i["x"], "wf_t": wf_t.reshape(P, -1), "wp_t": wp_t.reshape(P, -1),
        "b_filter": i["L0_conv_b_filter"].reshape(CT, P, K0).transpose(1, 0, 2), "w_eca": i["L0_conv_w_eca"],
        "b_proj": i["L0_conv_b_proj"].reshape(CT, P).T,
        "columns": np.concatenate(vectors, 1), "w1_t": i["L1_conv_w1"].reshape(RED, CT, P).transpose(2, 1, 0),
        "w2_pad": w2_pad.reshape(RED, -1), "b2_band": b2_band.transpose(0, 4, 5, 1, 2, 3).reshape(PAIRS, PATCH, 2 * POS),
        "shifts": shifts, "group_average": group_average, "select": select,
        "row_masks": np.repeat(row_masks[:, :, None], 2, 2), "group_masks": group_masks,
        "identity": np.eye(P, dtype=np.float32),
    }
    arrays = {n: np.ascontiguousarray(v) for n, v in arrays.items()}
    a = {n: nc.dram_tensor(n, v.shape, F32, kind="ExternalInput").ap() for n, v in arrays.items()}
    y_dram = nc.dram_tensor("y", (B, C, PX), F32, kind="Internal").ap()
    x1_dram = nc.dram_tensor("x1", (B, C, PX), F32, kind="Internal").ap()
    r_dram = nc.dram_tensor("r", (B, P, POS * BLK), F32, kind="Internal").ap()
    w2_dram = nc.dram_tensor("w2_parts", (PAIRS, P, 2, 2 * W2_LEN), F32, kind="Internal").ap()
    out = nc.dram_tensor("out", (B, C, H, W), F32, kind="ExternalOutput").ap()
    build(nc, a, y_dram, x1_dram, r_dram, w2_dram, out)
    return run_bass_kernel_spmd(nc, [arrays], core_ids=[0]).results[0]["out"]
```

```python
import concourse.bass as bass
from concourse import mybir
from contextlib import ExitStack

F32 = mybir.dt.float32
F32R = mybir.dt.float32r
ALU = mybir.AluOpType
ACT = mybir.ActivationFunctionType

P = 128
B, C, H, W = 8, 256, 64, 64
CT = C // P
PX = H * W
GN_CH = C // 32
GN_EPS = 1e-5
BN_EPS = 1e-5
K0 = 9
ROWS = 8
N = ROWS * W
CHUNKS = H // ROWS
WP = W + 2
HP = H + 2
TAPS = CT * K0
RING = 6
K1 = 7
HALO = K1 // 2
GROUPS = 16
RED = C // 2
BR, BC = 4, 6
PR, PC = BR + K1 - 1, BC + K1 - 1
PATCH = PR * PC
POS = BR * BC
NBR = H // BR
NBC = -(-W // BC)
BLK = NBR * NBC
WHOLE = W // BC * BC
QUARTERS = 4
QROWS = H // QUARTERS
QBR = QROWS // BR
QBLK = QBR * NBC
HROWS = QROWS + 2 * HALO
PAIRS = 8
PCH = C // PAIRS
GC = C // GROUPS
W2_AT = PC * (BR - 1) + BC - 1
W2_LEN = W2_AT + PATCH + 1
FINFO_EPS = 2.0 ** -23


def positive(engine, semaphore, value):
    if not isinstance(value, int) or value > 0:
        engine.wait_ge(semaphore, value)


def build(nc, a, y_dram, r_dram, w2_dram, out):
    with ExitStack() as ctx:
        ab = ctx.enter_context(nc.sbuf_tensor("ab", [P, B, PAIRS, 2], F32))
        yn = ctx.enter_context(nc.sbuf_tensor("yn", [P, PAIRS, 2], F32))
        with nc.sbuf_tensor("ystats", [P, CT, B * CHUNKS, 6], F32) as ystats:
            layer0(nc, a, y_dram, ystats)
            layer1_features(nc, a, y_dram, r_dram, w2_dram, ystats, ab, yn)
        layer1_involution(nc, a, y_dram, r_dram, w2_dram, out, ab, yn)


def newton(dve, sem, count, rstd, var, tmp):
    steps = (
        lambda: dve.tensor_tensor(tmp, rstd, rstd, ALU.mult),
        lambda: dve.tensor_tensor(tmp, tmp, var, ALU.mult),
        lambda: dve.tensor_scalar(tmp, tmp, -0.5, 1.5, ALU.mult, ALU.add),
        lambda: dve.tensor_tensor(rstd, rstd, tmp, ALU.mult),
    )
    for n, step in enumerate(steps):
        step().then_inc(sem, 1)
        dve.wait_ge(sem, count + n + 1)


def layer0(nc, a, y_dram, ystats):
    x_v = a["x"].rearrange("b (t p) h w -> b p t h w", p=P)
    y_v = y_dram.rearrange("b (t p) n -> b t p n", p=P)

    with ExitStack() as ctx:
        def sb(name, shape, dt=F32):
            return ctx.enter_context(nc.sbuf_tensor(name, shape, dt))

        def sem(name):
            return ctx.enter_context(nc.semaphore(name))

        wf_hi = sb("wf_hi", [P, CT, CT, K0, P], F32R)
        wf_lo = sb("wf_lo", [P, CT, CT, K0, P], F32R)
        wp_hi = sb("wp_hi", [P, CT, C], F32R)
        wp_lo = sb("wp_lo", [P, CT, C], F32R)
        xn = sb("xn", [P, 2, CT, HP, WP])
        prod = sb("prod", [P, 2, K0, N])
        sums = sb("sums", [P, 2, 4, N])
        fused = sb("fused", [P, 2, N])
        fu_hi = sb("fu_hi", [P, 2, CT, N], F32R)
        fu_lo = sb("fu_lo", [P, 2, CT, N], F32R)
        x_hi = sb("x_hi", [P, 2, CT, N], F32R)
        x_lo = sb("x_lo", [P, 2, CT, N], F32R)
        ybuf = sb("ybuf", [P, 2, N])
        bf = sb("bf", [P, CT, K0])
        bfc = sb("bfc", [P, 2, CT])
        bp = sb("bp", [P, CT])
        weca = sb("weca", [P, 3])
        band = sb("band", [P, CT, C])
        gavg = sb("gavg", [P, P])
        xst = sb("xst", [P, CT, CHUNKS, 6])
        mv = sb("mv", [P, CT, 2])
        gm = sb("gm", [P, CT])
        dm = sb("dm", [P, CT])
        ev = sb("ev", [P, CT])
        gv = sb("gv", [P, CT])
        rstd = sb("rstd", [P, CT])
        nt = sb("nt", [P, CT])
        nb = sb("nb", [P, CT])
        pooled = sb("pooled", [P, CT])
        attn = sb("attn", [P, CT])
        raw = prod[:, :, :, :].rearrange("p s k n -> p (s k n)")
        NF = CT * CT * K0 * P
        NW = K0 * P
        w_parts = [(a["wf_t"][:, NW * n:NW * n + NW], raw[:, NW * n:NW * n + NW],
                    wf_hi[:, n // CT, n % CT, :, :].rearrange("p k n -> p (k n)"),
                    wf_lo[:, n // CT, n % CT, :, :].rearrange("p k n -> p (k n)"))
                   for n in (c * CT + t for t in range(CT) for c in range(CT))]
        wp_raw = raw[:, NF:NF + CT * C]
        w_parts.append((a["wp_t"], wp_raw, wp_hi[:, :, :].rearrange("p t n -> p (t n)"),
                        wp_lo[:, :, :].rearrange("p t n -> p (t n)")))
        sh_raw = raw[:, NF + CT * C:NF + CT * C + 3 * CT * C].rearrange("p (s t c) -> p s t c", s=3, t=CT)

        filt = ctx.enter_context(nc.psum_tensor("filt", [P, RING, N], F32))
        yps = ctx.enter_context(nc.psum_tensor("yps", [P, N], F32))
        sps = ctx.enter_context(nc.psum_tensor("sps", [P, N], F32))

        consts_in = sem("consts_in")
        filters_in = [sem(f"filters_in{n}") for n in range(CT * CT + 1)]
        x0_in = [sem(f"x0_in{n}") for n in range(2 * CT)]
        x_in = sem("x_in")
        zeroed = sem("zeroed")
        w_hi_done, w_lo_done = sem("w_hi_done"), sem("w_lo_done")
        xn_done = sem("xn_done")
        x_hi_done, x_lo_done = sem("x_hi_done"), sem("x_lo_done")
        tap_ready, tap_used = sem("tap_ready"), sem("tap_used")
        pair_sums = sem("pair_sums")
        pool_sums = sem("pool_sums")
        half_sum, fused_done = sem("half_sum"), sem("fused_done")
        fu_hi_done, fu_lo_done = sem("fu_hi_done"), sem("fu_lo_done")
        y_ready, y_copied, y_stats = sem("y_ready"), sem("y_copied"), sem("y_stats")
        y_out = [sem(f"y_out{m}") for m in range(CT)]
        x_stats, chain, band_step = sem("x_stats"), sem("chain"), sem("band_step")
        mean_in, gmean_ps, dev_in, gvar_ps = sem("mean_in"), sem("gmean_ps"), sem("dev_in"), sem("gvar_ps")
        gvar_in, root = sem("gvar_in"), sem("root")
        norm_ready, eca_ps, attn_done, centre_done = sem("norm_ready"), sem("eca_ps"), sem("attn_done"), sem("centre_done")

        CHAIN = 10
        LAST = B - 1
        NPARTS = 3 * CT

        def batches(engine, body):
            body(0, 0, True, False)
            with engine.Fori(0, (LAST - 1) // 2) as two:
                body(2 * two + 1, 1, False, False)
                body(2 * two + 2, 0, False, False)
            body(LAST, 1, False, True)

        with nc.Block() as block:

            @block.sync
            def _(sp):
                sp.dma_start(gavg[:, :], a["group_average"]).then_inc(consts_in, 16)
                sp.dma_start(sh_raw, a["shifts"].rearrange("s (t p) c -> p s t c", p=P)).then_inc(consts_in, 16)
                sp.dma_start(weca[:, :], a["w_eca"].rearrange("(o k) -> o k", o=1).to_broadcast([P, 3])).then_inc(consts_in, 16)
                sp.dma_start(bf[:, :, :], a["b_filter"]).then_inc(consts_in, 16)
                sp.dma_start(bp[:, :], a["b_proj"]).then_inc(consts_in, 16)
                for t in range(CT):
                    for h in range(2):
                        sp.dma_start(xn[:, 0, t, 1 + 32 * h:33 + 32 * h, 1:1 + W],
                                     x_v[0, :, t, 32 * h:32 * h + 32, :]).then_inc(x0_in[2 * t + h], 16)
                for n, (dram, w, _, _) in enumerate(w_parts):
                    sp.dma_start(w, dram).then_inc(filters_in[n], 16)

                for b in range(1, B):
                    if b > 1:
                        sp.wait_ge(x_in, ((b - 1) * 2 * CT) * 16)
                    else:
                        for n in range(2 * CT):
                            sp.wait_ge(x0_in[n], 16)
                    positive(sp, tap_used, (b - 1) * CHUNKS * TAPS)
                    for t in range(CT):
                        for h in range(2):
                            sp.dma_start(xn[:, b % 2, t, 1 + 32 * h:33 + 32 * h, 1:1 + W],
                                         x_v[b, :, t, 32 * h:32 * h + 32, :]).then_inc(x_in, 16)

            @block.gpsimd
            def _(pool):
                for edge in (xn[:, :, :, 0, :], xn[:, :, :, HP - 1, :], xn[:, :, :, 1:HP - 1, 0], xn[:, :, :, 1:HP - 1, WP - 1]):
                    pool.memset(edge, 0.0).then_inc(zeroed, 1)

                def split_x(b, j, s):
                    n1 = b * CHUNKS + (j + 1)
                    pool.wait_ge(x_hi_done, n1)
                    for t in range(CT):
                        src = xn[:, s, t, 1 + ROWS * j:1 + ROWS * j + ROWS, 1:1 + W]
                        last = pool.tensor_tensor(x_lo[:, j % 2, t, :].rearrange("p (h w) -> p h w", w=W), src,
                                                  x_hi[:, j % 2, t, :].bitcast(F32).rearrange("p (h w) -> p h w", w=W),
                                                  ALU.subtract)
                    last.then_inc(x_lo_done, 1)

                split_x(0, 0, 0)

                def batch(b, s, first, last):
                    for j in range(CHUNKS):
                        for t in range(CT):
                            i = b * (CHUNKS * CT) + (j * CT + t)
                            done = b * (CHUNKS * TAPS) + (j * TAPS + t * K0)
                            positive(pool, fused_done, i - 1)
                            pool.wait_ge(tap_used, done + 4)
                            pool.tensor_tensor(sums[:, t, 0:2, :], prod[:, t, 0:2, :], prod[:, t, 2:4, :],
                                               ALU.add).then_inc(pair_sums, 1)
                            pool.wait_ge(tap_used, done + 8)
                            pool.tensor_tensor(sums[:, t, 2:4, :], prod[:, t, 4:6, :], prod[:, t, 6:8, :],
                                               ALU.add).then_inc(pair_sums, 1)
                            pool.wait_ge(pair_sums, 2 * i + 2)
                            pool.tensor_tensor(sums[:, t, 0:2, :], sums[:, t, 0:2, :], sums[:, t, 2:4, :],
                                               ALU.add).then_inc(pool_sums, 1)
                            if t == 0 and not (last and j == CHUNKS - 1):
                                if j < CHUNKS - 1:
                                    split_x(b, j + 1, s)
                                else:
                                    split_x(b + 1, 0, 1 - s)

                batches(pool, batch)

            @block.scalar
            def _(act):
                PARTS = (0, 2, 5, CHUNKS)

                def normalise(b, s, parts):
                    act.wait_ge(norm_ready, b + 1)
                    for part in parts:
                        r0, r1 = PARTS[part] * ROWS, PARTS[part + 1] * ROWS
                        for t in range(CT):
                            v = xn[:, s, t, 1 + r0:1 + r1, 1:1 + W]
                            act.activation(v, v, ACT.Identity, bias=nb[:, t:t + 1],
                                           scale=rstd[:, t:t + 1]).then_inc(xn_done, 1)

                def split_x(b, j, s):
                    n = b * CHUNKS + j
                    part = 1 if j < 2 else 2 if j < 5 else 3
                    act.wait_ge(xn_done, b * NPARTS + CT * part)
                    positive(act, tap_ready, (n - 1) * TAPS)
                    positive(act, x_lo_done, n - 1)
                    for t in range(CT):
                        src = xn[:, s, t, 1 + ROWS * j:1 + ROWS * j + ROWS, 1:1 + W]
                        last = act.activation(x_hi[:, j % 2, t, :].rearrange("p (h w) -> p h w", w=W), src, ACT.Identity)
                    last.then_inc(x_hi_done, 1)

                def split_fused(b, j, t):
                    i = b * (CHUNKS * CT) + (j * CT + t)
                    act.wait_ge(fused_done, i + 1)
                    positive(act, y_ready, b * (CHUNKS * CT) + (j * CT - CT))
                    positive(act, fu_lo_done, i - 3)
                    act.activation(fu_hi[:, j % 2, t, :], fused[:, t, :], ACT.Identity).then_inc(fu_hi_done, 1)

                def copy_y(b, j, m):
                    yi = b * (CHUNKS * CT) + (j * CT + m)
                    act.wait_ge(y_ready, yi + 1)
                    positive(act, y_out[m], b * (16 * CHUNKS) + 16 * j)
                    positive(act, y_stats, yi - 1)
                    act.activation(ybuf[:, m, :], yps[:, :], ACT.Identity, bias=bp[:, m:m + 1],
                                   scale=0.5).then_inc(y_copied, 1)
                    act.wait_ge(y_copied, yi + 1)
                    at = N * (j % CHUNKS)
                    act.dma_start(y_v[b if j >= 0 else b - 1, m, :, at:at + N], ybuf[:, m, :]).then_inc(y_out[m], 16)

                def sqrt(b1):
                    act.wait_ge(gvar_in, b1 + 1)
                    act.activation(rstd[:, :], gv[:, :], ACT.Sqrt).then_inc(root, 1)

                def attention(b1):
                    act.wait_ge(eca_ps, b1 + 1)
                    positive(act, centre_done, b1)
                    act.activation(attn[:, :], sps[:, 0:CT], ACT.Sigmoid).then_inc(attn_done, 1)

                for n, (_, w, w_hi, _) in enumerate(w_parts):
                    act.wait_ge(filters_in[n], 16)
                    act.activation(w_hi, w, ACT.Identity).then_inc(w_hi_done, 1)
                    if n == CT - 1:
                        sqrt(0)
                normalise(0, 0, (0,))
                split_x(0, 0, 0)
                normalise(0, 0, (1, 2))
                attention(0)

                def batch(b, s, first, last):
                    for j in range(CHUNKS):
                        i = b * (CHUNKS * CT) + j * CT
                        if j < CHUNKS - 1:
                            split_x(b, j + 1, s)
                        elif not last:
                            normalise(b + 1, 1 - s, (0,))
                            split_x(b + 1, 0, 1 - s)
                            attention(b + 1)
                        if not (first and j == 0):
                            copy_y(b, j - 1, 0)
                        split_fused(b, j, 0)
                        if not last and j == CHUNKS - 2:
                            sqrt(b + 1)
                        if not last and j == CHUNKS - 1:
                            normalise(b + 1, 1 - s, (1, 2))
                        if not (first and j == 0):
                            copy_y(b, j - 1, 1)
                        split_fused(b, j, 1)

                batches(act, batch)
                copy_y(LAST, CHUNKS - 1, 0)
                copy_y(LAST, CHUNKS - 1, 1)
                for m in range(CT):
                    act.wait_ge(y_out[m], 16 * B * CHUNKS)

            @block.vector
            def _(dve):
                def stats(b1, s, j, tiles=range(CT)):
                    for t in tiles:
                        src = xn[:, s, t, 1 + ROWS * j:1 + ROWS * j + ROWS, 1:1 + W]
                        if isinstance(b1, int) and b1 == 0:
                            dve.wait_ge(x0_in[2 * t + j // (CHUNKS // 2)], 16)
                        else:
                            dve.wait_ge(x_in, (b1 - 1) * (16 * 2 * CT) + 16 * 2 * CT)
                        dve.bn_stats(xst[:, t, j, :], src).then_inc(x_stats, 1)

                def step(ins, b1, n):
                    ins.then_inc(chain, 1)
                    dve.wait_ge(chain, b1 * CHAIN + n)

                def mean(b1):
                    for t in range(CT):
                        dve.bn_aggr(mv[:, t, :], xst[:, t, :, :].rearrange("p j s -> p (j s)")).then_inc(mean_in, 1)

                def deviation(b1):
                    dve.wait_ge(gmean_ps, b1 + 1)
                    step(dve.tensor_copy(gm[:, :], sps[:, 0:CT]), b1, 1)
                    dve.wait_ge(mean_in, b1 * CT + CT)
                    step(dve.tensor_tensor(dm[:, :], mv[:, :, 0], gm[:, :], ALU.subtract), b1, 2)
                    step(dve.tensor_tensor(ev[:, :], dm[:, :], dm[:, :], ALU.mult), b1, 3)
                    dve.tensor_tensor(ev[:, :], ev[:, :], mv[:, :, 1], ALU.add).then_inc(dev_in, 1)

                def variance(b1):
                    dve.wait_ge(gvar_ps, b1 + 1)
                    dve.tensor_scalar(gv[:, :], sps[:, 0:CT], GN_EPS, None, ALU.add).then_inc(gvar_in, 1)

                def norm(b1):
                    dve.wait_ge(gvar_in, b1 + 1)
                    dve.wait_ge(root, b1 + 1)
                    step(dve.reciprocal(rstd[:, :], rstd[:, :]), b1, 4)
                    newton(dve, chain, b1 * CHAIN + 4, rstd[:, :], gv[:, :], nt[:, :])
                    step(dve.tensor_tensor(pooled[:, :], dm[:, :], rstd[:, :], ALU.mult), b1, 9)
                    step(dve.tensor_tensor(nb[:, :], gm[:, :], rstd[:, :], ALU.mult), b1, 10)
                    dve.tensor_scalar(nb[:, :], nb[:, :], -1.0, None, ALU.mult).then_inc(norm_ready, 1)

                def centre(b1, s):
                    dve.wait_ge(attn_done, b1 + 1)
                    dve.tensor_tensor(bfc[:, s, :], bf[:, :, K0 // 2], attn[:, :], ALU.add).then_inc(centre_done, 1)

                def fuse(i, t):
                    dve.wait_ge(pool_sums, i + 1)
                    positive(dve, fu_hi_done, i - 1)
                    positive(dve, fu_lo_done, i - 1)
                    dve.tensor_tensor(fused[:, t, :], sums[:, t, 0, :], sums[:, t, 1, :], ALU.add).then_inc(half_sum, 1)
                    dve.wait_ge(half_sum, i + 1)
                    dve.tensor_tensor(fused[:, t, :], fused[:, t, :], prod[:, t, K0 - 1, :], ALU.add).then_inc(fused_done, 1)

                def split_fused(i, j, t):
                    dve.wait_ge(fu_hi_done, i + 1)
                    dve.wait_ge(fused_done, i + 1)
                    positive(dve, y_ready, i - t - CT)
                    dve.tensor_tensor(fu_lo[:, j % 2, t, :], fused[:, t, :], fu_hi[:, j % 2, t, :].bitcast(F32),
                                      ALU.subtract).then_inc(fu_lo_done, 1)

                def take_y_stats(yi, m, col):
                    dve.wait_ge(y_copied, yi + 1)
                    dst = ystats[:, m, col, :]
                    dve.bn_stats(dst, ybuf[:, m, :]).then_inc(y_stats, 1)

                def w_low(n):
                    _, w, w_hi, w_lo = w_parts[n]
                    dve.wait_ge(w_hi_done, n + 1)
                    dve.tensor_tensor(w_lo, w, w_hi.bitcast(F32), ALU.subtract).then_inc(w_lo_done, 1)

                dve.wait_ge(consts_in, 16 * 5)
                dve.tensor_scalar(band[:, :, :], sh_raw[:, 0, :, :], weca[:, 0:1], None, ALU.mult).then_inc(band_step, 1)
                for n in (1, 2):
                    dve.wait_ge(band_step, n)
                    dve.scalar_tensor_tensor(band[:, :, :], sh_raw[:, n, :, :], weca[:, n:n + 1], band[:, :, :],
                                             op0=ALU.mult, op1=ALU.add).then_inc(band_step, 1)
                for t in range(CT):
                    for j in range(CHUNKS):
                        stats(0, 0, j, (t,))
                dve.wait_ge(x_stats, CHUNKS * CT)
                mean(0)
                deviation(0)
                variance(0)
                for n in range(CT):
                    w_low(n)
                norm(0)
                for n in range(CT, len(w_parts)):
                    w_low(n)
                centre(0, 0)
                dve.wait_ge(w_lo_done, len(w_parts))
                dve.wait_ge(zeroed, 4)
                dve.wait_ge(band_step, 3)
                dve.wait_ge(centre_done, 1)

                def batch(b, s, first, last):
                    for j in range(CHUNKS):
                        dve.wait_ge(xn_done, b * NPARTS + CT * (1 if j < 1 else 2 if j < 4 else 3))
                        for t in range(CT):
                            i = b * (CHUNKS * CT) + (j * CT + t)
                            done = b * (CHUNKS * TAPS) + (j * TAPS + t * K0)
                            positive(dve, fused_done, i - 1)
                            for k in range(K0):
                                dve.wait_ge(tap_ready, done + k + 1)
                                patch = xn[:, s, t, ROWS * j + k // 3:ROWS * j + k // 3 + ROWS, k % 3:k % 3 + W]
                                bias = bf[:, t, k:k + 1] if k != K0 // 2 else bfc[:, s, t:t + 1]
                                dve.scalar_tensor_tensor(prod[:, t, k, :].rearrange("p (h w) -> p h w", w=W),
                                                         filt[:, (t * K0 + k) % RING, :].rearrange("p (h w) -> p h w", w=W),
                                                         bias, patch, op0=ALU.add, op1=ALU.mult).then_inc(tap_used, 1)
                                if (j, t, k) == (0, 0, 2):
                                    dve.wait_ge(centre_done, b + 1)
                                if k == 2 and not (first and j * CT + t < 3):
                                    back = j * CT + t - 3
                                    take_y_stats(b * (CHUNKS * CT) + back, back % CT, b * CHUNKS + back // CT)
                                if k == 3 and not last and 1 <= j <= 4:
                                    stats(b + 1, 1 - s, 2 * (j - 1) + t)
                                if k == 3 and not last and (j, t) == (6, 1):
                                    variance(b + 1)
                                if k == 5 and not last and (j, t) == (4, 1):
                                    dve.wait_ge(x_stats, b * (CHUNKS * CT) + 2 * CHUNKS * CT)
                                if k == 5 and not (first and j * CT + t < 1):
                                    fuse(i - 1, (t - 1) % CT)
                                if k == 6 and not (first and j * CT + t < 1):
                                    split_fused(i - 1, j if t else j - 1, (t - 1) % CT)
                        if not last and j == 4:
                            mean(b + 1)
                        if not last and j == 5:
                            deviation(b + 1)
                        if not last and j == 6:
                            norm(b + 1)
                        if not last and j == 7:
                            centre(b + 1, 1 - s)

                batches(dve, batch)
                items = B * CHUNKS * CT
                fuse(items - 1, CT - 1)
                split_fused(items - 1, CHUNKS - 1, CT - 1)
                for back in (3, 2, 1):
                    take_y_stats(items - back, (items - back) % CT, (items - back) // CT)
                dve.wait_ge(y_stats, items)

            @block.tensor
            def _(pe):
                def group_mean(b1):
                    pe.wait_ge(mean_in, b1 * CT + CT)
                    positive(pe, attn_done, b1)
                    pe.matmul(sps[:, 0:CT], gavg[:, :], mv[:, :, 0], start=True, stop=True).then_inc(gmean_ps, 1)

                def group_var(b1):
                    pe.wait_ge(dev_in, b1 + 1)
                    pe.matmul(sps[:, 0:CT], gavg[:, :], ev[:, :], start=True, stop=True).then_inc(gvar_ps, 1)

                def eca(b1):
                    pe.wait_ge(norm_ready, b1 + 1)
                    for m in range(CT):
                        for t in range(CT):
                            last = pe.matmul(sps[:, m:m + 1], band[:, t, P * m:P * m + P], pooled[:, t:t + 1],
                                             start=(t == 0), stop=(t == CT - 1))
                    last.then_inc(eca_ps, 1)

                def split_products(dst, w_hi, w_lo, v_hi, v_lo):
                    terms = [(w, v, t) for t in range(CT) for w, v in ((w_hi, v_hi), (w_hi, v_lo), (w_lo, v_hi))]
                    for n, (w, v, t) in enumerate(terms):
                        last = pe.matmul(dst, w(t), v(t), start=(n == 0), stop=(n == len(terms) - 1))
                    return last

                def taps(b, j, t):
                    n = b * CHUNKS + j
                    if t == 0:
                        pe.wait_ge(x_lo_done, n + 1)
                    for k in range(K0):
                        positive(pe, tap_used, n * TAPS + (t * K0 + k + 1 - RING))
                        split_products(filt[:, (t * K0 + k) % RING, :],
                                       lambda c: wf_hi[:, c, t, k, :], lambda c: wf_lo[:, c, t, k, :],
                                       lambda c: x_hi[:, j % 2, c, :], lambda c: x_lo[:, j % 2, c, :]).then_inc(tap_ready, 1)

                def project(b, j, m):
                    yi = b * (CHUNKS * CT) + (j * CT + m)
                    pe.wait_ge(fu_lo_done, b * (CHUNKS * CT) + (j * CT + CT))
                    positive(pe, y_copied, yi)
                    split_products(yps[:, :],
                                   lambda c: wp_hi[:, c, P * m:P * m + P], lambda c: wp_lo[:, c, P * m:P * m + P],
                                   lambda c: fu_hi[:, j % 2, c, :], lambda c: fu_lo[:, j % 2, c, :]).then_inc(y_ready, 1)

                pe.wait_ge(consts_in, 16 * 5)
                group_mean(0)
                group_var(0)
                pe.wait_ge(band_step, 3)
                eca(0)
                pe.wait_ge(w_lo_done, CT)
                taps(0, 0, 0)
                pe.wait_ge(w_lo_done, len(w_parts))
                taps(0, 0, 1)

                def batch(b, s, first, last):
                    for j in range(CHUNKS):
                        end = last and j == CHUNKS - 1
                        for t in range(CT):
                            if not end:
                                taps(b, j + 1, t)
                            project(b, j, t)
                            if t == 0 and not last and j == 4:
                                group_mean(b + 1)
                            if t == 0 and not last and j == 5:
                                group_var(b + 1)
                            if t == 0 and not last and j == 6:
                                eca(b + 1)

                batches(pe, batch)


def layer1_features(nc, a, y_dram, r_dram, w2_dram, ystats, ab, yn):
    PIECES = 4
    PN = PX // PIECES
    x_v = a["x"].rearrange("b (t p) h w -> b p t (h w)", p=P)
    y_v = y_dram.rearrange("b (t p) n -> b p t n", p=P)
    with ExitStack() as ctx:
        def sb(name, shape, dt=F32):
            return ctx.enter_context(nc.sbuf_tensor(name, shape, dt))

        def sem(name):
            return ctx.enter_context(nc.semaphore(name))

        xs = sb("xs", [P, 2, CT, PX])
        ys = sb("ys", [P, PIECES, CT, PN])
        rb = sb("rb", [P, 2, POS, NBR, NBC])
        w1t = sb("w1t", [P, CT, RED])
        w1s = sb("w1s", [P, 2, CT, RED])
        cols = sb("cols", [P, 9])
        gavg1 = sb("gavg1", [P, P])
        sel = sb("sel", [P, QUARTERS, P])
        w2_raw = sb("w2_raw", [P, GROUPS * W2_LEN])
        w2_hi = sb("w2_hi", [P, GROUPS * W2_LEN], F32R)
        w2_lo = sb("w2_lo", [P, GROUPS * W2_LEN], F32R)
        ymv = sb("ymv", [P, CT, 2])
        bvar = sb("bvar", [P, 3])
        brs = sb("brs", [P, 3])
        bnt = sb("bnt", [P, 3])
        bsc = sb("bsc", [P, 3])
        ysh = sb("ysh", [P, CT])
        rsh = sb("rsh", [P, 1])
        rbias = sb("rbias", [P, 2])
        st = sb("st", [P, CT, CHUNKS, 6])
        mv1 = sb("mv1", [P, CT, 2])
        gm1 = sb("gm1", [P, CT])
        dm1 = sb("dm1", [P, CT])
        ev1 = sb("ev1", [P, CT])
        gv1 = sb("gv1", [P, CT])
        rt1 = sb("rt1", [P, CT])
        nt1 = sb("nt1", [P, CT])
        nrm = sb("nrm", [P, CT, 3])
        ynt = sb("ynt", [P, CT, 2])

        rps = ctx.enter_context(nc.psum_tensor("rps", [P, 4, N], F32))
        cps1 = ctx.enter_context(nc.psum_tensor("cps1", [P, N], F32))

        vec_in, w2_in = sem("vec_in"), sem("w2_in")
        xy_in = [sem(f"xy_in{n}") for n in range(PIECES)]
        w2_hi_done, w2_lo_done, w2_out = sem("w2_hi_done"), sem("w2_lo_done"), sem("w2_out")
        r_zeroed = sem("r_zeroed")
        bn_chain, bn_var, bn_root, bn_ready = sem("bn_chain"), sem("bn_var"), sem("bn_root"), sem("bn_ready")
        y_scaled, x1_done = sem("y_scaled"), sem("x1_done")
        x1_stats, mean1, chain1, scratch = sem("x1_stats"), sem("mean1"), sem("chain1"), sem("scratch")
        gmean1, dev1, gvar1, gvar1_in, root1 = sem("gmean1"), sem("dev1"), sem("gvar1"), sem("gvar1_in"), sem("root1")
        norm1, w1_scaled, small_ps, small_done = sem("norm1"), sem("w1_scaled"), sem("small_ps"), sem("small_done")
        ynt_here, yn_ps, yn_done = sem("ynt_here"), sem("yn_ps"), sem("yn_done")
        r_ready, r_copied, r_out = sem("r_ready"), sem("r_copied"), [sem(f"r_out{n}") for n in range(2)]

        CHAIN = 12

        def batches(engine, body):
            body(0, 0)
            body(1, 1)
            with engine.Fori(1, B // 2) as two:
                body(2 * two, 0)
                body(2 * two + 1, 1)
            body(B, 0)

        def exists(b):
            return not isinstance(b, int) or 0 <= b < B

        with nc.Block() as block:

            @block.sync
            def _(sp):
                sp.dma_start(cols[:, :], a["columns"]).then_inc(vec_in, 16)
                sp.dma_start(gavg1[:, :], a["group_average"]).then_inc(vec_in, 16)
                sp.dma_start(sel[:, :, :], a["select"]).then_inc(vec_in, 16)
                sp.dma_start(w1t[:, :, :], a["w1_t"]).then_inc(vec_in, 16)
                for n in range(B * PIECES):
                    b, q, s = n // PIECES, n % PIECES, n // PIECES % 2
                    if b >= 1:
                        sp.wait_ge(x1_done, n - PIECES + 1)
                    if b >= 2:
                        sp.wait_ge(r_ready, (b - 2) * CHUNKS + CHUNKS // PIECES * (q + 1))
                    sp.dma_start(ys[:, q, :, :], y_v[b, :, :, PN * q:PN * q + PN]).then_inc(xy_in[q], 16)
                    sp.dma_start(xs[:, s, :, PN * q:PN * q + PN],
                                 x_v[b, :, :, PN * q:PN * q + PN]).then_inc(xy_in[q], 16)
                    if n == PIECES:
                        sp.dma_start(w2_raw[:, :], a["w2_pad"]).then_inc(w2_in, 16)
                for part, (w, done) in enumerate(((w2_hi, w2_hi_done), (w2_lo, w2_lo_done))):
                    sp.wait_ge(done, 1)
                    sp.dma_start(w2_dram[:, :, part, :].rearrange("g p n -> p g n"),
                                 w[:, :].bitcast(F32).rearrange("p (g n) -> p g n", g=PAIRS)).then_inc(w2_out, 16)
                sp.wait_ge(w2_out, 32)

            @block.gpsimd
            def _(pool):
                pool.memset(rb[:, :, :, :, :], 0.0).then_inc(r_zeroed, 1)

                for b in range(B):
                    pool.wait_ge(r_copied, (b + 1) * 4 * CHUNKS)
                    pool.dma_start(r_dram[b], rb[:, b % 2, :, :, :].rearrange("p k r c -> p (k r c)"))\
                        .then_inc(r_out[b % 2], 16)
                for s in range(2):
                    pool.wait_ge(r_out[s], 16 * B // 2)

            @block.scalar
            def _(act):
                act.wait_ge(bn_var, 1)
                act.activation(brs[:, :], bvar[:, :], ACT.Sqrt).then_inc(bn_root, 1)
                act.wait_ge(bn_ready, 1)

                def scale_y(b, q):
                    act.wait_ge(xy_in[q], b * 32 + 32)
                    for t in range(CT):
                        act.activation(ys[:, q, t, :], ys[:, q, t, :], ACT.Identity, bias=ysh[:, t:t + 1],
                                       scale=bsc[:, t:t + 1]).then_inc(y_scaled, 1)

                def reduce(b, s, j):
                    act.wait_ge(r_ready, b * CHUNKS + (j + 1))
                    if j == 0:
                        act.wait_ge(small_done, b + 1)
                        positive(act, r_out[s], (b - s) * 8)
                    for h in range(2):
                        src = rps[:, j % 4, 256 * h:256 * h + 256].rearrange("p (i w) -> p i w", i=BR)
                        dst = rb[:, s, :, 2 * j + h, :].rearrange("p (i j) c -> p i j c", i=BR)
                        for c0, c1, w0, w1 in ((0, W // BC, 0, BC), (W // BC, NBC, 0, W - WHOLE)):
                            act.activation(dst[:, :, w0:w1, c0:c1],
                                           src[:, :, BC * c0:min(BC * c1, W)].rearrange(
                                               "p i (c j) -> p i j c", j=w1 - w0),
                                           ACT.Relu, bias=rbias[:, s:s + 1], scale=bsc[:, 2:3]).then_inc(r_copied, 1)

                def batch(b, s):
                    if exists(b - 1):
                        act.wait_ge(gvar1_in, b)
                        act.activation(rt1[:, :], gv1[:, :], ACT.Sqrt).then_inc(root1, 1)
                    for q in range(PIECES):
                        if exists(b):
                            scale_y(b, q)
                        if exists(b - 1) and q > 0:
                            for j in range(3 * q - 3, min(3 * q, CHUNKS)):
                                reduce(b - 1, 1 - s, j)
                        if isinstance(b, int) and (b, q) == (1, 0):
                            act.wait_ge(w2_in, 16)
                            act.activation(w2_hi[:, :], w2_raw[:, :], ACT.Identity).then_inc(w2_hi_done, 1)

                act.wait_ge(r_zeroed, 1)
                batches(act, batch)

            @block.vector
            def _(dve):
                gamma0, beta0 = cols[:, 0:2], cols[:, 2:4]
                b1, gamma1, beta1, rmean, rvar = (cols[:, n:n + 1] for n in range(4, 9))
                dve.wait_ge(vec_in, 64)
                for t in range(CT):
                    dve.bn_aggr(ymv[:, t, :], ystats[:, t, :, :].rearrange("p n s -> p (n s)")).then_inc(bn_chain, 1)
                dve.wait_ge(bn_chain, 2)
                dve.tensor_scalar(bvar[:, 0:2], ymv[:, :, 1], BN_EPS, None, ALU.add).then_inc(bn_chain, 1)
                dve.tensor_scalar(bvar[:, 2:3], rvar, BN_EPS, None, ALU.add).then_inc(bn_chain, 1)
                dve.wait_ge(bn_chain, 4)
                dve.tensor_copy(bnt[:, :], bvar[:, :]).then_inc(bn_var, 1)
                dve.wait_ge(bn_var, 1)
                dve.wait_ge(bn_root, 1)
                dve.reciprocal(brs[:, :], brs[:, :]).then_inc(bn_chain, 1)
                dve.wait_ge(bn_chain, 5)
                newton(dve, bn_chain, 5, brs[:, :], bvar[:, :], bnt[:, :])
                dve.tensor_tensor(bsc[:, 0:2], brs[:, 0:2], gamma0, ALU.mult).then_inc(bn_chain, 1)
                dve.tensor_tensor(bsc[:, 2:3], brs[:, 2:3], gamma1, ALU.mult).then_inc(bn_chain, 1)
                dve.wait_ge(bn_chain, 11)
                dve.tensor_tensor(ysh[:, :], ymv[:, :, 0], bsc[:, 0:2], ALU.mult).then_inc(bn_chain, 1)
                dve.tensor_tensor(rsh[:, :], b1, rmean, ALU.subtract).then_inc(bn_chain, 1)
                dve.wait_ge(bn_chain, 13)
                dve.tensor_tensor(ysh[:, :], beta0, ysh[:, :], ALU.subtract).then_inc(bn_ready, 1)
                dve.tensor_tensor(rsh[:, :], rsh[:, :], bsc[:, 2:3], ALU.mult).then_inc(bn_chain, 1)
                dve.wait_ge(bn_chain, 14)
                dve.tensor_tensor(rsh[:, :], rsh[:, :], beta1, ALU.add).then_inc(bn_chain, 1)
                dve.wait_ge(bn_chain, 15)
                dve.wait_ge(bn_ready, 1)
                dve.tensor_copy(ynt[:, :, 0], bsc[:, 0:2]).then_inc(ynt_here, 1)
                dve.tensor_scalar(ynt[:, :, 1], ysh[:, :], K1 * K1 * FINFO_EPS, None, ALU.add).then_inc(ynt_here, 1)
                dve.wait_ge(yn_ps, 1)
                dve.tensor_copy(yn[:, :, :], cps1[:, 96:96 + 2 * PAIRS].rearrange("p (a n) -> p a n", n=2))\
                    .then_inc(yn_done, 1)

                def add(b, s, q):
                    dve.wait_ge(y_scaled, b * (PIECES * CT) + CT * (q + 1))
                    piece = xs[:, s, :, PN * q:PN * q + PN]
                    dve.tensor_tensor(piece, piece, ys[:, q, :, :], ALU.add).then_inc(x1_done, 1)
                    dve.wait_ge(x1_done, b * PIECES + (q + 1))
                    for t in range(CT):
                        for j in (2 * q, 2 * q + 1):
                            dve.bn_stats(st[:, t, j, :], xs[:, s, t, N * j:N * j + N]).then_inc(x1_stats, 1)
                    if q == PIECES - 1:
                        dve.wait_ge(x1_stats, b * (CHUNKS * CT) + CHUNKS * CT)
                        dve.memset(nt1[:, :], 0.0).then_inc(scratch, 1)
                        for t in range(CT):
                            dve.bn_aggr(mv1[:, t, :], st[:, t, :, :].rearrange("p j s -> p (j s)")).then_inc(mean1, 1)

                def norm(b, s):
                    def step(ins, n):
                        ins.then_inc(chain1, 1)
                        dve.wait_ge(chain1, b * CHAIN + n)

                    dve.wait_ge(gmean1, b + 1)
                    step(dve.tensor_copy(gm1[:, :], cps1[:, 0:CT]), 1)
                    dve.wait_ge(mean1, b * CT + CT)
                    step(dve.tensor_tensor(dm1[:, :], mv1[:, :, 0], gm1[:, :], ALU.subtract), 2)
                    step(dve.tensor_tensor(ev1[:, :], dm1[:, :], dm1[:, :], ALU.mult), 3)
                    dve.tensor_tensor(ev1[:, :], ev1[:, :], mv1[:, :, 1], ALU.add).then_inc(dev1, 1)
                    dve.wait_ge(gvar1, b + 1)
                    dve.tensor_scalar(gv1[:, :], cps1[:, 0:CT], GN_EPS, None, ALU.add).then_inc(gvar1_in, 1)
                    dve.wait_ge(gvar1_in, b + 1)
                    dve.wait_ge(root1, b + 1)
                    step(dve.reciprocal(rt1[:, :], rt1[:, :]), 4)
                    dve.wait_ge(scratch, b + 1)
                    newton(dve, chain1, b * CHAIN + 4, rt1[:, :], gv1[:, :], nt1[:, :])
                    step(dve.tensor_tensor(gm1[:, :], gm1[:, :], rt1[:, :], ALU.mult), 9)
                    step(dve.tensor_copy(nrm[:, :, 1], rt1[:, :]), 10)
                    step(dve.tensor_tensor(ev1[:, :], ysh[:, :], rt1[:, :], ALU.mult), 11)
                    dve.tensor_tensor(nrm[:, :, 2], ev1[:, :], gm1[:, :], ALU.subtract).then_inc(norm1, 1)
                    dve.tensor_scalar(nrm[:, :, 0], gm1[:, :], -1.0, None, ALU.mult).then_inc(norm1, 1)
                    for t in range(CT):
                        dve.tensor_scalar(w1s[:, s, t, :], w1t[:, t, :], rt1[:, t:t + 1], None,
                                          ALU.mult).then_inc(w1_scaled, 1)
                    dve.wait_ge(small_ps, b + 1)
                    dve.tensor_copy(ab[:, b, :, :], cps1[:, 16:16 + 2 * PAIRS].rearrange("p (a n) -> p a n", n=2))\
                        .then_inc(chain1, 1)
                    dve.tensor_scalar(rbias[:, s:s + 1], cps1[:, 64:65], bsc[:, 2:3], rsh[:, :], ALU.mult,
                                      ALU.add).then_inc(small_done, 1)
                    dve.wait_ge(chain1, b * CHAIN + 12)

                def batch(b, s):
                    if exists(b - 1):
                        norm(b - 1, 1 - s)
                    for q in range(PIECES):
                        if exists(b):
                            add(b, s, q)
                        if isinstance(b, int) and (b, q) == (1, 0):
                            dve.wait_ge(w2_hi_done, 1)
                            dve.tensor_tensor(w2_lo[:, :], w2_raw[:, :], w2_hi[:, :].bitcast(F32),
                                              ALU.subtract).then_inc(w2_lo_done, 1)

                dve.wait_ge(bn_ready, 1)
                batches(dve, batch)

            @block.tensor
            def _(pe):
                pe.wait_ge(vec_in, 64)
                pe.wait_ge(ynt_here, 2)
                for p in range(PAIRS):
                    last = pe.matmul(cps1[:, 96 + 2 * p:98 + 2 * p], sel[:, p % 4, :], ynt[:, p // 4, :],
                                     start=True, stop=True)
                last.then_inc(yn_ps, 1)
                pe.wait_ge(yn_done, 1)

                def batch(b1, s1):
                    if not exists(b1 - 1):
                        return
                    b, s = b1 - 1, 1 - s1
                    pe.wait_ge(mean1, b * CT + CT)
                    positive(pe, small_done, b)
                    pe.matmul(cps1[:, 0:CT], gavg1[:, :], mv1[:, :, 0], start=True, stop=True).then_inc(gmean1, 1)
                    pe.wait_ge(dev1, b + 1)
                    pe.matmul(cps1[:, 0:CT], gavg1[:, :], ev1[:, :], start=True, stop=True).then_inc(gvar1, 1)
                    pe.wait_ge(norm1, b * 2 + 2)
                    for p in range(PAIRS):
                        pe.matmul(cps1[:, 16 + 2 * p:18 + 2 * p], sel[:, p % 4, :], nrm[:, p // 4, 1:3],
                                  start=True, stop=True)
                    for t in range(CT):
                        last = pe.matmul(cps1[:, 64:65], w1t[:, t, :], nrm[:, t, 0:1], start=(t == 0), stop=(t == CT - 1))
                    last.then_inc(small_ps, 1)
                    pe.wait_ge(w1_scaled, b * CT + CT)
                    for j in range(CHUNKS):
                        positive(pe, r_copied, b * (4 * CHUNKS) + 4 * (j - 3))
                        for t in range(CT):
                            last = pe.matmul(rps[:, j % 4, :], w1s[:, s, t, :], xs[:, s, t, N * j:N * j + N],
                                             start=(t == 0), stop=(t == CT - 1))
                        last.then_inc(r_ready, 1)

                batches(pe, batch)


def layer1_involution(nc, a, y_dram, r_dram, w2_dram, out, ab, yn):
    x_v = a["x"].rearrange("b (a c) h w -> b a c h w", c=PCH)
    y_v = y_dram.rearrange("b (a c) (h w) -> b a c h w", c=PCH, w=W)
    out_v = out.rearrange("b (a c) (q r) w -> b a q c (r w)", c=PCH, q=QUARTERS)
    r_v = r_dram.rearrange("(t s) p (k n) -> t p k s n", s=2, k=POS)
    YROWS = HROWS // 2
    with ExitStack() as ctx:
        def sb(name, shape, dt=F32):
            return ctx.enter_context(nc.sbuf_tensor(name, shape, dt))

        def sem(name):
            return ctx.enter_context(nc.semaphore(name))

        cols2 = sb("cols2", [PATCH, 2 * BLK, 2, BR, BC])
        r_hi = sb("r_hi", [P, POS, 2, BLK], F32R)
        r_lo = sb("r_lo", [P, POS, 2, BLK], F32R)
        xt = sb("xt", [PATCH, 2, QBLK, P])
        xq = sb("xq", [P, HROWS, W])
        yq = sb("yq", [P, YROWS, W])
        res = sb("res", [P, 2, QROWS, W])
        xnq = sb("xnq", [P, NBC, HROWS, PC])
        w2u = sb("w2u", [P, 2, 2, W2_LEN], F32R)
        b2u = sb("b2u", [PATCH, 2, POS])
        abu = sb("abu", [P, 2, 3, 2])
        ynu = sb("ynu", [P, 3, 2])
        msk = sb("msk", [P, 3, 2])
        gsel = sb("gsel", [P, 2])
        ident = sb("ident", [P, P])
        r_raw = r_lo[:, :, :, :].bitcast(F32)

        aps = ctx.enter_context(nc.psum_tensor("aps", [P, 2, 2, N], F32))
        tps = ctx.enter_context(nc.psum_tensor("tps", [P, 2, N], F32))
        cps = ctx.enter_context(nc.psum_tensor("cps", [P, 2, N], F32))

        PARTS = 8
        PP = POS // PARTS
        TG = QBLK // 4
        CG = QBR
        UNITS = PAIRS * B // 2

        x1_half, yq_in = sem("x1_half"), sem("yq_in")
        const_in, w2_in, xq_in = sem("const_in"), sem("w2u_in"), sem("xq_in")
        r_in = [sem(f"r_in{part}") for part in range(PARTS)]
        pads = sem("pads")
        r_hi_done, r_lo_done = sem("r_hi_done"), sem("r_lo_done")
        a_ready, a_dve, a_act = sem("a_ready"), sem("a_dve"), sem("a_act")
        norm_here, xn_inner, xn_edges, res_begun = sem("norm_here"), sem("xn_inner"), sem("xn_edges"), sem("res_begun")
        t_ready, t_copied = sem("t_ready"), sem("t_copied")
        c_ready, c_first, c_done = sem("c_ready"), sem("c_first"), sem("c_done")
        stored = [sem(f"stored{s}") for s in range(2)]

        FIRST_AT = (0, 0, 1, 1, 2, 3, 4, 5, 6, 7, 8)
        SECOND_X1 = (3, 7)
        SECOND_NORM = (6, 9)
        SECOND_EDGES = (7, 8, 9)
        SECOND_AT = (12, 13, 14, 15, 16, 17, 18, 19, 21, 23, 23)
        NEXT_XQ = 10
        NEXT_NORM = 11
        NEXT_X1 = (16, 20)
        NEXT_YQ = 16
        AHEAD = 3
        R_SPLIT = (13, 14, 16, 17, 20)
        UPPER = -(-(QBR - 1) * NBC // 4)

        def windows(r0, r1):
            at = xq[:, r0:r1, BC - HALO:BC - HALO + PC]
            dims = [list(d) for d in at.ap]
            return bass.AP(at.tensor, at.offset, [dims[0], [BC, NBC - 2], *dims[1:]])

        def patch_columns(r0, r1):
            over = BC * (NBC - 1) - HALO
            return ((xnq[:, 0, r0:r1, HALO:PC], xq[:, r0:r1, 0:PC - HALO]),
                    (xnq[:, NBC - 1, r0:r1, 0:W - over], xq[:, r0:r1, over:W]),
                    (xnq[:, 1:NBC - 1, r0:r1, :], windows(r0, r1)))

        def rows_of(bank):
            return cps[:, bank, :].rearrange("p (g i w) -> p g i w", g=2, i=BR)

        def units(engine, unit):
            unit(0, 0, (0, 1))
            with engine.Fori(1, PAIRS - 1) as p:
                unit(0, p, (0, p + 1))
            with engine.Fori(1, B // 2) as t:
                unit(t - 1, PAIRS - 1, (t, 0))
                with engine.Fori(0, PAIRS - 1) as p:
                    unit(t, p, (t, p + 1))
            unit(B // 2 - 1, PAIRS - 1, None)

        def new_images(after):
            return after is not None and isinstance(after[1], int) and after[1] == 0

        def transposes_after(k):
            return [(s, g) for s, at in enumerate((FIRST_AT, SECOND_AT)) for g in range(TG) if at[g] == k]

        with nc.Block() as block:

            @block.sync
            def _(sp):
                def load_image(t, p, s):
                    u = t * PAIRS + p
                    positive(sp, xn_inner, u * 2 + s)
                    positive(sp, xn_edges, u * 2 + s)
                    positive(sp, res_begun, u * 2 + s)
                    for q in range(QUARTERS):
                        r0, r1 = max(QROWS * q - HALO, 0), min(QROWS * q + QROWS + HALO, H)
                        d = r0 - (QROWS * q - HALO)
                        sp.dma_start(xq[PCH * q:PCH * q + PCH, d:d + r1 - r0, :],
                                     x_v[2 * t + s, p, :, r0:r1, :]).then_inc(xq_in, 16)
                    load_y(t, p, s, 0)

                def load_y(t, p, s, h):
                    positive(sp, x1_half, (t * PAIRS + p) * 4 + (2 * s + h))
                    for q in range(QUARTERS):
                        top = QROWS * q - HALO + YROWS * h
                        r0, r1 = max(top, 0), min(top + YROWS, H)
                        sp.dma_start(yq[PCH * q:PCH * q + PCH, r0 - top:r1 - top, :],
                                     y_v[2 * t + s, p, :, r0:r1, :]).then_inc(yq_in, 16)

                def load_w2(p):
                    sp.dma_start(w2u[:, :, :, :].bitcast(F32).rearrange("p a g n -> p (a g n)"),
                                 w2_dram[p].rearrange("p a n -> p (a n)")).then_inc(w2_in, 16)
                    sp.dma_start(b2u[:, :, :].rearrange("p g k -> p (g k)"), a["b2_band"][p]).then_inc(w2_in, 16)

                def load_r(t, part):
                    for n in range(2):
                        sp.dma_start(r_raw[:, PP * part:PP * part + PP, n, :],
                                     r_v[t, :, PP * part:PP * part + PP, n, :]).then_inc(r_in[part], 16)

                def store(u, t, p, s):
                    sp.wait_ge(c_done, u * (2 * CG) + CG * (s + 1))
                    for q in reversed(range(QUARTERS)):
                        sp.dma_start(out_v[2 * t + s, p, q], res[PCH * q:PCH * q + PCH, s, :, :].rearrange("p r w -> p (r w)"))\
                            .then_inc(stored[s], 16)

                def unit(t, p, after):
                    u = t * PAIRS + p
                    load_y(t, p, 1, 1)
                    for k in range(POS):
                        if new_images(after) and k % PP == PP - 1:
                            sp.wait_ge(a_ready, u * (2 * POS) + (2 * k + 2))
                            load_r(after[0], k // PP)
                        if k == NEXT_XQ and after:
                            load_image(*after, 0)
                        if k == NEXT_YQ and after:
                            load_y(*after, 0, 1)
                    if after:
                        sp.wait_ge(c_ready, u * (2 * CG) + 1)
                        load_w2(after[1])
                    store(u, t, p, 0)
                    if after:
                        load_image(*after, 1)
                    store(u, t, p, 1)

                sp.dma_start(ident[:, :], a["identity"]).then_inc(const_in, 16)
                sp.dma_start(msk[:, :, :], a["row_masks"]).then_inc(const_in, 16)
                sp.dma_start(gsel[:, :], a["group_masks"]).then_inc(const_in, 16)
                load_w2(0)
                load_r(0, 0)
                sp.wait_ge(pads, 2)
                load_image(0, 0, 0)
                load_y(0, 0, 0, 1)
                for part in range(1, PARTS):
                    load_r(0, part)
                load_image(0, 0, 1)
                units(sp, unit)
                for s in range(2):
                    sp.wait_ge(stored[s], 16 * QUARTERS * UNITS)

            @block.gpsimd
            def _(pool):
                def begin(t, p):
                    u = t * PAIRS + p
                    for s in range(2):
                        pool.wait_ge(x1_half, u * 4 + (2 * s + 2))
                        pool.wait_ge(norm_here, u + 1)
                        positive(pool, stored[s], u * (16 * QUARTERS))
                        pool.tensor_tensor(res[:, s, :, :], xq[:, HALO:HALO + QROWS, :],
                                           ynu[:, 0:1, 1:2].to_broadcast([P, QROWS, W]),
                                           ALU.add).then_inc(res_begun, 1)

                pool.memset(xq[:, :, :], 0.0).then_inc(pads, 1)
                pool.memset(yq[:, :, :], 0.0).then_inc(pads, 1)
                pool.memset(xnq[:, :, :, :], 0.0).then_inc(pads, 1)
                begin(0, 0)
                with pool.Fori(1, UNITS) as u:
                    begin(0, u)

            @block.scalar
            def _(act):
                def normalise(u, s, halves=(0, 1)):
                    act.wait_ge(norm_here, u + 1)
                    for half in halves:
                        act.wait_ge(x1_half, u * 4 + (2 * s + half + 1))
                        positive(act, t_ready, u * (2 * TG) + TG * (s - 1) + (TG if half else UPPER))
                        r0 = HALO + QROWS // 2 * half
                        dst, src = patch_columns(r0, r0 + QROWS // 2)[2]
                        last = act.activation(dst, src, ACT.Identity, bias=abu[:, s, 0, 1:2], scale=abu[:, s, 0, 0:1])
                    if 1 in halves:
                        last.then_inc(xn_inner, 1)

                def split(t, k):
                    act.wait_ge(r_in[k // PP], t * 32 + 32)
                    act.activation(r_hi[:, k, :, :], r_raw[:, k, :, :], ACT.Identity).then_inc(r_hi_done, 1)

                def unit(t, p, after):
                    u = t * PAIRS + p
                    for k in range(POS):
                        act.wait_ge(a_ready, u * (2 * POS) + (2 * k + 2))
                        positive(act, c_ready, u * (2 * CG))
                        act.activation(cols2[:, :, 1, k // BC, k % BC], aps[0:PATCH, k % 2, 1, 0:2 * BLK],
                                       ACT.Identity, bias=b2u[:, 1, k:k + 1]).then_inc(a_act, 1)
                        for s, g in transposes_after(k):
                            n = s * TG + g
                            act.wait_ge(t_ready, u * (2 * TG) + (n + 1))
                            positive(act, c_ready, u * (2 * CG) - CG * (1 - s))
                            act.activation(xt[:, s, 4 * g:4 * g + 4, :].rearrange("p n c -> p (n c)"),
                                           tps[0:PATCH, n % 2, :], ACT.Identity).then_inc(t_copied, 1)
                        if k in SECOND_NORM:
                            normalise(u, 1, (SECOND_NORM.index(k),))
                        if isinstance(u, int) and u == 0 and k + AHEAD < POS:
                            split(0, k + AHEAD)
                        if new_images(after) and k in R_SPLIT:
                            split(after[0], R_SPLIT.index(k))
                    if after:
                        normalise(u + 1, 0)
                    if new_images(after):
                        for k in range(len(R_SPLIT), POS):
                            split(after[0], k)

                act.wait_ge(pads, 3)
                normalise(0, 0)
                for k in range(AHEAD):
                    split(0, k)
                units(act, unit)

            @block.vector
            def _(dve):
                def norm(t, p):
                    u = t * PAIRS + p
                    positive(dve, xn_inner, 2 * u)
                    positive(dve, xn_edges, 2 * u)
                    for s in range(2):
                        last = dve.tensor_tensor(abu[:, s, :, :],
                                                 ab[:, 2 * t + s, p, :].rearrange("p (o n) -> p o n", o=1).to_broadcast([P, 3, 2]),
                                                 msk[:, :, :], ALU.mult)
                    positive(dve, x1_half, 4 * u)
                    positive(dve, res_begun, 2 * u)
                    last = dve.tensor_tensor(ynu[:, :, :],
                                      yn[:, p, :].rearrange("p (o n) -> p o n", o=1).to_broadcast([P, 3, 2]),
                                      msk[:, :, :], ALU.mult)
                    last.then_inc(norm_here, 1)

                def add_y(u, s, h):
                    dve.wait_ge(xq_in, u * (2 * 16 * QUARTERS) + 16 * QUARTERS * (s + 1))
                    dve.wait_ge(yq_in, u * (4 * 16 * QUARTERS) + 16 * QUARTERS * (2 * s + h + 1))
                    dve.wait_ge(norm_here, u + 1)
                    outer = (0, HALO, 1) if h == 0 else (HALO + QROWS, HROWS, 2)
                    inner = (HALO, YROWS, 0) if h == 0 else (YROWS, HALO + QROWS, 0)
                    for r0, r1, n in (outer, inner):
                        v = xq[:, r0:r1, :]
                        last = dve.scalar_tensor_tensor(v, yq[:, r0 - YROWS * h:r1 - YROWS * h, :], ynu[:, n, 0:1], v,
                                                        op0=ALU.mult, op1=ALU.add)
                    last.then_inc(x1_half, 1)

                def normalise_edges(u, s, edges):
                    dve.wait_ge(norm_here, u + 1)
                    for edge in edges:
                        dve.wait_ge(x1_half, u * 4 + (2 * s + (1 if edge == 0 else 2)))
                        positive(dve, t_ready, u * (2 * TG) + TG * (s - 1) + (UPPER if edge == 0 else TG))
                        n, columns = ((1, patch_columns(0, HALO)), (2, patch_columns(HALO + QROWS, HROWS)),
                                      (0, patch_columns(HALO, HALO + QROWS)[0:2]))[edge]
                        for dst, src in columns:
                            last = dve.tensor_scalar(dst, src, abu[:, s, n, 0:1], abu[:, s, n, 1:2], ALU.mult, ALU.add)
                    if 2 in edges:
                        last.then_inc(xn_edges, 1)

                def split(t, k):
                    dve.wait_ge(r_hi_done, t * POS + (k + 1))
                    dve.tensor_tensor(r_lo[:, k, :, :], r_raw[:, k, :, :], r_hi[:, k, :, :].bitcast(F32),
                                      ALU.subtract).then_inc(r_lo_done, 1)

                def add_products(u, s, c):
                    if c == 0:
                        dve.wait_ge(res_begun, u * 2 + (s + 1))
                    n = s * CG + c
                    dve.wait_ge(c_ready, u * (2 * CG) + (n + 1))
                    src = rows_of(n % 2)
                    dst = res[:, s, BR * c:BR * c + BR, :]
                    dve.scalar_tensor_tensor(dst, src[:, 1], gsel[:, 1:2], dst, op0=ALU.mult,
                                             op1=ALU.add).then_inc(c_first, 1)
                    dve.wait_ge(c_first, u * (2 * CG) + (n + 1))
                    dve.scalar_tensor_tensor(dst, src[:, 0], gsel[:, 0:1], dst, op0=ALU.mult,
                                             op1=ALU.add).then_inc(c_done, 1)

                def unit(t, p, after):
                    u = t * PAIRS + p
                    for k in range(POS):
                        dve.wait_ge(a_ready, u * (2 * POS) + (2 * k + 1))
                        positive(dve, c_ready, u * (2 * CG))
                        dve.tensor_scalar(cols2[:, :, 0, k // BC, k % BC], aps[0:PATCH, k % 2, 0, 0:2 * BLK],
                                          b2u[:, 0, k:k + 1], None, ALU.add).then_inc(a_dve, 1)
                        if k in SECOND_EDGES:
                            normalise_edges(u, 1, (SECOND_EDGES.index(k),))
                        if k in SECOND_X1:
                            add_y(u, 1, SECOND_X1.index(k))
                        if k == NEXT_NORM and after:
                            norm(*after)
                        if k in NEXT_X1 and after:
                            add_y(u + 1, 0, NEXT_X1.index(k))
                        if isinstance(u, int) and u == 0 and k + AHEAD < POS:
                            split(0, k + AHEAD)
                        if new_images(after) and k in R_SPLIT:
                            split(after[0], R_SPLIT.index(k))
                    if after:
                        normalise_edges(u + 1, 0, (0, 1, 2))
                    k = len(R_SPLIT)
                    for n in range(2 * CG + 1):
                        if n > 0:
                            add_products(u, (n - 1) // CG, (n - 1) % CG)
                        if new_images(after):
                            upto = POS - 2 * (2 * CG - n)
                            for k in range(k, upto):
                                split(after[0], k)
                            k = upto

                dve.wait_ge(const_in, 48)
                dve.wait_ge(pads, 3)
                norm(0, 0)
                for h in range(2):
                    add_y(0, 0, h)
                normalise_edges(0, 0, (0, 1, 2))
                for k in range(AHEAD):
                    split(0, k)
                units(dve, unit)

            @block.tensor
            def _(pe):
                def transposes(u, s, g):
                    n = s * TG + g
                    if g == 0:
                        pe.wait_ge(xn_inner, u * 2 + (s + 1))
                        pe.wait_ge(xn_edges, u * 2 + (s + 1))
                    positive(pe, t_copied, u * (2 * TG) + (n - 1))
                    for m in range(4):
                        r, c = (4 * g + m) // NBC, (4 * g + m) % NBC
                        last = pe.transpose(tps[0:PATCH, n % 2, P * m:P * m + P],
                                            xnq[:, c, BR * r:BR * r + PR, :].rearrange("p r c -> p (r c)"), ident[:, :])
                    last.then_inc(t_ready, 1)

                def taps(u, k):
                    for g in range(2):
                        if k >= 2:
                            pe.wait_ge((a_dve, a_act)[g], u * POS + (k - 1))
                        terms = ((0, r_hi), (0, r_lo), (1, r_hi))
                        for n, (part, r) in enumerate(terms):
                            at = W2_AT - PC * (k // BC) - k % BC
                            last = pe.matmul(aps[0:PATCH, k % 2, g, 0:2 * BLK], w2u[:, part, g, at:at + PATCH],
                                             r[:, k, :, :].rearrange("p s n -> p (s n)"),
                                             start=(n == 0), stop=(n == 2))
                        last.then_inc(a_ready, 1)

                def products(u, s, c):
                    n = s * CG + c
                    if c == 0:
                        pe.wait_ge(t_copied, u * (2 * TG) + TG * (s + 1))
                    positive(pe, c_done, u * (2 * CG) + (n - 1))
                    for m in range(NBC):
                        width = min(BC, W - BC * m)
                        for q in range(QUARTERS):
                            at = s * BLK + (QBR * q + c) * NBC + m
                            last = pe.matmul(rows_of(n % 2)[PCH * q:PCH * q + PCH, :, :, BC * m:BC * m + width],
                                             xt[:, s, c * NBC + m, PCH * q:PCH * q + PCH],
                                             cols2[:, at, :, :, 0:width], start=True, stop=True)
                    last.then_inc(c_ready, 1)

                def unit(t, p, after):
                    u = t * PAIRS + p
                    pe.wait_ge(w2_in, u * 32 + 32)
                    for k in range(POS):
                        pe.wait_ge(r_lo_done, t * POS + (k + 1))
                        taps(u, k)
                        for s, g in transposes_after(k):
                            transposes(u, s, g)
                    pe.wait_ge(a_act, u * POS + POS)
                    pe.wait_ge(a_dve, u * POS + POS)
                    for s in range(2):
                        for c in range(CG):
                            products(u, s, c)

                pe.wait_ge(const_in, 48)
                units(pe, unit)


def kernel(**inputs):
    import numpy as np
    import concourse.bacc as bacc
    from concourse.bass_utils import run_bass_kernel_spmd

    nc = bacc.Bacc("TRN2", target_bir_lowering=False, num_devices=1)
    i = {n: np.ascontiguousarray(v) for n, v in inputs.items()}

    wf_t = i["L0_conv_W_filter"].reshape(CT, P, K0, CT, P).transpose(4, 3, 0, 2, 1)
    wp_t = i["L0_conv_W_proj"].reshape(C, CT, P).transpose(2, 1, 0)
    vectors = [i[n].reshape(-1, P).T for n in ("L0_conv_gamma", "L0_conv_beta", "L1_conv_b1", "L1_conv_gamma",
                                               "L1_conv_beta", "L1_conv_run_mean", "L1_conv_run_var")]
    taps = i["L1_conv_w2"].reshape(GROUPS, K1, K1, RED)
    w2_pad = np.zeros((RED, GROUPS, W2_LEN), np.float32)
    for r in range(K1):
        w2_pad[:, :, W2_AT + PC * r:W2_AT + PC * r + K1] = taps[:, r].transpose(2, 0, 1)
    b2_band = np.zeros((PAIRS, 2, BR, BC, PR, PC), np.float32)
    b2 = i["L1_conv_b2"].reshape(PAIRS, 2, K1, K1)
    for r in range(BR):
        for c in range(BC):
            b2_band[:, :, r, c, r:r + K1, c:c + K1] = b2
    c = np.arange(C)
    shifts = np.stack([(c[:, None] == c[None, :] + d) for d in (-1, 0, 1)]).astype(np.float32)
    p = np.arange(P)
    group_average = ((p[:, None] // GN_CH == p[None, :] // GN_CH) / GN_CH).astype(np.float32)
    select = np.stack([(p[:, None] == PCH * n + p[None, :] % PCH) for n in range(4)], 1).astype(np.float32)
    quarter = p // PCH
    row_masks = np.stack([quarter >= 0, quarter > 0, quarter < QUARTERS - 1], 1).astype(np.float32)
    group_masks = np.stack([p % PCH // GC == n for n in range(2)], 1).astype(np.float32)
    arrays = {
        "x": i["x"], "wf_t": wf_t.reshape(P, -1), "wp_t": wp_t.reshape(P, -1),
        "b_filter": i["L0_conv_b_filter"].reshape(CT, P, K0).transpose(1, 0, 2), "w_eca": i["L0_conv_w_eca"],
        "b_proj": i["L0_conv_b_proj"].reshape(CT, P).T,
        "columns": np.concatenate(vectors, 1), "w1_t": i["L1_conv_w1"].reshape(RED, CT, P).transpose(2, 1, 0),
        "w2_pad": w2_pad.reshape(RED, -1), "b2_band": b2_band.transpose(0, 4, 5, 1, 2, 3).reshape(PAIRS, PATCH, 2 * POS),
        "shifts": shifts, "group_average": group_average, "select": select,
        "row_masks": np.repeat(row_masks[:, :, None], 2, 2), "group_masks": group_masks,
        "identity": np.eye(P, dtype=np.float32),
    }
    arrays = {n: np.ascontiguousarray(v) for n, v in arrays.items()}
    a = {n: nc.dram_tensor(n, v.shape, F32, kind="ExternalInput").ap() for n, v in arrays.items()}
    y_dram = nc.dram_tensor("y", (B, C, PX), F32, kind="Internal").ap()
    r_dram = nc.dram_tensor("r", (B, P, POS * BLK), F32, kind="Internal").ap()
    w2_dram = nc.dram_tensor("w2_parts", (PAIRS, P, 2, 2 * W2_LEN), F32, kind="Internal").ap()
    out = nc.dram_tensor("out", (B, C, H, W), F32, kind="ExternalOutput").ap()
    build(nc, a, y_dram, r_dram, w2_dram, out)
    return run_bass_kernel_spmd(nc, [arrays], core_ids=[0]).results[0]["out"]
```
